# Optimizing a Trainium2 kernel written in Bass

```python
import numpy as np
import jax
import jax.numpy as jnp

def _softmax(x, axis=-1):
    return jax.nn.softmax(x, axis=axis)

def _gelu(x):
    return jax.nn.gelu(x, approximate=True)

def _silu(x):
    return jax.nn.silu(x)

def _sigmoid(x):
    return jax.nn.sigmoid(x)

def _layernorm(x, axis=-1, eps=1e-05):
    m = jnp.mean(x, axis=axis, keepdims=True)
    v = jnp.var(x, axis=axis, keepdims=True)
    return (x - m) / jnp.sqrt(v + eps)

def _scatter_add(tgt, idx, src, axis=0):
    return tgt.at[idx].add(src)

def _segment_sum(src, seg, n):
    return jax.ops.segment_sum(src, seg, n)
kernel_name = 'mk_gnn_ffn_d2_gnn_r32_eb74c6'

def setup_inputs(seed: int=0):
    np.random.seed(seed)
    _w = jnp.asarray

    def _rec_inputs():
        import jax
        import jax.numpy as jnp
        _gk = jax.random.key(seed)
        x = -0.0003713 + 1 * jax.random.normal(jax.random.fold_in(_gk, 1), (3125, 256), jnp.float32)
        _s = jax.random.randint(jax.random.fold_in(_gk, 2), (25000,), 0, 3125, jnp.int32)
        _d = jax.random.randint(jax.random.fold_in(_gk, 3), (25000,), 0, 3125, jnp.int32)
        _loop = jnp.arange(3125, dtype=jnp.int32)
        src = jnp.concatenate([_s, _d, _loop])
        dst = jnp.concatenate([_d, _s, _loop])
        _o = jnp.argsort(dst, stable=True)
        src = src[_o]
        dst = dst[_o]
        edge_attr_20 = jax.random.uniform(jax.random.fold_in(_gk, 11), (53125, 20), jnp.float32, 0.0, 1)
        return (x, src, dst, edge_attr_20)
    x, src, dst, edge_attr_20 = _rec_inputs()

    def _L0_gnn_setup():
        import jax, jax.numpy as jnp
        import numpy as np
        N, IN_CH, HEADS, OUT_CH, E = (50000, 256, 4, 64, 25000)
        key = jax.random.key(seed)
        k1, k2, k3, k4, k5 = jax.random.split(key, 5)
        x = jax.random.normal(k1, (N, IN_CH), dtype=jnp.float32)
        edge_index = jax.random.randint(k2, (2, E), 0, N, dtype=jnp.int64)
        bw = float(np.sqrt(6.0 / (IN_CH + HEADS * OUT_CH)))
        ba = float(np.sqrt(6.0 / (HEADS + OUT_CH)))
        weight = jax.random.uniform(k3, (IN_CH, HEADS * OUT_CH), jnp.float32, -bw, bw)
        attn_l = jax.random.uniform(k4, (HEADS, OUT_CH), jnp.float32, -ba, ba)
        attn_r = jax.random.uniform(k5, (HEADS, OUT_CH), jnp.float32, -ba, ba)
        return {'x': x, 'edge_index': edge_index, 'weight': weight, 'attn_l': attn_l, 'attn_r': attn_r}
    _L0_gnn_all = _L0_gnn_setup()
    _L0_gnn_in = {k: v for k, v in _L0_gnn_all.items() if k in ('weight', 'attn_l', 'attn_r')}
    del _L0_gnn_all

    def _L0_ffn_setup():
        import math
        import jax, jax.numpy as jnp
        import numpy as np
        CAPACITY_FACTOR = 1.25
        key = jax.random.key(seed)
        ks = jax.random.split(key, 5)
        B, L, D, F, E = (8, 256, 256, 1024, 8)
        h = jax.random.normal(ks[0], (B, L, D), dtype=jnp.float32)
        gate_w = jax.random.normal(ks[1], (D, E), dtype=jnp.float32) * 0.02
        gate_b = jnp.zeros((E,), dtype=jnp.float32)
        w1 = jax.random.normal(ks[2], (E, D, F), dtype=jnp.float32) * (1.0 / math.sqrt(D))
        b1 = jnp.zeros((E, F), dtype=jnp.float32)
        w2 = jax.random.normal(ks[3], (E, F, D), dtype=jnp.float32) * (1.0 / math.sqrt(F))
        b2 = jnp.zeros((E, D), dtype=jnp.float32)
        return {'h': h, 'gate_w': gate_w, 'gate_b': gate_b, 'w1': w1, 'b1': b1, 'w2': w2, 'b2': b2}
    _L0_ffn_all = _L0_ffn_setup()
    _L0_ffn_in = {k: v for k, v in _L0_ffn_all.items() if k in ('gate_w', 'gate_b', 'w1', 'b1', 'w2', 'b2')}
    del _L0_ffn_all

    def _L1_gnn_setup():
        import jax, jax.numpy as jnp
        import numpy as np
        N, E, HDIM, NG = (10000, 10000, 256, 20)
        BN_EPS = 1e-05
        key = jax.random.key(seed)
        ks = jax.random.split(key, 12)
        inp = {'x': jax.random.normal(ks[0], (N, HDIM), dtype=jnp.float32), 'rbf': jax.random.uniform(ks[1], (E, NG), dtype=jnp.float32), 'ei': jax.random.randint(ks[2], (2, E), 0, N, dtype=jnp.int64), 'Wf1': jax.random.normal(ks[3], (NG, HDIM), dtype=jnp.float32) / np.sqrt(NG), 'bf1': jnp.zeros((HDIM,), dtype=jnp.float32), 'Wf2': jax.random.normal(ks[4], (HDIM, HDIM), dtype=jnp.float32) / np.sqrt(HDIM), 'bf2': jnp.zeros((HDIM,), dtype=jnp.float32), 'Wu1': jax.random.normal(ks[5], (HDIM, HDIM), dtype=jnp.float32) / np.sqrt(HDIM), 'bu1': jnp.zeros((HDIM,), dtype=jnp.float32), 'Wu2': jax.random.normal(ks[6], (HDIM, HDIM), dtype=jnp.float32) / np.sqrt(HDIM), 'bu2': jnp.zeros((HDIM,), dtype=jnp.float32), 'gamma': jnp.ones((HDIM,), dtype=jnp.float32), 'beta': jnp.zeros((HDIM,), dtype=jnp.float32)}
        return inp
    _L1_gnn_all = _L1_gnn_setup()
    _L1_gnn_in = {k: v for k, v in _L1_gnn_all.items() if k in ('Wf1', 'bf1', 'Wf2', 'bf2', 'Wu1', 'bu1', 'Wu2', 'bu2', 'gamma', 'beta')}
    del _L1_gnn_all

    def _L1_ffn_setup():
        import jax, jax.numpy as jnp
        import numpy as np
        BN_EPS = 0.001

        def _bn(h, g, b, m, v):
            return g * (h - m) * jax.lax.rsqrt(v + BN_EPS) + b
        key = jax.random.key(seed)
        ks = jax.random.split(key, 8)
        B, F, Df = (256, 64, 256)
        E, H, D = (8, 256, 256)
        s1 = 1.0 / np.sqrt(Df)
        s2 = 1.0 / np.sqrt(H)
        return {'x': jax.random.normal(ks[0], (B, F, Df), jnp.float32), 'Wr': jax.random.normal(ks[1], (Df, E), jnp.float32) * s1, 'br': jnp.zeros((E,), jnp.float32), 'W1': jax.random.normal(ks[2], (E, Df, H), jnp.float32) * s1, 'b1': jnp.zeros((E, H), jnp.float32), 'g1': jnp.ones((E, H), jnp.float32), 'be1': jnp.zeros((E, H), jnp.float32), 'm1': jnp.zeros((E, H), jnp.float32), 'v1': jnp.ones((E, H), jnp.float32), 'W2': jax.random.normal(ks[3], (E, H, H), jnp.float32) * s2, 'b2': jnp.zeros((E, H), jnp.float32), 'g2': jnp.ones((E, H), jnp.float32), 'be2': jnp.zeros((E, H), jnp.float32), 'm2': jnp.zeros((E, H), jnp.float32), 'v2': jnp.ones((E, H), jnp.float32), 'Wo': jax.random.normal(ks[4], (E, H, D), jnp.float32) * s2, 'bo': jnp.zeros((E, D), jnp.float32)}
    _L1_ffn_all = _L1_ffn_setup()
    _L1_ffn_in = {k: v for k, v in _L1_ffn_all.items() if k in ('Wr', 'br', 'W1', 'b1', 'g1', 'be1', 'm1', 'v1', 'W2', 'b2', 'g2', 'be2', 'm2', 'v2', 'Wo', 'bo')}
    del _L1_ffn_all
    return {'x': x, 'src': src, 'dst': dst, 'edge_attr_20': edge_attr_20, 'L0_gnn_weight': _L0_gnn_in['weight'], 'L0_gnn_attn_l': _L0_gnn_in['attn_l'], 'L0_gnn_attn_r': _L0_gnn_in['attn_r'], 'L0_ffn_gate_w': _L0_ffn_in['gate_w'], 'L0_ffn_gate_b': _L0_ffn_in['gate_b'], 'L0_ffn_w1': _L0_ffn_in['w1'], 'L0_ffn_b1': _L0_ffn_in['b1'], 'L0_ffn_w2': _L0_ffn_in['w2'], 'L0_ffn_b2': _L0_ffn_in['b2'], 'L1_gnn_Wf1': _L1_gnn_in['Wf1'], 'L1_gnn_bf1': _L1_gnn_in['bf1'], 'L1_gnn_Wf2': _L1_gnn_in['Wf2'], 'L1_gnn_bf2': _L1_gnn_in['bf2'], 'L1_gnn_Wu1': _L1_gnn_in['Wu1'], 'L1_gnn_bu1': _L1_gnn_in['bu1'], 'L1_gnn_Wu2': _L1_gnn_in['Wu2'], 'L1_gnn_bu2': _L1_gnn_in['bu2'], 'L1_gnn_gamma': _L1_gnn_in['gamma'], 'L1_gnn_beta': _L1_gnn_in['beta'], 'L1_ffn_Wr': _L1_ffn_in['Wr'], 'L1_ffn_br': _L1_ffn_in['br'], 'L1_ffn_W1': _L1_ffn_in['W1'], 'L1_ffn_b1': _L1_ffn_in['b1'], 'L1_ffn_g1': _L1_ffn_in['g1'], 'L1_ffn_be1': _L1_ffn_in['be1'], 'L1_ffn_m1': _L1_ffn_in['m1'], 'L1_ffn_v1': _L1_ffn_in['v1'], 'L1_ffn_W2': _L1_ffn_in['W2'], 'L1_ffn_b2': _L1_ffn_in['b2'], 'L1_ffn_g2': _L1_ffn_in['g2'], 'L1_ffn_be2': _L1_ffn_in['be2'], 'L1_ffn_m2': _L1_ffn_in['m2'], 'L1_ffn_v2': _L1_ffn_in['v2'], 'L1_ffn_Wo': _L1_ffn_in['Wo'], 'L1_ffn_bo': _L1_ffn_in['bo']}

def reference(x, src, dst, edge_attr_20, L0_gnn_weight, L0_gnn_attn_l, L0_gnn_attn_r, L0_ffn_gate_w, L0_ffn_gate_b, L0_ffn_w1, L0_ffn_b1, L0_ffn_w2, L0_ffn_b2, L1_gnn_Wf1, L1_gnn_bf1, L1_gnn_Wf2, L1_gnn_bf2, L1_gnn_Wu1, L1_gnn_bu1, L1_gnn_Wu2, L1_gnn_bu2, L1_gnn_gamma, L1_gnn_beta, L1_ffn_Wr, L1_ffn_br, L1_ffn_W1, L1_ffn_b1, L1_ffn_g1, L1_ffn_be1, L1_ffn_m1, L1_ffn_v1, L1_ffn_W2, L1_ffn_b2, L1_ffn_g2, L1_ffn_be2, L1_ffn_m2, L1_ffn_v2, L1_ffn_Wo, L1_ffn_bo):
    import jax
    import jax.numpy as jnp

    def _L0_gnn_ref(x, edge_index, weight, attn_l, attn_r):
        import jax, jax.numpy as jnp
        import numpy as np
        N, IN_CH, HEADS, OUT_CH, E = (50000, 256, 4, 64, 25000)
        heads, out_ch = attn_l.shape
        n = x.shape[0]
        xt = jnp.matmul(x, weight).reshape(-1, heads, out_ch)
        row, col = (edge_index[0], edge_index[1])
        alpha_l = jnp.einsum('ehd,hd->eh', xt[row], attn_l)
        alpha_r = jnp.einsum('ehd,hd->eh', xt[col], attn_r)
        alpha = jax.nn.softmax(jax.nn.leaky_relu(alpha_l + alpha_r, 0.01), axis=1)
        tmp = jnp.einsum('nh,nhd->nd', alpha[:n], xt[col[:n]])
        out = jnp.broadcast_to(tmp[:, None, :], (n, heads, out_ch))
        return out.reshape(n, heads * out_ch)

    def _L0_ffn_ref(h, gate_w, gate_b, w1, b1, w2, b2):
        import math
        import jax, jax.numpy as jnp
        import numpy as np
        CAPACITY_FACTOR = 1.25
        B, L, D = h.shape
        E = gate_w.shape[1]
        T = B * L
        C = max(1, math.ceil(CAPACITY_FACTOR * T / E))
        x = h.reshape(T, D)
        logits = x @ gate_w + gate_b
        probs = jax.nn.softmax(logits, axis=-1)
        idx = jnp.argmax(probs, axis=-1)
        prb = jnp.take_along_axis(probs, idx[:, None], axis=1)[:, 0]
        one_hot = jax.nn.one_hot(idx, E, dtype=jnp.float32)
        pos = (jnp.cumsum(one_hot, axis=0) * one_hot).sum(-1).astype(jnp.int32) - 1
        kept = pos < C
        pos_safe = jnp.where(kept, pos, C)
        buf = jnp.zeros((E, C, D), dtype=h.dtype).at[idx, pos_safe].set(x, mode='drop')
        hmid = jax.nn.relu(jnp.einsum('ecd,edf->ecf', buf, w1) + b1[:, None, :])
        ybuf = jnp.einsum('ecf,efd->ecd', hmid, w2) + b2[:, None, :]
        pos_g = jnp.minimum(pos, C - 1)
        y_tok = ybuf[idx, pos_g] * (prb * kept)[:, None]
        y = y_tok.reshape(B, L, D)
        y = jnp.nan_to_num(y, nan=0.0, posinf=10000.0, neginf=-10000.0)
        return y

    def _L1_gnn_ref(x, rbf, Wf1, bf1, Wf2, bf2, Wu1, bu1, Wu2, bu2, gamma, beta, ei):
        import jax, jax.numpy as jnp
        import numpy as np
        N, E, HDIM, NG = (10000, 10000, 256, 20)
        BN_EPS = 1e-05
        row, col = (ei[0], ei[1])
        filt = jax.nn.silu(rbf @ Wf1 + bf1) @ Wf2 + bf2
        msg = x[col] * filt
        agg = jax.ops.segment_sum(msg, row, num_segments=x.shape[0])
        h = jax.nn.silu(agg @ Wu1 + bu1) @ Wu2 + bu2
        mean = jnp.mean(h, axis=0)
        var = jnp.mean(jnp.square(h - mean), axis=0)
        bn = gamma * (h - mean) * jax.lax.rsqrt(var + BN_EPS) + beta
        return x + bn

    def _L1_ffn_ref(x, Wr, br, W1, b1, g1, be1, m1, v1, W2, b2, g2, be2, m2, v2, Wo, bo):
        import jax, jax.numpy as jnp
        import numpy as np
        BN_EPS = 0.001

        def _bn(h, g, b, m, v):
            return g * (h - m) * jax.lax.rsqrt(v + BN_EPS) + b
        feat = jnp.mean(x, axis=0)
        w = jax.nn.softmax(feat @ Wr + br, axis=-1)
        h = jnp.einsum('bfd,edh->bfeh', x, W1) + b1
        h = jax.nn.relu(_bn(h, g1, be1, m1, v1))
        h = jnp.einsum('bfeh,ehk->bfek', h, W2) + b2
        h = jax.nn.relu(_bn(h, g2, be2, m2, v2))
        y = jnp.einsum('bfeh,ehd->bfed', h, Wo) + bo
        return jnp.einsum('bfed,fe->bfd', y, w)
    edge_index = jnp.stack([src, dst])
    x = x + _L0_gnn_ref(_layernorm(x, axis=-1), edge_index, L0_gnn_weight, L0_gnn_attn_l, L0_gnn_attn_r)
    x = x + _L0_ffn_ref(_layernorm(x, axis=-1)[None], L0_ffn_gate_w, L0_ffn_gate_b, L0_ffn_w1, L0_ffn_b1, L0_ffn_w2, L0_ffn_b2)[0]
    x = x + _L1_gnn_ref(_layernorm(x, axis=-1), edge_attr_20, L1_gnn_Wf1, L1_gnn_bf1, L1_gnn_Wf2, L1_gnn_bf2, L1_gnn_Wu1, L1_gnn_bu1, L1_gnn_Wu2, L1_gnn_bu2, L1_gnn_gamma, L1_gnn_beta, edge_index)
    x = x + _L1_ffn_ref(_layernorm(x, axis=-1)[None], L1_ffn_Wr, L1_ffn_br, L1_ffn_W1, L1_ffn_b1, L1_ffn_g1, L1_ffn_be1, L1_ffn_m1, L1_ffn_v1, L1_ffn_W2, L1_ffn_b2, L1_ffn_g2, L1_ffn_be2, L1_ffn_m2, L1_ffn_v2, L1_ffn_Wo, L1_ffn_bo)[0]
    return x

_drawn_inputs = setup_inputs


def setup_inputs(seed=0):
    import zlib

    import numpy as np

    out = dict(_drawn_inputs(seed))
    spreads = {'L0_ffn_gate_b': (0.0, 0.1),
     'L0_ffn_b1': (0.0, 0.682),
     'L0_ffn_b2': (0.0, 0.47),
     'L1_gnn_bf1': (0.0, 0.1),
     'L1_gnn_bf2': (0.0, 0.1),
     'L1_gnn_bu1': (0.0, 0.402),
     'L1_gnn_bu2': (0.0, 0.8),
     'L1_gnn_gamma': (1.0, 0.2),
     'L1_gnn_beta': (0.0, 0.1),
     'L1_ffn_br': (0.0, 0.8),
     'L1_ffn_b1': (0.0, 0.721),
     'L1_ffn_g1': (1.0, 0.6),
     'L1_ffn_be1': (0.0, 0.786),
     'L1_ffn_m1': (0.0, 0.745),
     'L1_ffn_v1': (1.0, 0.6),
     'L1_ffn_b2': (0.0, 0.54),
     'L1_ffn_g2': (1.0, 0.6),
     'L1_ffn_be2': (0.0, 0.594),
     'L1_ffn_m2': (0.0, 0.526),
     'L1_ffn_v2': (1.0, 0.6),
     'L1_ffn_bo': (0.0, 0.406)}
    factors = {}
    for name, (base, spread) in spreads.items():
        noise = np.random.default_rng([zlib.crc32(name.encode()), seed]).standard_normal(out[name].shape)
        drawn = base * np.exp(spread * noise) if base else spread * noise
        out[name] = jnp.asarray(drawn.astype(out[name].dtype))
    for name, factor in factors.items():
        out[name] = (out[name] * factor).astype(out[name].dtype)
    return out
```

```python
from contextlib import ExitStack

import numpy as np

import concourse.bass as bass
from concourse import mybir

F32 = mybir.dt.float32
I32 = mybir.dt.int32
ALU = mybir.AluOpType
ACT = mybir.ActivationFunctionType
AX_X = mybir.AxisListType.X

N_NODES, D = 3125, 256
P = 125
TILES = N_NODES // P
HALF = 128
KD = D // HALF
LN_EPS = 1e-5

HEADS, HEAD_D = 4, 64
TAB = D + 2 * HEADS
LEAK = 0.01

EXPERTS = 8
FF = 1024
FC = FF // HALF
CAP = 489
SLOTS = 512
ROW_TILES = SLOTS // HALF
LAST_ROWS = CAP - (ROW_TILES - 1) * HALF
DROPPED = 2 * EXPERTS * SLOTS
FLT_MAX = 3.4028234663852886e38
BIG = 10000.0

N_EDGES = 53125
N_RBF = 20
E_TILES = N_EDGES // P
GROUP = 5
CHUNKS = E_TILES // GROUP
CE = GROUP * P
CUT = 3 * P
PIECES = ((0, CUT), (CUT, CE))
AGG_ROWS = N_NODES + P
BN_EPS = 1e-5
FOLD = 5
FOLDS = TILES // FOLD

BN2_EPS = 1e-3
TOK = 4
STEPS = [(s, min(TOK, TILES - s)) for s in range(0, TILES, TOK)]

CHAN = ["bf1", "bu1", "bu2", "gamma", "beta"]
PAIR = ["b1", "g1", "be1", "m1", "v1", "b2", "g2", "be2", "m2", "v2"]
CH_AT = {n: KD * k for k, n in enumerate(CHAN)}
PAIR_AT = {n: KD * len(CHAN) + k * EXPERTS * KD for k, n in enumerate(PAIR)}
FFB1_AT = KD * len(CHAN) + len(PAIR) * EXPERTS * KD
N_CHAN = FFB1_AT + EXPERTS * FC
ROW_AT = {"attn_l": 0, "attn_r": D, "bf2": 2 * D, "b2": 3 * D,
          "gate_b": (3 + EXPERTS) * D, "br": (3 + EXPERTS) * D + EXPERTS}
N_ROW = (3 + EXPERTS) * D + 2 * EXPERTS


class Tally:

    def __init__(self, sem):
        self.sem, self.n = sem, 0

    def inc(self, instruction, by=1):
        self.n += by
        instruction.then_inc(self.sem, by)
        return self.n


def build(nc, A, out):
    with ExitStack() as ctx:
        def sb(name, shape, dt=F32):
            return ctx.enter_context(nc.sbuf_tensor(name, shape, dt))

        def sem(name):
            return ctx.enter_context(nc.semaphore(name))

        def dram(name, shape):
            return nc.dram_tensor(name, shape, F32).ap()

        bank = [ctx.enter_context(nc.psum_tensor(f"bank{i}", [128, 512], F32)) for i in range(8)]

        tab_d = dram("tab_d", [N_NODES, TAB])
        al_d = dram("al_d", [N_NODES, HEADS])
        buf_d = dram("buf_d", [EXPERTS * SLOTS, D])
        ybuf_d = dram("ybuf_d", [EXPERTS * CAP, D])
        xn_d = dram("xn_d", [N_NODES, D])
        agg_d = [dram(f"agg{i}_d", [AGG_ROWS, D]) for i in range(GROUP)]

        x = sb("x_sb", [P, TILES, D])
        xn = sb("xn", [P, TILES, D])
        xT = sb("xT", [HALF, KD, N_NODES])
        chan = sb("chan_sb", [HALF, N_CHAN])
        rows = sb("rows_sb", [HALF, N_ROW])
        arena = sb("arena", [128, 21504])
        ident = sb("ident", [128, 128])
        ones = sb("ones", [128, 128])
        zeros = sb("zeros", [128, 2048])
        before = sb("before", [P, P])
        upper = sb("upper", [P, P])
        trash = sb("trash", [P, 1])
        rev = sb("rev", [P, EXPERTS])
        eno = sb("eno", [P, EXPERTS])
        stats = sb("stats", [P, TILES, 6])
        mv = sb("mv", [P, TILES, 2])
        rstd = sb("rstd", [P, TILES])
        eps1 = sb("eps1", [128, 2])
        sm8 = sb("sm8", [P, 6, TILES, EXPERTS])
        sm1 = sb("sm1", [P, 12, TILES])
        tot8 = sb("tot8", [P, EXPERTS])
        off8 = sb("off8", [P, EXPERTS])
        slot_i = sb("slot_i", [P, TILES], I32)
        row_i = sb("row_i", [P, TILES], I32)
        e0src = sb("e0src", [P, TILES], I32)
        e0dst = sb("e0dst", [P, TILES], I32)
        src_col = sb("src_col_sb", [P, E_TILES], I32)
        dst_col = sb("dst_col_sb", [P, E_TILES], I32)
        wf1 = sb("wf1", [N_RBF, D])
        wf2 = sb("wf2", [HALF, KD, D])
        wu1 = sb("wu1", [HALF, KD, D])
        wu2 = sb("wu2", [HALF, KD, D])
        waug = sb("waug", [HALF, KD, TAB])
        wprod = sb("wprod", [HALF, KD * HEADS, HEAD_D])
        gate_w = sb("gate_w_sb", [HALF, KD, EXPERTS])
        wr = sb("wr_sb", [HALF, KD, EXPERTS])
        bo = sb("bo_sb", [EXPERTS, D])
        mix = sb("mix", [P, TILES, EXPERTS])
        scl = sb("scl", [HALF, 2, EXPERTS * KD])
        shf = sb("shf", [HALF, 2, EXPERTS * KD])
        cstat = sb("cstat", [HALF, KD, 2 * FOLDS, 6])
        cmv = sb("cmv", [HALF, KD, 2])
        csc = sb("csc", [HALF, 3, KD])

        def carve(at, parts, *shape):
            size = int(np.prod(shape))
            v = arena[0:parts, at:at + size]
            if len(shape) == 2:
                v = v.rearrange("p (a b) -> p a b", b=shape[1])
            elif len(shape) == 3:
                v = v.rearrange("p (a b c) -> p a b c", b=shape[1], c=shape[2])
            return v

        tab = carve(0, P, TILES, TAB)
        tdst = carve(6600, P, TILES, TAB)
        tsrc = carve(13200, P, TILES, HEADS)
        brow = [carve(b * 1024, 128, ROW_TILES, D) for b in range(2)]
        bT = carve(2048, 128, KD, SLOTS)
        hid = [carve(3072 + b * 4096, 128, FC, SLOTS) for b in range(2)]
        yrow = [carve(11264 + b * 1024, 128, ROW_TILES, D) for b in range(2)]
        w1 = [carve(13312 + b * 2048, 128, KD, FF) for b in range(2)]
        w2 = [carve(17408 + b * 2048, 128, FC, D) for b in range(2)]
        yg = carve(3072, P, TILES, D)
        ytmp = [carve(9472 + b * 1280, P, 5, D) for b in range(2)]
        srow = [carve(b * CE, P, GROUP, P).bitcast(I32) for b in range(2)]
        attr = [carve(1250 + b * CE, N_RBF, CE) for b in range(2)]
        same = [carve(2500 + b * CE, P, GROUP, P) for b in range(2)]
        earlier = carve(3750, P, GROUP, P)
        eh = [carve(4375 + b * KD * CE, 128, KD, CE) for b in range(2)]
        xg = [carve(6875 + b * GROUP * D, P, GROUP, D) for b in range(2)]
        filt = [carve(9435 + b * D, P, D) for b in range(2)]
        msg = [carve(9947 + b * D, P, D) for b in range(2)]
        summed = [carve(10459 + b * GROUP * D, P, GROUP, D) for b in range(2)]
        dup = sb("dup", [P, 3, GROUP])
        srcf = sb("srcf", [P, GROUP])
        sidx = [sb(f"sidx{b}", [P, GROUP], I32) for b in range(2)]
        gidx = [sb(f"gidx{b}", [P, GROUP], I32) for b in range(2)]
        part = [[carve((b * GROUP + i) * FOLD * D, P, FOLD, D) for i in range(GROUP)] for b in range(2)]
        aggT = [carve(12800 + b * KD * FOLD * P, 128, KD, FOLD * P) for b in range(2)]
        uT = [carve(15300 + b * KD * FOLD * P, 128, KD, FOLD * P) for b in range(2)]
        mixT = carve(0, EXPERTS, N_NODES)
        dw = [carve(13312 + b * 3 * KD * D, 128, 3 * KD, D) for b in range(2)]
        h1 = [carve(16384 + b * KD * TOK * P, 128, KD, TOK * P) for b in range(2)]
        h2 = [carve(18432 + b * KD * TOK * P, 128, KD, TOK * P) for b in range(2)]

        row = {k: rows[:, v:v + (EXPERTS * D if k == "b2" else EXPERTS if k in ("gate_b", "br") else D)]
               for k, v in ROW_AT.items()}

        consts_ready = sem("consts_ready")
        x_in = sem("x_in")
        idx_in = sem("idx_in")
        vec_in = sem("vec_in")
        gnn_w_in = sem("gnn_w_in")
        small_w_in = sem("small_w_in")
        zero_filled = sem("zero_filled")
        dve_chain = sem("dve_chain")
        act_chain = sem("act_chain")
        waug_ready = sem("waug_ready")
        ln_var = [sem(f"ln_var{k}") for k in range(4)]
        ln_std = [sem(f"ln_std{k}") for k in range(4)]
        ln_tile = [sem(f"ln_tile{k}") for k in range(4)]
        turned = [sem(f"turned{k}") for k in range(3)]
        turned_copied = [sem(f"turned_copied{k}") for k in range(3)]
        tab_mm = sem("tab_mm")
        tab_copied = sem("tab_copied")
        tab_stored = sem("tab_stored")
        tab_gathered = sem("tab_gathered")
        att_shift = sem("att_shift")
        att_exp = sem("att_exp")
        gate_mm = sem("gate_mm")
        gate_shift = sem("gate_shift")
        gate_exp = sem("gate_exp")
        count_ready = sem("count_ready")
        count_mm = sem("count_mm")
        slots_ready = sem("slots_ready")
        scattered = sem("scattered")
        brow_in = [sem(f"brow_in{b}") for b in range(2)]
        ffw_in = [sem(f"ffw_in{b}") for b in range(2)]
        b_turned = sem("b_turned")
        b_copied = sem("b_copied")
        ff1_mm = sem("ff1_mm")
        ff1_act = sem("ff1_act")
        ff2_mm = sem("ff2_mm")
        ff2_bias = sem("ff2_bias")
        y_stored = [sem(f"y_stored{b}") for b in range(2)]
        y_gathered = sem("y_gathered")
        x2_ready = sem("x2_ready")
        xn_stored = sem("xn_stored")
        srow_in = [sem(f"srow_in{b}") for b in range(2)]
        attr_in = [sem(f"attr_in{b}") for b in range(2)]
        same_ready = sem("same_ready")
        sidx_ready = sem("sidx_ready")
        gidx_ready = sem("gidx_ready")
        e1_mm = sem("e1_mm")
        e1_silu = sem("e1_silu")
        e2_mm = sem("e2_mm")
        filt_ready = sem("filt_ready")
        msg_ready = sem("msg_ready")
        sum_mm = sem("sum_mm")
        sum_copied = sem("sum_copied")
        xg_in = [[sem(f"xg_in{b}_{t}") for t in range(GROUP)] for b in range(2)]
        added = [sem(f"added{t}") for t in range(GROUP)]
        edge_chain = sem("edge_chain")
        part_in = [sem(f"part_in{b}") for b in range(2)]
        agg_ready = sem("agg_ready")
        agg_turned = sem("agg_turned")
        agg_copied = sem("agg_copied")
        u_mm = sem("u_mm")
        u_silu = sem("u_silu")
        h_mm = sem("h_mm")
        h_ready = sem("h_ready")
        bn_var = sem("bn_var")
        bn_std = sem("bn_std")
        bn_scale = sem("bn_scale")
        bn_applied = sem("bn_applied")
        bn_turned = sem("bn_turned")
        x3_ready = sem("x3_ready")
        mix_mm = sem("mix_mm")
        mix_shift = sem("mix_shift")
        mix_exp = sem("mix_exp")
        mix_ready = sem("mix_ready")
        mix_turned = sem("mix_turned")
        mixT_ready = sem("mixT_ready")
        bo_mm = sem("bo_mm")
        bo_added = sem("bo_added")
        aff_var = sem("aff_var")
        aff_std = sem("aff_std")
        aff_ready = sem("aff_ready")
        dw_in = [sem(f"dw_in{b}") for b in range(2)]
        d1_mm = sem("d1_mm")
        d1_act = sem("d1_act")
        d2_mm = sem("d2_mm")
        d2_act = sem("d2_act")
        d3_mm = sem("d3_mm")
        d3_added = sem("d3_added")
        stored = sem("stored")
        sp_passed = sem("sp_passed")
        pool_passed = sem("pool_passed")
        act_passed = sem("act_passed")

        def ff1_bank(e, b, f):
            return bank[2 + (b * FC + f) % 4]

        block = ctx.enter_context(nc.Block())

        def waits(eng, passed, *needs):
            for s, v in needs:
                eng.wait_ge(s, v)
            eng.sem_inc(passed, 1)

        NS = len(STEPS)
        D3 = TILES

        @block.sync
        def _(sp):
            sp.dma_start(x[:], A["x"].rearrange("(p t) d -> p t d", t=TILES)).then_inc(x_in, 16)
            sp.dma_start(rows[:], A["rows"].partition_broadcast(HALF)).then_inc(vec_in, 16)
            sp.dma_start(waug[:, :, 0:D], A["gnn_w"].rearrange("(k p) d -> p k d", p=HALF)).then_inc(gnn_w_in, 16)
            sp.dma_start(chan[:], A["chan"]).then_inc(vec_in, 16)
            sp.dma_start(e0src[:], A["src"][0:N_NODES].rearrange("(p t) -> p t", t=TILES)).then_inc(idx_in, 16)
            sp.dma_start(e0dst[:], A["dst"][0:N_NODES].rearrange("(p t) -> p t", t=TILES)).then_inc(idx_in, 16)
            sp.dma_start(src_col[:], A["src_col"]).then_inc(idx_in, 16)
            sp.dma_start(dst_col[:], A["dst_col"]).then_inc(idx_in, 16)
            sp.dma_start(gate_w[:], A["gate_w"].rearrange("(k p) e -> p k e", p=HALF)).then_inc(small_w_in, 16)
            sp.dma_start(wr[:], A["wr"].rearrange("(k p) e -> p k e", p=HALF)).then_inc(small_w_in, 16)
            sp.dma_start(bo[:], A["bo"]).then_inc(small_w_in, 16)
            sp.dma_start(wf1[:], A["wf1"]).then_inc(small_w_in, 16)
            for w, name in ((wf2, "wf2"), (wu1, "wu1"), (wu2, "wu2")):
                sp.dma_start(w[:], A[name].rearrange("(k p) d -> p k d", p=HALF)).then_inc(small_w_in, 16)

            sp.wait_ge(consts_ready, 1)
            for q in range(4):
                sp.dma_start(buf_d[q * 1024:(q + 1) * 1024, :].rearrange("(p r) d -> p (r d)", p=128),
                             zeros[:]).then_inc(zero_filled, 16)
            zq = [(i, q) for i in range(GROUP) for q in range(4)]
            for i, q in zq:
                lo, hi = q * 1024, min((q + 1) * 1024, AGG_ROWS)
                n = (hi - lo) // 128 if hi - lo == 1024 else 0
                if n:
                    sp.dma_start(agg_d[i][lo:hi, :].rearrange("(p r) d -> p (r d)", p=128),
                                 zeros[:]).then_inc(zero_filled, 16)
                else:
                    sp.dma_start(agg_d[i][lo:hi, :].rearrange("(p r) d -> p (r d)", r=2),
                                 zeros[0:(hi - lo) // 2, 0:2 * D]).then_inc(zero_filled, 16)

            sp.wait_ge(tab_copied, TILES)
            sp.dma_start(tab_d.rearrange("(p t) c -> p t c", t=TILES), tab[:]).then_inc(tab_stored, 16)
            sp.dma_start(al_d.rearrange("(p t) c -> p t c", t=TILES),
                         tab[:, :, D:D + HEADS]).then_inc(tab_stored, 16)

            def expert_loads(e, b, n, warm):
                if warm:
                    waits(sp, sp_passed, (ff1_mm, (e - 1) * FC))
                    waits(sp, sp_passed, (ff2_mm, (e - 1) * ROW_TILES))
                sp.dma_start(w1[b], A["w1"][bass.ds(e, 1)].rearrange("o (k p) f -> p (o k) f", p=HALF)).then_inc(ffw_in[b], 16)
                sp.dma_start(w2[b], A["w2"][bass.ds(e, 1)].rearrange("o (k p) f -> p (o k) f", p=HALF)).then_inc(ffw_in[b], 16)

            def expert_rows(e, b, warm):
                if warm:
                    waits(sp, sp_passed, (b_turned, (e - 1) * KD))
                sp.dma_start(brow[b], buf_d[bass.ds(e * SLOTS, SLOTS), :].rearrange("(j p) d -> p j d", p=128)).then_inc(brow_in[b], 16)

            def expert_store(e, b):
                waits(sp, sp_passed, (ff2_bias, (e + 1) * ROW_TILES))
                full = (ROW_TILES - 1) * HALF
                sp.dma_start(ybuf_d[bass.ds(e * CAP, full), :].rearrange("(j p) d -> p j d", p=128),
                             yrow[b][:, 0:ROW_TILES - 1, :]).then_inc(y_stored[b], 16)
                sp.dma_start(ybuf_d[bass.ds(e * CAP + full, LAST_ROWS), :],
                             yrow[b][0:LAST_ROWS, ROW_TILES - 1, :]).then_inc(y_stored[b], 16)

            sp.wait_ge(att_shift, 1)
            for b in range(2):
                expert_loads(b, b, 0, False)
            sp.wait_ge(scattered, 16 * TILES)
            sp.wait_ge(tab_gathered, 16 * 2 * TILES)
            for b in range(2):
                expert_rows(b, b, False)
            with sp.Fori(0, EXPERTS // 2 - 1) as i:
                for b in range(2):
                    expert_loads(i * 2 + 2 + b, b, 0, True)
                    expert_rows(i * 2 + 2 + b, b, True)
                    expert_store(i * 2 + b, b)
            for b in range(2):
                expert_store(EXPERTS - 2 + b, b)

            sp.wait_ge(ln_tile[2], TILES)
            sp.dma_start(xn_d.rearrange("(p t) d -> p t d", t=TILES), xn[:]).then_inc(xn_stored, 16)

            def edge_loads(c, b, warm):
                if warm:
                    waits(sp, sp_passed, (same_ready, c - 1))
                    waits(sp, sp_passed, (e1_mm, 4 * (c - 1)))
                sp.dma_start(srow[b].rearrange("p g e -> p (g e)"),
                             A["src"][bass.ds(c * CE, CE)].partition_broadcast(P)).then_inc(srow_in[b], 16)
                sp.dma_start(attr[b], A["rbf_t"][:, bass.ds(c * CE, CE)]).then_inc(attr_in[b], 16)

            sp.wait_ge(x2_ready, FOLDS)
            for c in range(2):
                edge_loads(c, c, False)
            with sp.Fori(1, CHUNKS // 2) as i:
                for b in range(2):
                    edge_loads(i * 2 + b, b, True)
            edge_loads(CHUNKS - 1, 0, True)

            for i in range(GROUP):
                sp.wait_ge(added[i], 16 * CHUNKS)
            for f in range(FOLDS):
                if f >= 2:
                    sp.wait_ge(agg_turned, (f - 1) * FOLD)
                for i in range(GROUP):
                    src = agg_d[i][0:N_NODES, :].rearrange("(p t) d -> p t d", t=TILES)
                    sp.dma_start(part[f % 2][i], src[:, f * FOLD:(f + 1) * FOLD, :]).then_inc(part_in[f % 2], 16)

            def dense_loads(e, b, warm):
                if warm:
                    waits(sp, sp_passed, (d3_mm, (e - 1) * D3))
                for j, name in enumerate(("dw1", "dw2", "dwo")):
                    sp.dma_start(dw[b][:, j * KD:(j + 1) * KD, :],
                                 A[name][bass.ds(e, 1)].rearrange("o (k p) d -> p (o k) d", p=HALF)).then_inc(dw_in[b], 16)

            sp.wait_ge(h_ready, FOLDS * 2 * KD)
            for b in range(2):
                dense_loads(b, b, False)
            with sp.Fori(0, EXPERTS // 2 - 1) as i:
                for b in range(2):
                    dense_loads(i * 2 + 2 + b, b, True)

            sp.wait_ge(d3_added, EXPERTS * D3)
            sp.dma_start(out.rearrange("(p t) d -> p t d", t=TILES), x[:]).then_inc(stored, 16)
            sp.wait_ge(stored, 16)

        @block.gpsimd
        def _(pool):
            made = Tally(sem("pool_made"))
            pool.memset(zeros[:], 0.0).then_inc(consts_ready, 1)
            made.inc(pool.memset(ident[:], 0.0))
            made.inc(pool.memset(ones[:], 1.0))
            made.inc(pool.memset(before[:], 1.0))
            made.inc(pool.memset(upper[:], 1.0))
            made.inc(pool.memset(eps1[:, 0:1], LN_EPS))
            made.inc(pool.memset(eps1[:, 1:2], BN2_EPS))
            pool.wait_ge(made.sem, made.n)
            pool.affine_select(out=ident[:], in_=ident[:], compare_op=ALU.not_equal, fill=1.0, base=0,
                               pattern=[[-1, 128]], channel_multiplier=1).then_inc(consts_ready, 1)
            pool.affine_select(out=before[:], in_=before[:], compare_op=ALU.is_gt, fill=0.0, base=0,
                               pattern=[[-1, P]], channel_multiplier=1).then_inc(consts_ready, 1)
            pool.affine_select(out=upper[:], in_=upper[:], compare_op=ALU.is_gt, fill=0.0, base=0,
                               pattern=[[1, P]], channel_multiplier=-1).then_inc(consts_ready, 1)
            pool.iota(trash[:], pattern=[[0, 1]], base=N_NODES, channel_multiplier=1,
                      allow_small_or_imprecise_dtypes=True).then_inc(consts_ready, 1)
            pool.iota(rev[:], pattern=[[-1, EXPERTS]], base=EXPERTS, channel_multiplier=0,
                      allow_small_or_imprecise_dtypes=True).then_inc(consts_ready, 1)
            pool.iota(eno[:], pattern=[[1, EXPERTS]], base=0, channel_multiplier=0,
                      allow_small_or_imprecise_dtypes=True).then_inc(consts_ready, 1)

            pool.wait_ge(idx_in, 64)
            pool.wait_ge(tab_stored, 32)
            for t in range(TILES):
                pool.indirect_dma_start(tdst[:, t, :], None, tab_d, bass.IndirectOffsetOnAxis(ap=e0dst[:, t:t + 1], axis=0)).then_inc(tab_gathered, 16)
                pool.indirect_dma_start(tsrc[:, t, :], None, al_d, bass.IndirectOffsetOnAxis(ap=e0src[:, t:t + 1], axis=0)).then_inc(tab_gathered, 16)

            pool.wait_ge(zero_filled, 16 * 4 + 16 * GROUP * 4)
            pool.wait_ge(slots_ready, 1)
            for t in range(TILES):
                pool.indirect_dma_start(buf_d, bass.IndirectOffsetOnAxis(ap=slot_i[:, t:t + 1], axis=0), xn[:, t, :], None,
                                        bounds_check=EXPERTS * SLOTS - 1, oob_is_err=False).then_inc(scattered, 16)
            pool.wait_ge(slots_ready, 2)
            for b in range(2):
                pool.wait_ge(y_stored[b], EXPERTS // 2 * 32)
            for t in range(TILES):
                pool.indirect_dma_start(yg[:, t, :], None, ybuf_d, bass.IndirectOffsetOnAxis(ap=row_i[:, t:t + 1], axis=0)).then_inc(y_gathered, 16)

            def copy_gather_indices(c, b, warm):
                if warm:
                    for t in range(GROUP):
                        pool.wait_ge(xg_in[b][t], (c // 2) * 16 if isinstance(c, int) else (c - b) * 8)
                pool.tensor_copy(gidx[b][:], dst_col[:, bass.ds(c * GROUP, GROUP)]).then_inc(gidx_ready, 1)

            def gather(c, b, t, warm):
                waits(pool, pool_passed, (gidx_ready, c + 1), *([(msg_ready, (c - 2) * GROUP + t + 1)] if warm else []))
                pool.indirect_dma_start(xg[b][:, t, :], None, xn_d, bass.IndirectOffsetOnAxis(ap=gidx[b][:, t:t + 1], axis=0)).then_inc(xg_in[b][t], 16)

            def scatter(c, b, t, warm):
                waits(pool, pool_passed, (sidx_ready, c + 1), (sum_copied, c * GROUP + t + 1), *([(added[t], c * 16)] if warm else []))
                pool.indirect_dma_start(agg_d[t], bass.IndirectOffsetOnAxis(ap=sidx[b][:, t:t + 1], axis=0), summed[b][:, t, :], None,
                                        compute_op=ALU.add).then_inc(added[t], 16)

            def edge_chunk(c, b, last=False):
                if not last:
                    warm_next = not isinstance(c, int) or c >= 1
                    copy_gather_indices(c + 1, 1 - b, warm_next)
                for t in range(GROUP):
                    if not last:
                        gather(c + 1, 1 - b, t, warm_next)
                    scatter(c, b, t, not isinstance(c, int) or c >= 1)

            pool.wait_ge(xn_stored, 16)
            copy_gather_indices(0, 0, False)
            for t in range(GROUP):
                gather(0, 0, t, False)
            for c in range(2):
                edge_chunk(c, c)
            with pool.Fori(1, CHUNKS // 2) as i:
                for b in range(2):
                    edge_chunk(i * 2 + b, b)
            edge_chunk(CHUNKS - 1, 0, last=True)

        @block.tensor
        def _(pe):
            pe.wait_ge(consts_ready, 4)

            def turn(k, t, src):
                pe.wait_ge(ln_tile[LN_OF[k]], t + 1)
                if t >= 2:
                    pe.wait_ge(turned_copied[k], t - 1)
                for j in range(KD):
                    ins = pe.transpose(bank[t % 2][:, j * P:(j + 1) * P], src[:, t, j * HALF:(j + 1) * HALF], ident[0:P, 0:P])
                ins.then_inc(turned[k], 1)

            LN_OF = (0, 1, 3)

            pe.wait_ge(waug_ready, 1)

            def table(t):
                pe.wait_ge(turned_copied[0], t + 1)
                if t >= 2:
                    pe.wait_ge(tab_copied, t - 1)
                for k in range(KD):
                    ins = pe.matmul(bank[2 + t % 2][0:P, 0:TAB], xT[:, k, t * P:(t + 1) * P], waug[:, k, :], start=k == 0, stop=k == KD - 1)
                ins.then_inc(tab_mm, 1)

            for t in range(TILES + 1):
                if t < TILES:
                    turn(0, t, xn)
                if t >= 1:
                    table(t - 1)

            def gate(k, t, w, done):
                pe.wait_ge(turned_copied[k], t + 1)
                for j in range(KD):
                    ins = pe.matmul(bank[4][0:P, t * EXPERTS:(t + 1) * EXPERTS], xT[:, j, t * P:(t + 1) * P], w[:, j, :], start=j == 0, stop=j == KD - 1)
                ins.then_inc(done, 1)

            pe.wait_ge(small_w_in, 16 * 7)
            for t in range(TILES + 1):
                if t < TILES:
                    turn(1, t, xn)
                if t >= 1:
                    gate(1, t - 1, gate_w, gate_mm)
            pe.wait_ge(count_ready, 1)
            pe.matmul(bank[5][0:P, 0:EXPERTS], upper[:], tot8[:], start=True, stop=True).then_inc(count_mm, 1)

            def expert(e, b, n):
                warm = not isinstance(e, int) or e >= 1
                pe.wait_ge(brow_in[b], n * 16)
                if warm:
                    pe.wait_ge(b_copied, e * KD)
                for k in range(KD):
                    for j in range(ROW_TILES):
                        ins = pe.transpose(bank[k][:, j * HALF:(j + 1) * HALF], brow[b][:, j, k * HALF:(k + 1) * HALF], ident[:])
                    ins.then_inc(b_turned, 1)
                pe.wait_ge(ffw_in[b], n * 32)
                pe.wait_ge(b_copied, (e + 1) * KD)
                for f in range(FC):
                    if warm or f >= 3:
                        pe.wait_ge(ff1_act, e * FC + f - 2)
                    for k in range(KD):
                        ins = pe.matmul(ff1_bank(e, b, f)[:, 0:CAP], w1[b][:, k, f * HALF:(f + 1) * HALF], bT[:, k, 0:CAP], start=k == 0, stop=k == KD - 1)
                    ins.then_inc(ff1_mm, 1)
                pe.wait_ge(ff1_act, (e + 1) * FC)
                for j in range(ROW_TILES):
                    m = HALF if j < ROW_TILES - 1 else LAST_ROWS
                    if warm or j >= 2:
                        pe.wait_ge(ff2_bias, e * ROW_TILES + j - 1)
                    for f in range(FC):
                        ins = pe.matmul(bank[6 + j % 2][0:m, 0:D], hid[b][:, f, j * HALF:j * HALF + m], w2[b][:, f, :], start=f == 0, stop=f == FC - 1)
                    ins.then_inc(ff2_mm, 1)

            for e in range(2):
                expert(e, e, 1)
            with pe.Fori(1, EXPERTS // 2) as i:
                for b in range(2):
                    expert(i * 2 + b, b, i + 1)

            def edge_first(c, b, n):
                pe.wait_ge(attr_in[b], n * 16)
                for a, (lo, hi) in enumerate(PIECES):
                    for k in range(KD):
                        if not isinstance(c, int) or c >= 1:
                            pe.wait_ge(e1_silu, (c - 1) * 4 + 2 * a + k + 1)
                        pe.matmul(bank[2 * a + k][:, 0:hi - lo], wf1[:, k * HALF:(k + 1) * HALF], attr[b][:, lo:hi],
                                  start=True, stop=True).then_inc(e1_mm, 1)

            def edge_filter(c, b, t):
                if t == 0:
                    pe.wait_ge(e1_silu, c * 4 + 2)
                if t == 3:
                    pe.wait_ge(e1_silu, c * 4 + 4)
                g = c * GROUP + t
                if not isinstance(c, int) or g >= 2:
                    pe.wait_ge(filt_ready, g - 1)
                for k in range(KD):
                    ins = pe.matmul(bank[4 + (b + t) % 2][0:P, 0:D], eh[b][:, k, t * P:(t + 1) * P], wf2[:, k, :], start=k == 0, stop=k == KD - 1)
                ins.then_inc(e2_mm, 1)

            def edge_sum(c, b, t):
                g = c * GROUP + t
                pe.wait_ge(msg_ready, g + 1)
                pe.wait_ge(same_ready, c + 1)
                if not isinstance(c, int) or g >= 2:
                    pe.wait_ge(sum_copied, g - 1)
                pe.matmul(bank[6 + (b + t) % 2][0:P, 0:D], same[b][:, t, :], msg[(b + t) % 2], start=True, stop=True).then_inc(sum_mm, 1)

            def edge_chunk(c, b, n_next, last=False):
                if not last:
                    edge_first(c + 1, 1 - b, n_next)
                for t in range(GROUP + 1):
                    if t < GROUP:
                        edge_filter(c, b, t)
                    if t >= 1:
                        edge_sum(c, b, t - 1)

            pe.wait_ge(ff2_bias, EXPERTS * ROW_TILES)
            edge_first(0, 0, 1)
            edge_chunk(0, 0, 1)
            edge_chunk(1, 1, 2)
            with pe.Fori(1, CHUNKS // 2) as i:
                edge_chunk(i * 2, 0, i + 1)
                edge_chunk(i * 2 + 1, 1, i + 2)
            edge_chunk(CHUNKS - 1, 0, None, last=True)

            pe.wait_ge(sum_copied, E_TILES)

            def fold_turn(f):
                pe.wait_ge(agg_ready, f + 1)
                for q in range(FOLD):
                    g = f * FOLD + q
                    if g >= 2:
                        pe.wait_ge(agg_copied, g - 1)
                    for k in range(KD):
                        ins = pe.transpose(bank[g % 2][:, k * P:(k + 1) * P], part[f % 2][0][:, q, k * HALF:(k + 1) * HALF], ident[0:P, 0:P])
                    ins.then_inc(agg_turned, 1)

            def fold_layer(f, w, src, used, need, done, at):
                pe.wait_ge(used, need)
                for a, (lo, hi) in enumerate(PIECES):
                    for o in range(KD):
                        n = f * 4 + a * 2 + o
                        if n >= 2:
                            pe.wait_ge(u_silu if done is u_mm else h_ready, n - 1)
                        for k in range(KD):
                            ins = pe.matmul(bank[at + o][:, 0:hi - lo], w[:, k, o * HALF:(o + 1) * HALF], src[:, k, lo:hi], start=k == 0, stop=k == KD - 1)
                        ins.then_inc(done, 1)

            for f in range(FOLDS + 1):
                if f < FOLDS:
                    fold_turn(f)
                    fold_layer(f, wu1, aggT[f % 2], agg_copied, (f + 1) * FOLD, u_mm, 2)
                if f >= 1:
                    fold_layer(f - 1, wu2, uT[(f - 1) % 2], u_silu, f * 4, h_mm, 4)
            for t in range(TILES):
                pe.wait_ge(bn_applied, KD * FOLDS if t >= TILES - 1 else KD * (t // FOLD + 1))
                if t >= 2:
                    pe.wait_ge(x3_ready, t - 1)
                for k in range(KD):
                    ins = pe.transpose(bank[6 + t % 2][0:P, k * HALF:(k + 1) * HALF], xT[:, k, t * P:(t + 1) * P], ident[:])
                ins.then_inc(bn_turned, 1)

            for t in range(TILES + 1):
                if t < TILES:
                    turn(2, t, xn)
                if t >= 1:
                    gate(2, t - 1, wr, mix_mm)
            pe.wait_ge(mix_ready, 1)
            for t in range(TILES):
                if t >= 2:
                    pe.wait_ge(mixT_ready, t - 1)
                pe.transpose(bank[2 + t % 2][0:EXPERTS, 0:P], mix[:, t, :], ident[0:P, 0:P]).then_inc(mix_turned, 1)
            for t in range(TILES):
                pe.wait_ge(mixT_ready, t + 1)
                if t >= 2:
                    pe.wait_ge(bo_added, t - 1)
                pe.matmul(bank[6 + t % 2][0:P, 0:D], mixT[:, t * P:(t + 1) * P], bo[:], start=True, stop=True).then_inc(bo_mm, 1)

            def dense_first(e, b, s, layer):
                at, n = STEPS[s]
                m = n * P
                done, act = ((d1_mm, d1_act), (d2_mm, d2_act))[layer]
                g = e * (NS * KD) + s * KD
                if layer == 1:
                    pe.wait_ge(d1_act, g + KD)
                for o in range(KD):
                    if not isinstance(e, int) or e or s:
                        pe.wait_ge(act, g + o - 1)
                    for k in range(KD):
                        rhs = xT[:, k, at * P:at * P + m] if layer == 0 else h1[s % 2][:, k, 0:m]
                        ins = pe.matmul(bank[2 * layer + o][:, 0:m], dw[b][:, layer * KD + k, o * HALF:(o + 1) * HALF], rhs, start=k == 0, stop=k == KD - 1)
                    ins.then_inc(done, 1)

            def dense_last(e, b, s):
                at, n = STEPS[s]
                pe.wait_ge(d2_act, e * (NS * KD) + s * KD + KD)
                for q in range(n):
                    g = e * D3 + at + q
                    if not isinstance(e, int) or e or at + q >= 2:
                        pe.wait_ge(d3_added, g - 1)
                    for k in range(KD):
                        ins = pe.matmul(bank[4 + (b + at + q) % 2][0:P, 0:D], h2[s % 2][:, k, q * P:(q + 1) * P], dw[b][:, 2 * KD + k, :], start=k == 0, stop=k == KD - 1)
                    ins.then_inc(d3_mm, 1)

            def dense_expert(e, b, n):
                pe.wait_ge(dw_in[b], n * 48)
                for s in range(NS + 2):
                    if s < NS:
                        dense_first(e, b, s, 0)
                    if 1 <= s <= NS:
                        dense_first(e, b, s - 1, 1)
                    if s >= 2:
                        dense_last(e, b, s - 2)

            pe.wait_ge(mix_shift, 1)
            pe.wait_ge(bo_added, TILES)
            for e in range(2):
                dense_expert(e, e, 1)
            with pe.Fori(1, EXPERTS // 2) as i:
                for b in range(2):
                    dense_expert(i * 2 + b, b, i + 1)

        @block.scalar
        def _(act):
            def ln_sqrt(k):
                act.wait_ge(ln_var[k], 1)
                act.activation(rstd[:], mv[:, :, 1], ACT.Sqrt, bias=eps1[0:P, 0:1]).then_inc(ln_std[k], 1)

            def turn_copies(k):
                for t in range(TILES):
                    act.wait_ge(turned[k], t + 1)
                    act.activation(xT[:, :, t * P:(t + 1) * P], bank[t % 2][:, 0:KD * P].rearrange("p (k e) -> p k e", k=KD), ACT.Copy).then_inc(turned_copied[k], 1)

            act.wait_ge(consts_ready, 7)
            ln_sqrt(0)
            act.wait_ge(vec_in, 32)
            for j, v in enumerate(("v1", "v2")):
                ins = act.activation(scl[:, j, :], chan[:, PAIR_AT[v]:PAIR_AT[v] + EXPERTS * KD], ACT.Sqrt, bias=eps1[:, 1:2])
                ins.then_inc(aff_std, 1)
            turn_copies(0)
            act.wait_ge(att_shift, 1)
            act.activation(sm8[:, 1, :, 0:HEADS], sm8[:, 0, :, 0:HEADS], ACT.Exp).then_inc(att_exp, 1)
            ln_sqrt(1)
            turn_copies(1)
            act.wait_ge(gate_shift, 1)
            act.activation(sm8[:, 2, :, :], sm8[:, 1, :, :], ACT.Exp).then_inc(gate_exp, 1)

            def expert(e, b, n):
                for k in range(KD):
                    act.wait_ge(b_turned, e * KD + k + 1)
                    if not isinstance(e, int) or e >= 1:
                        act.wait_ge(ff1_mm, e * FC)
                    act.activation(bT[:, k, :], bank[k][:], ACT.Copy).then_inc(b_copied, 1)
                for f in range(FC):
                    waits(act, act_passed, (ff1_mm, e * FC + f + 1), *([] if isinstance(e, int) and e < 2 else [(ff2_mm, (e - 1) * ROW_TILES)]))
                    act.activation(hid[b][:, f, 0:CAP], ff1_bank(e, b, f)[:, 0:CAP], ACT.Relu,
                                   bias=chan[:, bass.ds(e * FC + FFB1_AT + f, 1)]).then_inc(ff1_act, 1)

            for e in range(2):
                expert(e, e, 1)
            with act.Fori(1, EXPERTS // 2) as i:
                for b in range(2):
                    expert(i * 2 + b, b, i + 1)

            ln_sqrt(2)

            def edge_silu(c, b):
                for a, (lo, hi) in enumerate(PIECES):
                    for k in range(KD):
                        act.wait_ge(e1_mm, c * 4 + 2 * a + k + 1)
                        if not isinstance(c, int) or c >= 2:
                            act.wait_ge(e2_mm, (c - 1) * GROUP)
                        act.activation(eh[b][:, k, lo:hi], bank[2 * a + k][:, 0:hi - lo], ACT.Silu,
                                       bias=chan[:, CH_AT["bf1"] + k:CH_AT["bf1"] + k + 1]).then_inc(e1_silu, 1)

            def edge_chunk(c, b, last=False):
                if not last:
                    edge_silu(c + 1, 1 - b)
                for t in range(GROUP):
                    g = c * GROUP + t
                    act.wait_ge(sum_mm, g + 1)
                    if not isinstance(c, int) or c >= 2:
                        act.wait_ge(added[t], (c - 1) * 16)
                    act.activation(summed[b][:, t, :], bank[6 + (b + t) % 2][0:P, 0:D], ACT.Copy).then_inc(sum_copied, 1)

            act.wait_ge(x2_ready, FOLDS)
            edge_silu(0, 0)
            for c in range(2):
                edge_chunk(c, c)
            with act.Fori(1, CHUNKS // 2) as i:
                for b in range(2):
                    edge_chunk(i * 2 + b, b)
            edge_chunk(CHUNKS - 1, 0, last=True)

            def fold_copies(f):
                for q in range(FOLD):
                    g = f * FOLD + q
                    act.wait_ge(agg_turned, g + 1)
                    if f >= 2:
                        act.wait_ge(u_mm, (f - 1) * 4)
                    act.activation(aggT[f % 2][:, :, q * P:(q + 1) * P], bank[g % 2][:, 0:KD * P].rearrange("p (k e) -> p k e", k=KD), ACT.Copy).then_inc(agg_copied, 1)
                for a, (lo, hi) in enumerate(PIECES):
                    for o in range(KD):
                        act.wait_ge(u_mm, f * 4 + a * 2 + o + 1)
                        if f >= 2:
                            act.wait_ge(h_mm, (f - 1) * 4)
                        act.activation(uT[f % 2][:, o, lo:hi], bank[2 + o][:, 0:hi - lo], ACT.Silu,
                                       bias=chan[:, CH_AT["bu1"] + o:CH_AT["bu1"] + o + 1]).then_inc(u_silu, 1)

            def fold_bias(f):
                for a, (lo, hi) in enumerate(PIECES):
                    for o in range(KD):
                        act.wait_ge(h_mm, f * 4 + a * 2 + o + 1)
                        act.activation(xT[:, o, f * FOLD * P + lo:f * FOLD * P + hi], bank[4 + o][:, 0:hi - lo], ACT.Identity,
                                       bias=chan[:, CH_AT["bu2"] + o:CH_AT["bu2"] + o + 1]).then_inc(h_ready, 1)

            for f in range(FOLDS + 1):
                if f < FOLDS:
                    fold_copies(f)
                if f >= 1:
                    fold_bias(f - 1)
            act.wait_ge(bn_var, 1)
            act.activation(csc[:, 0, :], cmv[:, :, 1], ACT.Sqrt, bias=eps1[:, 0:1]).then_inc(bn_std, 1)
            act.wait_ge(bn_scale, 1)
            for f in range(FOLDS):
                for k in range(KD):
                    act.activation(xT[:, k, f * FOLD * P:(f + 1) * FOLD * P], xT[:, k, f * FOLD * P:(f + 1) * FOLD * P], ACT.Identity,
                                   bias=csc[:, 2, k:k + 1], scale=csc[:, 1, k:k + 1]).then_inc(bn_applied, 1)
            ln_sqrt(3)
            turn_copies(2)
            act.wait_ge(mix_shift, 1)
            act.activation(sm8[:, 1, :, :], sm8[:, 0, :, :], ACT.Exp).then_inc(mix_exp, 1)
            for t in range(TILES):
                act.wait_ge(mix_turned, t + 1)
                act.activation(mixT[:, t * P:(t + 1) * P], bank[2 + t % 2][0:EXPERTS, 0:P], ACT.Copy).then_inc(mixT_ready, 1)
            act.wait_ge(aff_ready, 1)

            def dense_act(e, s, layer):
                at, n = STEPS[s]
                m = n * P
                mm, done, used = ((d1_mm, d1_act, d2_mm), (d2_mm, d2_act, d3_mm))[layer]
                g = e * (NS * KD) + s * KD
                dst = (h1, h2)[layer][s % 2]
                for o in range(KD):
                    if s >= 2:
                        back = [(used, (g - KD) if layer == 0 else e * D3 + STEPS[s - 2][0] + STEPS[s - 2][1])]
                    elif not isinstance(e, int) or e:
                        back = [(used, e * (NS * KD) if layer == 0 else e * D3)]
                    else:
                        back = []
                    waits(act, act_passed, (mm, g + o + 1), *back)
                    act.activation(dst[:, o, 0:m], bank[2 * layer + o][:, 0:m], ACT.Relu,
                                   bias=shf[:, layer, bass.ds(e * KD + o, 1)], scale=scl[:, layer, bass.ds(e * KD + o, 1)]).then_inc(done, 1)

            def dense_expert(e):
                for s in range(NS + 1):
                    if s < NS:
                        dense_act(e, s, 0)
                    if s >= 1:
                        dense_act(e, s - 1, 1)

            for e in range(2):
                dense_expert(e)
            with act.Fori(1, EXPERTS // 2) as i:
                for b in range(2):
                    dense_expert(i * 2 + b)

        @block.vector
        def _(dve):
            chain = Tally(dve_chain)

            def step(ins):
                dve.wait_ge(chain.sem, chain.inc(ins))

            def layer_norm(k, ready):
                for t in range(TILES):
                    ready(t)
                    ins = dve.bn_stats(stats[:, t, :], x[:, t, :])
                step(ins)
                for t in range(TILES):
                    ins = dve.bn_aggr(mv[:, t, :], stats[:, t, :])
                ins.then_inc(ln_var[k], 1)
                dve.wait_ge(ln_std[k], 1)
                step(dve.reciprocal(rstd[:], rstd[:]))
                for t in range(TILES):
                    dve.tensor_scalar(xn[:, t, :], x[:, t, :], mv[:, t, 0:1], rstd[:, t:t + 1], ALU.subtract, ALU.mult).then_inc(ln_tile[k], 1)

            dve.wait_ge(vec_in, 32)
            dve.wait_ge(gnn_w_in, 16)
            for j, name in enumerate(("attn_l", "attn_r")):
                w4 = waug[:, :, 0:D].rearrange("p k (h d) -> p k h d", d=HEAD_D)
                a4 = row[name].rearrange("p (h d) -> p h d", d=HEAD_D)
                for k in range(KD):
                    ins = dve.tensor_tensor(wprod[:, k * HEADS:(k + 1) * HEADS, :], w4[:, k], a4, ALU.mult)
                step(ins)
                for k in range(KD):
                    ins = dve.tensor_reduce(waug[:, k, D + j * HEADS:D + (j + 1) * HEADS], wprod[:, k * HEADS:(k + 1) * HEADS, :], AX_X, ALU.add)
                step(ins)
            dve.wait_ge(x_in, 16)
            dve.engine_nop().then_inc(waug_ready, 1)
            layer_norm(0, lambda t: None)

            dve.wait_ge(aff_std, 2)
            step(dve.reciprocal(scl[:].rearrange("p a b -> p (a b)"), scl[:].rearrange("p a b -> p (a b)")))

            def pair(name):
                return chan[:, PAIR_AT[name]:PAIR_AT[name] + EXPERTS * KD]

            for j in range(2):
                ins = dve.tensor_tensor(scl[:, j, :], scl[:, j, :], pair(f"g{j + 1}"), ALU.mult)
                dve.tensor_tensor(shf[:, j, :], pair(f"b{j + 1}"), pair(f"m{j + 1}"), ALU.subtract)
                step(dve.engine_nop())
            for j in range(2):
                ins = dve.tensor_tensor(shf[:, j, :], shf[:, j, :], scl[:, j, :], ALU.mult)
            step(ins)
            for j in range(2):
                ins = dve.tensor_tensor(shf[:, j, :], shf[:, j, :], pair(f"be{j + 1}"), ALU.add)
            ins.then_inc(aff_ready, 1)

            for t in range(TILES):
                dve.wait_ge(tab_mm, t + 1)
                dve.tensor_copy(tab[:, t, :], bank[2 + t % 2][0:P, 0:TAB]).then_inc(tab_copied, 1)

            dve.wait_ge(tab_gathered, 16 * 2 * TILES)
            s4, e4 = sm8[:, 0, :, 0:HEADS], sm8[:, 1, :, 0:HEADS]
            step(dve.tensor_tensor(s4, tsrc, tdst[:, :, D + HEADS:TAB], ALU.add))
            step(dve.tensor_scalar(e4, s4, LEAK, None, ALU.mult))
            step(dve.tensor_tensor(s4, s4, e4, ALU.max))
            step(dve.tensor_reduce(sm1[:, 0, :], s4, AX_X, ALU.max))
            dve.tensor_tensor(s4, s4, sm1[:, 0, :].rearrange("p (t o) -> p t o", o=1).to_broadcast([P, TILES, HEADS]), ALU.subtract).then_inc(att_shift, 1)
            dve.wait_ge(att_exp, 1)
            step(dve.tensor_reduce(sm1[:, 1, :], e4, AX_X, ALU.add))
            step(dve.reciprocal(sm1[:, 1, :], sm1[:, 1, :]))
            step(dve.tensor_tensor(e4, e4, sm1[:, 1, :].rearrange("p (t o) -> p t o", o=1).to_broadcast([P, TILES, HEADS]), ALU.mult))
            for h in range(HEADS):
                hd = tdst[:, :, h * HEAD_D:(h + 1) * HEAD_D]
                ins = dve.tensor_tensor(hd, hd, sm8[:, 1, :, h:h + 1].to_broadcast([P, TILES, HEAD_D]), ALU.mult)
            step(ins)
            for h in (2, 3):
                ins = dve.tensor_tensor(tdst[:, :, (h - 2) * HEAD_D:(h - 1) * HEAD_D], tdst[:, :, (h - 2) * HEAD_D:(h - 1) * HEAD_D],
                                        tdst[:, :, h * HEAD_D:(h + 1) * HEAD_D], ALU.add)
            step(ins)
            step(dve.tensor_tensor(tdst[:, :, 0:HEAD_D], tdst[:, :, 0:HEAD_D], tdst[:, :, HEAD_D:2 * HEAD_D], ALU.add))
            for h in range(HEADS):
                xh = x[:, :, h * HEAD_D:(h + 1) * HEAD_D]
                ins = dve.tensor_tensor(xh, xh, tdst[:, :, 0:HEAD_D], ALU.add)
            step(ins)

            layer_norm(1, lambda t: None)

            def bc(v, n):
                return v.rearrange("p (t o) -> p t o", o=1).to_broadcast([P, TILES, n])

            def rowbc(v):
                return v.rearrange("p (o e) -> p o e", o=1).to_broadcast([P, TILES, EXPERTS])

            dve.wait_ge(consts_ready, 7)
            dve.wait_ge(gate_mm, TILES)
            lg, sh, ex, oh, cum, tmp = [sm8[:, j] for j in range(6)]
            g8 = bank[4][0:P, 0:TILES * EXPERTS].rearrange("p (t e) -> p t e", e=EXPERTS)
            step(dve.tensor_tensor(lg, g8, rowbc(row["gate_b"][0:P]), ALU.add))
            step(dve.tensor_reduce(sm1[:, 0, :], lg, AX_X, ALU.max))
            dve.tensor_tensor(sh, lg, bc(sm1[:, 0, :], EXPERTS), ALU.subtract).then_inc(gate_shift, 1)
            step(dve.tensor_tensor(oh, lg, bc(sm1[:, 0, :], EXPERTS), ALU.is_equal))
            step(dve.tensor_tensor(tmp, oh, rowbc(rev[:]), ALU.mult))
            step(dve.tensor_reduce(sm1[:, 1, :], tmp, AX_X, ALU.max))
            step(dve.tensor_tensor(oh, tmp, bc(sm1[:, 1, :], EXPERTS), ALU.is_equal))
            ins = dve.tensor_reduce(tot8[:], oh.rearrange("p t e -> p e t"), AX_X, ALU.add)
            ins.then_inc(count_ready, 1)
            for e in range(EXPERTS):
                ins = dve.tensor_tensor_scan(cum[:, :, e], ones[0:P, 0:TILES], oh[:, :, e], 0.0, ALU.mult, ALU.add)
            step(ins)
            dve.wait_ge(count_mm, 1)
            step(dve.tensor_scalar(off8[:], bank[5][0:P, 0:EXPERTS], -1.0, None, ALU.add))
            step(dve.tensor_tensor(cum, cum, rowbc(off8[:]), ALU.add))
            step(dve.tensor_tensor(cum, cum, oh, ALU.mult))
            step(dve.tensor_reduce(sm1[:, 2, :], cum, AX_X, ALU.add))
            step(dve.tensor_tensor(tmp, oh, rowbc(eno[:]), ALU.mult))
            step(dve.tensor_reduce(sm1[:, 3, :], tmp, AX_X, ALU.add))
            pos, idx, kept, slot, drop = [sm1[:, j, :] for j in (2, 3, 4, 5, 6)]
            step(dve.tensor_scalar(kept, pos, float(CAP), None, ALU.is_lt))
            step(dve.scalar_tensor_tensor(slot, idx, float(SLOTS), pos, ALU.mult, ALU.add))
            step(dve.tensor_scalar(drop, kept, -float(DROPPED), float(DROPPED), ALU.mult, ALU.add))
            step(dve.tensor_tensor(slot, slot, drop, ALU.add))
            dve.tensor_copy(slot_i[:], slot).then_inc(slots_ready, 1)
            step(dve.tensor_scalar(pos, pos, float(CAP - 1), None, ALU.min))
            step(dve.scalar_tensor_tensor(pos, idx, float(CAP), pos, ALU.mult, ALU.add))
            dve.tensor_copy(row_i[:], pos).then_inc(slots_ready, 1)
            dve.wait_ge(gate_exp, 1)
            step(dve.tensor_reduce(sm1[:, 7, :], ex, AX_X, ALU.add))
            step(dve.reciprocal(sm1[:, 7, :], sm1[:, 7, :]))
            step(dve.tensor_tensor(sm1[:, 8, :], sm1[:, 7, :], kept, ALU.mult))

            def expert(e, b, n):
                for j in range(ROW_TILES):
                    m = HALF if j < ROW_TILES - 1 else LAST_ROWS
                    dve.wait_ge(ff2_mm, e * ROW_TILES + j + 1)
                    if not isinstance(n, int):
                        dve.wait_ge(y_stored[b], n * 32)
                    dve.tensor_tensor(yrow[b][0:m, j, :], bank[6 + j % 2][0:m, 0:D], rows[0:m, bass.ds(e * D + ROW_AT["b2"], D)], ALU.add).then_inc(ff2_bias, 1)

            for e in range(2):
                expert(e, e, 0)
            with dve.Fori(1, EXPERTS // 2) as i:
                for b in range(2):
                    expert(i * 2 + b, b, i)

            for f in range(FOLDS):
                dve.wait_ge(y_gathered, 16 * TILES)
                y = yg[:, f * FOLD:(f + 1) * FOLD, :]
                a, z = ytmp
                g5 = sm1[:, 8, f * FOLD:(f + 1) * FOLD].rearrange("p (t o) -> p t o", o=1).to_broadcast([P, FOLD, D])
                step(dve.tensor_tensor(y, y, g5, ALU.mult))
                step(dve.tensor_scalar(a, y, -FLT_MAX, FLT_MAX, ALU.max, ALU.min))
                step(dve.tensor_tensor(z, a, y, ALU.is_equal))
                step(dve.tensor_tensor(a, a, z, ALU.mult))
                step(dve.tensor_scalar(z, y, FLT_MAX, None, ALU.is_gt))
                step(dve.scalar_tensor_tensor(z, y, -FLT_MAX, z, ALU.is_lt, ALU.subtract))
                step(dve.scalar_tensor_tensor(a, z, -BIG, a, ALU.mult, ALU.add))
                xf = x[:, f * FOLD:(f + 1) * FOLD, :]
                ins = dve.tensor_tensor(xf, xf, a, ALU.add)
                ins.then_inc(x2_ready, 1)
            dve.wait_ge(x2_ready, FOLDS)
            layer_norm(2, lambda t: None)
            dve.wait_ge(ln_tile[2], TILES)
            for t in range(TILES):
                ins = dve.tensor_tensor(x[:, t, :], x[:, t, :], xn[:, t, :], ALU.add)
            step(ins)

            edge = [0]

            def edge_chunk(c, b, n):
                warm = not isinstance(c, int) or c >= 2
                scol = src_col[:, bass.ds(c * GROUP, GROUP)]
                dve.wait_ge(srow_in[b], n * 16)
                if warm:
                    dve.wait_ge(sum_mm, (c - 1) * GROUP)
                dve.tensor_tensor(same[b], srow[b], scol.rearrange("p (g o) -> p g o", o=1).to_broadcast([P, GROUP, P]), ALU.is_equal).then_inc(same_ready, 1)
                dve.wait_ge(same_ready, c + 1)
                k = c * 6
                dve.tensor_tensor(earlier, same[b], before[:].rearrange("p (o e) -> p o e", o=1).to_broadcast([P, GROUP, P]), ALU.mult).then_inc(edge_chain, 1)
                dve.wait_ge(edge_chain, k + 1)
                dve.tensor_reduce(dup[:, 0, :], earlier, AX_X, ALU.add).then_inc(edge_chain, 1)
                dve.tensor_copy(srcf[:], scol).then_inc(edge_chain, 1)
                dve.wait_ge(edge_chain, k + 3)
                dve.tensor_scalar(dup[:, 1, :], srcf[:], -1.0, trash[:, 0:1], ALU.mult, ALU.add).then_inc(edge_chain, 1)
                dve.wait_ge(edge_chain, k + 4)
                dve.scalar_tensor_tensor(dup[:, 2, :], dup[:, 0, :], 0.5, dup[:, 1, :], ALU.is_gt, ALU.mult).then_inc(edge_chain, 1)
                dve.wait_ge(edge_chain, k + 5)
                dve.tensor_tensor(dup[:, 1, :], dup[:, 2, :], srcf[:], ALU.add).then_inc(edge_chain, 1)
                dve.wait_ge(edge_chain, k + 6)
                if warm:
                    for t in range(GROUP):
                        dve.wait_ge(added[t], (c - 1) * 16)
                dve.tensor_copy(sidx[b][:], dup[:, 1, :]).then_inc(sidx_ready, 1)
                for t in range(GROUP):
                    g = c * GROUP + t
                    q = (b + t) % 2
                    dve.wait_ge(e2_mm, g + 1)
                    dve.tensor_tensor(filt[q], bank[4 + q][0:P, 0:D], row["bf2"][0:P], ALU.add).then_inc(filt_ready, 1)
                    dve.wait_ge(filt_ready, g + 1)
                    dve.wait_ge(xg_in[b][t], n * 16)
                    if not isinstance(c, int) or g >= 2:
                        dve.wait_ge(sum_mm, g - 1)
                    dve.tensor_tensor(msg[q], filt[q], xg[b][:, t, :], ALU.mult).then_inc(msg_ready, 1)

            for c in range(2):
                edge_chunk(c, c, 1)
            with dve.Fori(1, CHUNKS // 2) as i:
                for b in range(2):
                    edge_chunk(i * 2 + b, b, i + 1)
            edge_chunk(CHUNKS - 1, 0, CHUNKS // 2 + 1)

            def stats_of(f):
                for a, (lo, hi) in enumerate(PIECES):
                    for o in range(KD):
                        dve.wait_ge(h_ready, f * 4 + a * 2 + o + 1)
                        ins = dve.bn_stats(cstat[:, o, 2 * f + a, :], xT[:, o, f * FOLD * P + lo:f * FOLD * P + hi])
                return ins

            for f in range(FOLDS):
                dve.wait_ge(part_in[f % 2], (f // 2 + 1) * GROUP * 16)
                p = part[f % 2]
                dve.tensor_tensor(p[1], p[1], p[2], ALU.add)
                step(dve.tensor_tensor(p[0], p[0], p[3], ALU.add))
                step(dve.tensor_tensor(p[1], p[1], p[4], ALU.add))
                dve.tensor_tensor(p[0], p[0], p[1], ALU.add).then_inc(agg_ready, 1)
                if f >= 2:
                    stats_of(f - 2)
            stats_of(FOLDS - 2)
            step(stats_of(FOLDS - 1))
            for k in range(KD):
                ins = dve.bn_aggr(cmv[:, k, :], cstat[:, k].rearrange("p a b -> p (a b)"))
            ins.then_inc(bn_var, 1)
            dve.wait_ge(bn_std, 1)
            step(dve.reciprocal(csc[:, 0, :], csc[:, 0, :]))
            step(dve.tensor_tensor(csc[:, 1, :], csc[:, 0, :], chan[:, CH_AT["gamma"]:CH_AT["gamma"] + KD], ALU.mult))
            step(dve.tensor_tensor(csc[:, 0, :], csc[:, 1, :], cmv[:, :, 0], ALU.mult))
            dve.tensor_tensor(csc[:, 2, :], chan[:, CH_AT["beta"]:CH_AT["beta"] + KD], csc[:, 0, :], ALU.subtract).then_inc(bn_scale, 1)
            for t in range(TILES):
                dve.wait_ge(bn_turned, t + 1)
                dve.tensor_tensor(x[:, t, :], x[:, t, :], bank[6 + t % 2][0:P, 0:D], ALU.add).then_inc(x3_ready, 1)

            layer_norm(3, lambda t: dve.wait_ge(x3_ready, t + 1))
            dve.wait_ge(mix_mm, TILES)
            lg, ex = sm8[:, 0], sm8[:, 1]
            step(dve.tensor_tensor(lg, g8, rowbc(row["br"][0:P]), ALU.add))
            step(dve.tensor_reduce(sm1[:, 0, :], lg, AX_X, ALU.max))
            dve.tensor_tensor(lg, lg, bc(sm1[:, 0, :], EXPERTS), ALU.subtract).then_inc(mix_shift, 1)
            dve.wait_ge(mix_exp, 1)
            step(dve.tensor_reduce(sm1[:, 1, :], ex, AX_X, ALU.add))
            step(dve.reciprocal(sm1[:, 1, :], sm1[:, 1, :]))
            dve.tensor_tensor(mix[:], ex, bc(sm1[:, 1, :], EXPERTS), ALU.mult).then_inc(mix_ready, 1)
            for t in range(TILES):
                dve.wait_ge(bo_mm, t + 1)
                dve.tensor_tensor(x[:, t, :], x[:, t, :], bank[6 + t % 2][0:P, 0:D], ALU.add).then_inc(bo_added, 1)
            dve.wait_ge(mix_ready, 1)
            dve.wait_ge(bo_added, TILES)

            def dense_expert(e, b):
                for t in range(TILES):
                    dve.wait_ge(d3_mm, e * D3 + t + 1)
                    if not isinstance(e, int) or e:
                        dve.wait_ge(d3_added, (e - 1) * D3 + t + 1)
                    dve.scalar_tensor_tensor(x[:, t, :], bank[4 + (b + t) % 2][0:P, 0:D], mix[:, t, bass.ds(e, 1)], x[:, t, :],
                                             ALU.mult, ALU.add).then_inc(d3_added, 1)

            for e in range(2):
                dense_expert(e, e)
            with dve.Fori(1, EXPERTS // 2) as i:
                for b in range(2):
                    dense_expert(i * 2 + b, b)



_L0 = "L0_gnn_", "L0_ffn_"
_L1 = "L1_gnn_", "L1_ffn_"


def _arrange(inputs):
    def get(name):
        return np.asarray(inputs[name])

    def halves(name):
        return get(name).reshape(KD, HALF).T

    def pairs(name):
        return get("L1_ffn_" + name).reshape(EXPERTS, KD, HALF).transpose(2, 0, 1).reshape(HALF, EXPERTS * KD)

    chan = [halves("L1_gnn_" + n) for n in CHAN] + [pairs(n) for n in PAIR]
    chan.append(get("L0_ffn_b1").reshape(EXPERTS, FC, HALF).transpose(2, 0, 1).reshape(HALF, EXPERTS * FC))
    rows = [get("L0_gnn_attn_l"), get("L0_gnn_attn_r"), get("L1_gnn_bf2"), get("L0_ffn_b2"), get("L0_ffn_gate_b"), get("L1_ffn_br")]
    arrays = {
        "x": get("x"), "src": get("src"), "dst": get("dst"),
        "src_col": get("src").reshape(E_TILES, P).T, "dst_col": get("dst").reshape(E_TILES, P).T,
        "rbf_t": get("edge_attr_20").T,
        "chan": np.concatenate(chan, axis=1), "rows": np.concatenate([r.reshape(-1) for r in rows]),
        "gnn_w": get("L0_gnn_weight"), "gate_w": get("L0_ffn_gate_w"), "w1": get("L0_ffn_w1"), "w2": get("L0_ffn_w2"),
        "wf1": get("L1_gnn_Wf1"), "wf2": get("L1_gnn_Wf2"), "wu1": get("L1_gnn_Wu1"), "wu2": get("L1_gnn_Wu2"),
        "wr": get("L1_ffn_Wr"), "dw1": get("L1_ffn_W1"), "dw2": get("L1_ffn_W2"), "dwo": get("L1_ffn_Wo"),
        "bo": get("L1_ffn_bo"),
    }
    return {f"in_{k}": np.ascontiguousarray(v) for k, v in arrays.items()}


def kernel(**inputs):
    import concourse.bacc as bacc
    from concourse.bass_utils import run_bass_kernel_spmd

    nc = bacc.Bacc("TRN2", target_bir_lowering=False, num_devices=1)
    arrays = _arrange(inputs)
    A = {k[3:]: nc.dram_tensor(k, v.shape, mybir.dt.from_np(v.dtype), kind="ExternalInput").ap() for k, v in arrays.items()}
    out = nc.dram_tensor("out_0", (N_NODES, D), F32, kind="ExternalOutput").ap()
    build(nc, A, out)
    r = run_bass_kernel_spmd(nc, [arrays], core_ids=[0])
    return r.results[0]["out_0"]
```

```python
from contextlib import ExitStack

import numpy as np

import concourse.bass as bass
from concourse import mybir

F32 = mybir.dt.float32
I32 = mybir.dt.int32
F32R = mybir.dt.float32r
ALU = mybir.AluOpType
ACT = mybir.ActivationFunctionType
AX_X = mybir.AxisListType.X

N_NODES, D = 3125, 256
P = 125
TILES = N_NODES // P
HALF = 128
KD = D // HALF
LN_EPS = 1e-5

HEADS, HEAD_D = 4, 64
TAB = D + 2 * HEADS
LEAK = 0.01

EXPERTS = 8
FF = 1024
FC = FF // HALF
CAP = 489
SLOTS = 512
CAP_EVEN = CAP + CAP % 2
ROW_TILES = SLOTS // HALF
LAST_ROWS = CAP - (ROW_TILES - 1) * HALF
DROPPED = 2 * EXPERTS * SLOTS
ROW = D + 1
ZERO_ROW = EXPERTS * CAP
ZROWS = 4
FLT_MAX = 3.4028234663852886e38
BIG = 10000.0

N_EDGES = 53125
N_RBF = 20
E_TILES = N_EDGES // P
GROUP = 5
CHUNKS = E_TILES // GROUP
CE = GROUP * P
CUT = 3 * P
PIECES = ((0, CUT), (CUT, CE))
AGG_ROWS = N_NODES + P
BN_EPS = 1e-5
STACK = 32
KS = 2 * STACK + N_RBF
THIRDS = [(a, min(2, GROUP - a)) for a in range(0, GROUP, 2)]
NT = len(THIRDS)
FOLD = 5
FOLDS = TILES // FOLD

BN2_EPS = 1e-3
TOK = 4
STEPS = [(s, min(TOK, TILES - s)) for s in range(0, TILES, TOK)]

CHAN = ["bf1", "bu1", "bu2", "gamma", "beta"]
PAIR = ["b1", "g1", "be1", "m1", "v1", "b2", "g2", "be2", "m2", "v2"]
CH_AT = {n: KD * k for k, n in enumerate(CHAN)}
PAIR_AT = {n: KD * len(CHAN) + k * EXPERTS * KD for k, n in enumerate(PAIR)}
FFB1_AT = KD * len(CHAN) + len(PAIR) * EXPERTS * KD
N_CHAN = FFB1_AT + EXPERTS * FC
ROW_AT = {"attn_l": 0, "attn_r": D, "bf2": 2 * D, "gate_b": 3 * D, "br": 3 * D + EXPERTS}
N_ROW = 3 * D + 2 * EXPERTS
PASSES = ((0, 0), (0, 1), (1, 0))


class Tally:

    def __init__(self, sem):
        self.sem, self.n = sem, 0

    def inc(self, instruction, by=1):
        self.n += by
        instruction.then_inc(self.sem, by)
        return self.n


def build(nc, A, out):
    with ExitStack() as ctx:
        def sb(name, shape, dt=F32):
            return ctx.enter_context(nc.sbuf_tensor(name, shape, dt))

        def sem(name):
            return ctx.enter_context(nc.semaphore(name))

        def dram(name, shape):
            return nc.dram_tensor(name, shape, F32).ap()

        psum = ctx.enter_context(nc.psum_tensor("psum", [128, 8, 512], F32))
        bank = [psum[:, i, :] for i in range(8)]

        tab_d = dram("tab_d", [N_NODES, TAB])
        al_d = dram("al_d", [N_NODES, HEADS])
        buf_d = dram("buf_d", [EXPERTS * SLOTS, ROW])
        ybuf_d = dram("ybuf_d", [ZERO_ROW + 1, D])
        xn_d = dram("xn_d", [N_NODES, D])
        agg_d = [dram(f"agg{i}_d", [AGG_ROWS, D]) for i in range(GROUP)]

        x = sb("x_sb", [P, TILES, D])
        chan = sb("chan_sb", [HALF, N_CHAN])
        rows = sb("rows_sb", [HALF, N_ROW])
        ident = sb("ident", [128, 128])
        ones = sb("ones", [128, 128])
        before = sb("before", [P, P])
        upper = sb("upper", [P, P])
        trash = sb("trash", [P, 1])
        rev = sb("rev", [P, EXPERTS])
        eno = sb("eno", [P, EXPERTS])
        stats = sb("stats", [P, TILES, 6])
        mv = sb("mv", [P, TILES, 2])
        rstd = sb("rstd", [P, TILES])
        eps1 = sb("eps1", [128, 3])
        sm8 = sb("sm8", [P, 6, TILES, EXPERTS])
        sm1 = sb("sm1", [P, 10, TILES])
        tot8 = sb("tot8", [P, EXPERTS])
        off8 = sb("off8", [P, EXPERTS])
        slot_i = sb("slot_i", [P, TILES], I32)
        row_i = sb("row_i", [P, TILES], I32)
        e0src = sb("e0src", [P, TILES], I32)
        e0dst = sb("e0dst", [P, TILES], I32)
        wf1 = sb("wf1", [N_RBF, D])
        wf2 = sb("wf2", [HALF, KD, D])
        wu1 = sb("wu1", [HALF, KD, D])
        wu2 = sb("wu2", [HALF, KD, D])
        waug = sb("waug", [HALF, KD, TAB])
        wprod = sb("wprod", [HALF, KD * HEADS, HEAD_D])
        gate_w = sb("gate_w_sb", [HALF, KD, EXPERTS])
        wr = sb("wr_sb", [HALF, KD, EXPERTS])
        bo = sb("bo_sb", [EXPERTS, D])
        mix = sb("mix", [P, TILES, EXPERTS])
        scl = sb("scl", [HALF, 2, EXPERTS * KD])
        shf = sb("shf", [HALF, 2, EXPERTS * KD])
        cstat = sb("cstat", [HALF, KD, 2 * FOLDS, 6])
        cmv = sb("cmv", [HALF, KD, 2])
        csc = sb("csc", [HALF, 3, KD])

        dup = sb("dup", [P, 2, GROUP])
        wcol = sb("wcol", [128, 1])
        flag = sb("flag", [1, 1], I32)
        flag_f = sb("flag_f", [1, 1])
        sidx = [sb(f"sidx{b}", [P, GROUP], I32) for b in range(2)]
        gidx = [sb(f"gidx{b}", [P, GROUP], I32) for b in range(2)]
        wrs = sb("wrs", [HALF, 2, KD * EXPERTS], F32R)

        base = -(-nc.sbuf_base // 32) * 32

        def place(name, at, shape, dt=F32):
            return nc.alloc_sbuf_tensor_at(name, shape, dt, offset=base + 4 * at)

        xn = place("xn", 0, [P, TILES, ROW])
        xT = place("xT", 6432, [HALF, KD, N_NODES])
        tab = place("tab", 12688, [P, TILES, TAB])
        tdst = place("tdst", 19288, [P, TILES, TAB])
        tsrc = place("tsrc", 25888, [P, TILES, HEADS])
        zeros = place("zeros", 38304, [128, ZROWS * ROW])
        b2 = place("b2_rows", 6432, [128, EXPERTS * D])
        yrow = [place(f"yrow{b}", 8480 + b * 1024, [128, ROW_TILES, D]) for b in range(2)]
        ytmp = [[place(f"ytmp{a}{b}", 10528 + (a * 2 + b) * D, [128, D]) for b in range(2)] for a in range(3)]
        hid = [place(f"hid{h}", 12688 + h * 4096, [128, FC, SLOTS], F32R) for h in range(2)]
        act_full = [place(f"act_full{b}", 20880 + b * SLOTS, [128, SLOTS]) for b in range(2)]
        bT = [place(f"bT{h}", 21904 + h * 1024, [128, KD, SLOTS], F32R) for h in range(2)]
        brow = [place(f"brow{b}", 23952 + b * 1032, [128, ROW_TILES, ROW]) for b in range(2)]
        w1 = [place(f"w1_{h}", 26016 + h * 2048, [128, KD, FF], F32R) for h in range(2)]
        w2 = [place(f"w2_{h}", 30112 + h * 2048, [128, FC, D], F32R) for h in range(2)]
        w1_full = place("w1_full", 34208, [128, KD, FF])
        w2_full = place("w2_full", 36256, [128, FC, D])
        yg = place("yg", 12688, [P, TILES, D])
        E0 = 12688
        CW = 632
        srow = [place(f"srow{b}", E0 + b * CW, [P, GROUP, P], I32) for b in range(2)]
        attr = [place(f"attr{b}", E0 + 2 * CW + b * CW, [N_RBF, CE]) for b in range(2)]
        same = [place(f"same{b}", E0 + 4 * CW + b * CW, [P, GROUP, P]) for b in range(2)]
        earlier = place("earlier", E0 + 6 * CW, [P, GROUP, P])
        eh = [place(f"eh{b}", E0 + 7 * CW + b * KD * CW, [128, KD, CE]) for b in range(2)]
        xg = [place(f"xg{b}", E0 + 11 * CW + b * GROUP * D, [P, GROUP, D]) for b in range(2)]
        filt = [place(f"filt{b}", E0 + 11 * CW + 2 * GROUP * D + b * D, [P, D]) for b in range(2)]
        msg = [place(f"msg{b}", E0 + 11 * CW + 2 * (GROUP + 1) * D + b * D, [P, D]) for b in range(2)]
        summed = [place(f"summed{b}", E0 + 11 * CW + 2 * (GROUP + 2) * D + b * GROUP * D, [P, GROUP, D]) for b in range(2)]
        src_col = place("src_col_sb", 34208, [P, E_TILES], I32)
        dst_col = place("dst_col_sb", 34640, [P, E_TILES], I32)
        src_f = place("src_f", 30848, [P, E_TILES])
        to_trash = place("to_trash", 31280, [P, E_TILES])
        dst_f = place("dst_f", 19096, [P, E_TILES])
        ends = place("ends", 19528, [P, 2, CHUNKS])
        span = place("span", 19704, [CHUNKS, 4])
        window_f = place("window_f", 19712, [1, 2 * CHUNKS])
        window = place("window", 31712, [1, CHUNKS], I32)
        wstart = place("wstart", 31800, [128, CHUNKS])
        w3 = place("w3", 31888, [KS, D])
        w3s = place("w3s", 32144, [KS, D], F32R)
        b3 = place("b3", 32400, [STACK + 1, D])
        b3s = place("b3s", 32656, [STACK + 1, D], F32R)
        wf2s = place("wf2s", 32912, [HALF, 2, KD, D], F32R)
        one_row = place("one_row", 33936, [STACK + 1, 128], F32R)
        eh_full = place("eh_full", E0 + 7 * CW, [128, KD, CE])
        eh2 = [[place(f"eh2_{b}{h}", 6432 + (2 * b + h) * KD * CW, [128, KD, CE], F32R) for h in range(2)] for b in range(2)]
        xw = [place(f"xw{b}", E0 + 11 * CW + b * D, [HALF, D]) for b in range(2)]
        xws = [place(f"xws{b}", E0 + 11 * CW + 2 * D + b * 2 * D, [HALF, 2, D], F32R) for b in range(2)]
        msgs = place("msgs", E0 + 11 * CW + 6 * D, [P, GROUP, D])
        ends_x = place("ends_x", 35080, [P, GROUP, D])
        drow = [place(f"drow{b}", 25792 + b * CW, [HALF, CE], I32) for b in range(2)]
        hot = [place(f"hot{b}", 25792 + (2 + b) * CW, [HALF, CE], F32R) for b in range(2)]
        att3 = [place(f"att3_{b}", 25792 + (4 + b) * CW, [KS, CE]) for b in range(2)]
        att3s = [place(f"att3s_{b}", 25792 + (6 + b) * CW, [KS, CE], F32R) for b in range(2)]
        part = [[place(f"part{b}_{i}", 12688 + (b * GROUP + i) * FOLD * D, [P, FOLD, D]) for i in range(GROUP)] for b in range(2)]
        aggT = [place(f"aggT{b}", 25488 + b * KD * CW, [128, KD, CE]) for b in range(2)]
        uT = [place(f"uT{b}", 28016 + b * KD * CW, [128, KD, CE]) for b in range(2)]
        mixT = place("mixT", 0, [EXPERTS, N_NODES])
        h1 = [[place(f"h1_{b}{h}", 6432 + (2 * b + h) * KD * TOK * P, [128, KD, TOK * P], F32R) for h in range(2)] for b in range(2)]
        h_full = [[place(f"h_full{j}{b}", 10432 + (2 * j + b) * 504, [128, TOK * P]) for b in range(2)] for j in range(2)]
        xTs = [place(f"xTs{h}", 12688 + h * 6256, [128, KD, N_NODES], F32R) for h in range(2)]
        h2 = [[place(f"h2_{b}{h}", 25200 + (2 * b + h) * KD * TOK * P, [128, KD, TOK * P], F32R) for h in range(2)] for b in range(2)]
        dw = [[place(f"dw{b}{h}", 30720 + (2 * b + h) * 3 * KD * D, [128, 3 * KD, D], F32R) for h in range(2)] for b in range(2)]
        dw_full = place("dw_full", 36864, [128, 3 * KD, D])

        row = {k: rows[:, v:v + (EXPERTS if k in ("gate_b", "br") else D)]
               for k, v in ROW_AT.items()}

        consts_ready = sem("consts_ready")
        x_in = [sem(f"x_in{f}") for f in range(FOLDS)]
        idx_in = sem("idx_in")
        vec_in = sem("vec_in")
        gnn_w_in = sem("gnn_w_in")
        small_w_in = sem("small_w_in")
        buf_zeroed = sem("buf_zeroed")
        agg_zeroed = sem("agg_zeroed")
        col_in = sem("col_in")
        node_w_in = sem("node_w_in")
        wr_halved = sem("wr_halved")
        dve_chain = sem("dve_chain")
        waug_ready = sem("waug_ready")
        ln_var = sem("ln_var")
        ln_std = sem("ln_std")
        ln_tile = sem("ln_tile")
        turned = sem("turned")
        turned_copied = sem("turned_copied")
        tab_mm = sem("tab_mm")
        tab_copied = sem("tab_copied")
        tab_stored = sem("tab_stored")
        att_in = [sem(f"att_in{f}") for f in range(FOLDS)]
        att_shift = sem("att_shift")
        att_exp = sem("att_exp")
        gate_mm = sem("gate_mm")
        gate_shift = sem("gate_shift")
        gate_exp = sem("gate_exp")
        count_ready = sem("count_ready")
        count_mm = sem("count_mm")
        slots_ready = sem("slots_ready")
        scattered = sem("scattered")
        brow_in = [sem(f"brow_in{b}") for b in range(2)]
        ffw_in = sem("ffw_in")
        w_halved = sem("w_halved")
        b2_in = sem("b2_in")
        b_turned = sem("b_turned")
        b_high = sem("b_high")
        b_low = sem("b_low")
        ff1_mm = sem("ff1_mm")
        ff1_act = sem("ff1_act")
        ff1_low = sem("ff1_low")
        ff2_mm = sem("ff2_mm")
        ff2_bias = sem("ff2_bias")
        y_stored = [sem(f"y_stored{b}") for b in range(2)]
        y_chain = sem("y_chain")
        y_ready = sem("y_ready")
        y_in = [sem(f"y_in{f}") for f in range(FOLDS)]
        xn_stored = sem("xn_stored")
        srow_in = [sem(f"srow_in{b}") for b in range(2)]
        attr_in = [sem(f"attr_in{b}") for b in range(2)]
        same_ready = sem("same_ready")
        sidx_ready = sem("sidx_ready")
        gidx_ready = sem("gidx_ready")
        e1_mm = sem("e1_mm")
        e1_silu = sem("e1_silu")
        e2_mm = sem("e2_mm")
        filt_ready = sem("filt_ready")
        msg_ready = sem("msg_ready")
        sum_mm = sem("sum_mm")
        sum_copied = sem("sum_copied")
        xg_in = [[sem(f"xg_in{b}_{t}") for t in range(GROUP)] for b in range(2)]
        added = [sem(f"added{t}") for t in range(GROUP)]
        edge_chain = sem("edge_chain")
        edge_set = sem("edge_set")
        edge_w_in = sem("edge_w_in")
        edge_w_ready = sem("edge_w_ready")
        stack_ready = sem("stack_ready")
        ends_ready = sem("ends_ready")
        ends_turned = sem("ends_turned")
        window_ready = sem("window_ready")
        window_turned = sem("window_turned")
        window_int = sem("window_int")
        window_spread = sem("window_spread")
        path_ready = sem("path_ready")
        att_high = sem("att_high")
        att_low = sem("att_low")
        xw_high = sem("xw_high")
        xw_low = sem("xw_low")
        hot_ready = sem("hot_ready")
        hid_mm = sem("hid_mm")
        hid_act = sem("hid_act")
        hid_low = sem("hid_low")
        pair_mm = sem("pair_mm")
        ends_copied = sem("ends_copied")
        part_in = [sem(f"part_in{b}") for b in range(2)]
        agg_ready = sem("agg_ready")
        agg_turned = sem("agg_turned")
        agg_copied = sem("agg_copied")
        u_mm = sem("u_mm")
        u_silu = sem("u_silu")
        h_mm = sem("h_mm")
        h_ready = sem("h_ready")
        bn_var = sem("bn_var")
        bn_std = sem("bn_std")
        bn_scale = sem("bn_scale")
        bn_applied = sem("bn_applied")
        bn_turned = sem("bn_turned")
        x3_ready = sem("x3_ready")
        x_low = sem("x_low")
        mix_mm = sem("mix_mm")
        mix_shift = sem("mix_shift")
        mix_exp = sem("mix_exp")
        mix_ready = sem("mix_ready")
        mix_turned = sem("mix_turned")
        mixT_ready = sem("mixT_ready")
        bo_mm = sem("bo_mm")
        bo_added = sem("bo_added")
        aff_std = sem("aff_std")
        aff_ready = sem("aff_ready")
        dw_in = sem("dw_in")
        dw_halved = sem("dw_halved")
        d1_mm = sem("d1_mm")
        d1_act = sem("d1_act")
        d1_low = sem("d1_low")
        d2_mm = sem("d2_mm")
        d2_act = sem("d2_act")
        d2_low = sem("d2_low")
        d3_mm = sem("d3_mm")
        d3_added = sem("d3_added")
        stored = sem("stored")
        sp_passed = sem("sp_passed")
        pool_passed = sem("pool_passed")
        act_passed = sem("act_passed")

        block = ctx.enter_context(nc.Block())

        def waits(eng, passed, *needs):
            for s, v in needs:
                eng.wait_ge(s, v)
            eng.sem_inc(passed, 1)

        def by_path(eng, windows, gathers):
            eng.wait_ge(path_ready, 1)
            all_in = eng.value_load(flag[0:1, 0:1], min_val=0, max_val=1)
            with eng.If(all_in == 1):
                windows()
            with eng.If(all_in == 0):
                gathers()

        def chunks(eng, chunk, ahead):
            chunk(0, 0, 1, 2)
            chunk(1, 1, 1, 2)
            pairs = (CHUNKS - ahead) // 2
            with eng.Fori(1, pairs) as i:
                for b in range(2):
                    chunk(i * 2 + b, b, i + 1, 2)
            for c in range(2 * pairs, CHUNKS):
                chunk(c, c % 2, c // 2 + 1, min(2, CHUNKS - 1 - c))

        def warm(c, n):
            return not isinstance(c, int) or c >= n

        def tiles_behind(c, b, t, n):
            if t >= n:
                return c, b, t - n
            return (c - 1, 1 - b, t - n + GROUP) if warm(c, 1) else None

        def next_n(b, n):
            return n + b

        NS = len(STEPS)
        N_ZERO = GROUP * -(-AGG_ROWS // (128 * ZROWS))

        def three_passes(pe, dst, lhs, rhs, first=True, last=True):
            n = len(lhs) * len(PASSES)
            at = 0
            for l, r in zip(lhs, rhs):
                for i, j in PASSES:
                    ins = pe.matmul(dst, l[i], r[j], start=first and at == 0, stop=last and at == n - 1)
                    at += 1
            return ins

        @block.sync
        def _(sp):
            xv = A["x"].rearrange("(p t) d -> p t d", t=TILES)
            for f in range(FOLDS):
                sp.dma_start(x[:, f * FOLD:(f + 1) * FOLD, :], xv[:, f * FOLD:(f + 1) * FOLD, :]).then_inc(x_in[f], 16)
                if f == 0:
                    sp.dma_start(rows[:], A["rows"].partition_broadcast(HALF)).then_inc(vec_in, 16)
                    sp.dma_start(waug[:, :, 0:D], A["gnn_w"].rearrange("(k p) d -> p k d", p=HALF)).then_inc(gnn_w_in, 16)
                    sp.dma_start(e0src[:], A["src"][0:N_NODES].rearrange("(p t) -> p t", t=TILES)).then_inc(idx_in, 16)
                    sp.dma_start(e0dst[:], A["dst"][0:N_NODES].rearrange("(p t) -> p t", t=TILES)).then_inc(idx_in, 16)
            sp.dma_start(chan[:], A["chan"]).then_inc(vec_in, 16)
            for w, name in ((gate_w, "gate_w"), (wr, "wr")):
                sp.dma_start(w[:], A[name].rearrange("(k p) e -> p k e", p=HALF)).then_inc(small_w_in, 16)

            def expert_loads(e, warm):
                if warm:
                    waits(sp, sp_passed, (w_halved, e * 4))
                sp.dma_start(w1_full[:], A["w1"][bass.ds(e, 1)].rearrange("o (k p) f -> p (o k) f", p=HALF)).then_inc(ffw_in, 16)
                sp.dma_start(w2_full[:], A["w2"][bass.ds(e, 1)].rearrange("o (k p) f -> p (o k) f", p=HALF)).then_inc(ffw_in, 16)

            expert_loads(0, False)

            sp.wait_ge(consts_ready, 1)
            step = 128 * ZROWS
            for q in range(0, EXPERTS * SLOTS, step):
                sp.dma_start(buf_d[q:q + step, :].rearrange("(p r) d -> p (r d)", p=128), zeros[:]).then_inc(buf_zeroed, 16)
            sp.dma_start(ybuf_d[ZERO_ROW:ZERO_ROW + 1, :], zeros[0:1, 0:D]).then_inc(buf_zeroed, 16)

            tv = tab_d.rearrange("(p t) c -> p t c", t=TILES)
            av = al_d.rearrange("(p t) c -> p t c", t=TILES)
            for f in range(FOLDS):
                fs = slice(f * FOLD, (f + 1) * FOLD)
                sp.wait_ge(tab_copied, (f + 1) * FOLD)
                sp.dma_start(tv[:, fs, :], tab[:, fs, :]).then_inc(tab_stored, 16)
                sp.dma_start(av[:, fs, :], tab[:, fs, D:D + HEADS]).then_inc(tab_stored, 16)

            for i in range(GROUP):
                for lo in range(0, AGG_ROWS, step):
                    n = min(step, AGG_ROWS - lo)
                    r = ZROWS if n == step else 2
                    sp.dma_start(agg_d[i][lo:lo + n, :].rearrange("(p r) d -> p (r d)", r=r), zeros[0:n // r, 0:r * D]).then_inc(agg_zeroed, 16)
            sp.dma_start(bo[:], A["bo"]).then_inc(node_w_in, 16)
            sp.dma_start(wf1[:], A["wf1"]).then_inc(node_w_in, 16)
            for w, name in ((wf2, "wf2"), (wu1, "wu1"), (wu2, "wu2")):
                sp.dma_start(w[:], A[name].rearrange("(k p) d -> p k d", p=HALF)).then_inc(node_w_in, 16)

            def expert_rows(e, b, warm):
                if warm:
                    waits(sp, sp_passed, (b_turned, (e - 1) * KD))
                    waits(sp, sp_passed, (ff2_bias, (e - 1) * ROW_TILES))
                sp.dma_start(brow[b][:], buf_d[bass.ds(e * SLOTS, SLOTS), :].rearrange("(j p) d -> p j d", p=128)).then_inc(brow_in[b], 16)

            def expert_store(e, b):
                waits(sp, sp_passed, (y_ready, (e + 1) * 2))
                full = (ROW_TILES - 1) * HALF
                sp.dma_start(ybuf_d[bass.ds(e * CAP, full), :].rearrange("(j p) d -> p j d", p=128),
                             yrow[b][:, 0:ROW_TILES - 1, :]).then_inc(y_stored[b], 16)
                sp.dma_start(ybuf_d[bass.ds(e * CAP + full, LAST_ROWS), :],
                             yrow[b][0:LAST_ROWS, ROW_TILES - 1, :]).then_inc(y_stored[b], 16)

            sp.wait_ge(gate_mm, TILES)
            sp.dma_start(b2[:], A["b2"].partition_broadcast(HALF)).then_inc(b2_in, 16)
            sp.wait_ge(scattered, 16 * TILES)
            for b in range(2):
                expert_rows(b, b, False)
            expert_loads(1, True)
            with sp.Fori(0, EXPERTS // 2 - 1) as i:
                for b in range(2):
                    expert_loads(i * 2 + 2 + b, True)
                    expert_store(i * 2 + b, b)
                    expert_rows(i * 2 + 2 + b, b, True)
            sp.wait_ge(w_halved, EXPERTS * 4)
            sp.dma_start(src_col[:], A["src_col"]).then_inc(col_in, 16)
            sp.dma_start(dst_col[:], A["dst_col"]).then_inc(col_in, 16)
            for b in range(2):
                expert_store(EXPERTS - 2 + b, b)

            nv = xn_d.rearrange("(p t) d -> p t d", t=TILES)
            for f in range(FOLDS):
                fs = slice(f * FOLD, (f + 1) * FOLD)
                sp.wait_ge(ln_tile, 2 * TILES + (f + 1) * FOLD)
                sp.dma_start(nv[:, fs, :], xn[:, fs, 0:D]).then_inc(xn_stored, 16)
                if f == 0:
                    sp.wait_ge(edge_set, 4)
                    for q in range(3):
                        sp.dma_start(w3[q * STACK:q * STACK + N_RBF, :], A["wf1"]).then_inc(edge_w_in, 16)
                    for q in range(2):
                        sp.dma_start(w3[q * STACK + N_RBF:q * STACK + N_RBF + 1, :], A["bf1"]).then_inc(edge_w_in, 16)
                        sp.dma_start(b3[q * STACK:q * STACK + 1, :], A["bf2"]).then_inc(edge_w_in, 16)

            def window_loads(c, b, n):
                at = c * CE
                if warm(c, 2):
                    waits(sp, sp_passed, (att_low, c - 1))
                for q in range(3):
                    sp.dma_start(att3[b][q * STACK:q * STACK + N_RBF, :], A["rbf_t"][:, bass.ds(at, CE)]).then_inc(attr_in[b], 16)
                start = sp.value_load(window[0:1, bass.ds(c, 1)], min_val=0, max_val=N_NODES - HALF)
                if warm(c, 2):
                    waits(sp, sp_passed, (same_ready, c - 1))
                    waits(sp, sp_passed, (hot_ready, c - 1))
                    waits(sp, sp_passed, (xw_low, c - 1))
                sp.dma_start(xw[b][:], xn_d[bass.ds(start, HALF), :]).then_inc(srow_in[b], 16)
                sp.dma_start(drow[b][:], A["dst"][bass.ds(at, CE)].partition_broadcast(HALF)).then_inc(srow_in[b], 16)
                sp.dma_start(srow[b][:].rearrange("p g e -> p (g e)"), A["src"][bass.ds(at, CE)].partition_broadcast(P)).then_inc(srow_in[b], 16)

            def windows():
                sp.wait_ge(xn_stored, 16 * FOLDS)
                chunks(sp, lambda c, b, n, left: window_loads(c, b, n), 1)

            def edge_loads(c, b, warm):
                if warm:
                    waits(sp, sp_passed, (same_ready, c - 1))
                    waits(sp, sp_passed, (e1_mm, 4 * (c - 1)))
                sp.dma_start(srow[b][:].rearrange("p g e -> p (g e)"),
                             A["src"][bass.ds(c * CE, CE)].partition_broadcast(P)).then_inc(srow_in[b], 16)
                sp.dma_start(attr[b][:], A["rbf_t"][:, bass.ds(c * CE, CE)]).then_inc(attr_in[b], 16)

            by_path(sp, windows, lambda: chunks(sp, lambda c, b, n, left: edge_loads(c, b, warm(c, 2)), 1))

            def dense_loads(e, warm):
                if warm:
                    waits(sp, sp_passed, (dw_halved, e * 2))
                for j, name in enumerate(("dw1", "dw2", "dwo")):
                    sp.dma_start(dw_full[:, j * KD:(j + 1) * KD, :],
                                 A[name][bass.ds(e, 1)].rearrange("o (k p) d -> p (o k) d", p=HALF)).then_inc(dw_in, 16)

            dense_loads(0, False)

            for i in range(GROUP):
                sp.wait_ge(added[i], 16 * CHUNKS)
            for f in range(FOLDS):
                if f >= 2:
                    sp.wait_ge(agg_turned, (f - 1) * FOLD)
                for i in range(GROUP):
                    src = agg_d[i][0:N_NODES, :].rearrange("(p t) d -> p t d", t=TILES)
                    sp.dma_start(part[f % 2][i][:], src[:, f * FOLD:(f + 1) * FOLD, :]).then_inc(part_in[f % 2], 16)

            with sp.Fori(1, EXPERTS) as e:
                dense_loads(e, True)

            ov = out.rearrange("(p t) d -> p t d", t=TILES)
            for f in range(FOLDS):
                fs = slice(f * FOLD, (f + 1) * FOLD)
                sp.wait_ge(d3_added, (EXPERTS - 1) * TILES + (f + 1) * FOLD)
                sp.dma_start(ov[:, fs, :], x[:, fs, :]).then_inc(stored, 16)
            sp.wait_ge(stored, 16 * FOLDS)

        @block.gpsimd
        def _(pool):
            made = Tally(sem("pool_made"))
            pool.memset(zeros[:], 0.0).then_inc(consts_ready, 1)
            made.inc(pool.memset(ident[:], 0.0))
            made.inc(pool.memset(ones[:], 1.0))
            made.inc(pool.memset(before[:], 1.0))
            made.inc(pool.memset(upper[:], 1.0))
            made.inc(pool.memset(eps1[:, 0:1], LN_EPS))
            made.inc(pool.memset(eps1[:, 1:2], BN2_EPS))
            made.inc(pool.memset(eps1[:, 2:3], 0.0))
            pool.wait_ge(made.sem, made.n)
            pool.affine_select(out=ident[:], in_=ident[:], compare_op=ALU.not_equal, fill=1.0, base=0,
                               pattern=[[-1, 128]], channel_multiplier=1).then_inc(consts_ready, 1)
            pool.affine_select(out=before[:], in_=before[:], compare_op=ALU.is_gt, fill=0.0, base=0,
                               pattern=[[-1, P]], channel_multiplier=1).then_inc(consts_ready, 1)
            pool.affine_select(out=upper[:], in_=upper[:], compare_op=ALU.is_gt, fill=0.0, base=0,
                               pattern=[[1, P]], channel_multiplier=-1).then_inc(consts_ready, 1)
            pool.iota(trash[:], pattern=[[0, 1]], base=N_NODES, channel_multiplier=1,
                      allow_small_or_imprecise_dtypes=True).then_inc(consts_ready, 1)
            pool.iota(wcol[:], pattern=[[0, 1]], base=0, channel_multiplier=1,
                      allow_small_or_imprecise_dtypes=True).then_inc(consts_ready, 1)
            pool.iota(rev[:], pattern=[[-1, EXPERTS]], base=EXPERTS, channel_multiplier=0,
                      allow_small_or_imprecise_dtypes=True).then_inc(consts_ready, 1)
            pool.iota(eno[:], pattern=[[1, EXPERTS]], base=0, channel_multiplier=0,
                      allow_small_or_imprecise_dtypes=True).then_inc(consts_ready, 1)

            def halve_weights(e, warm):
                waits(pool, pool_passed, (ffw_in, (e + 1) * 32), *([(ff1_mm, e * FC)] if warm else []))
                pool.tensor_copy(w1[0][:], w1_full[:]).then_inc(w_halved, 1)
                waits(pool, pool_passed, (w_halved, e * 4 + 1))
                pool.tensor_tensor(w1[1][:], w1_full[:], w1[0][:].bitcast(F32), ALU.subtract).then_inc(w_halved, 1)
                if warm:
                    waits(pool, pool_passed, (ff2_mm, e * ROW_TILES))
                pool.tensor_copy(w2[0][:], w2_full[:]).then_inc(w_halved, 1)
                waits(pool, pool_passed, (w_halved, e * 4 + 3))
                pool.tensor_tensor(w2[1][:], w2_full[:], w2[0][:].bitcast(F32), ALU.subtract).then_inc(w_halved, 1)

            halve_weights(0, False)

            pool.wait_ge(idx_in, 32)
            pool.wait_ge(tab_stored, 32 * FOLDS)
            for t in range(TILES):
                pool.indirect_dma_start(tdst[:, t, :], None, tab_d, bass.IndirectOffsetOnAxis(ap=e0dst[:, t:t + 1], axis=0)).then_inc(att_in[t // FOLD], 16)
                pool.indirect_dma_start(tsrc[:, t, :], None, al_d, bass.IndirectOffsetOnAxis(ap=e0src[:, t:t + 1], axis=0)).then_inc(att_in[t // FOLD], 16)

            pool.wait_ge(buf_zeroed, 16 * (EXPERTS * SLOTS // (128 * ZROWS) + 1))
            pool.wait_ge(slots_ready, 1)
            for t in range(TILES):
                pool.indirect_dma_start(buf_d, bass.IndirectOffsetOnAxis(ap=slot_i[:, t:t + 1], axis=0), xn[:, t, :], None,
                                        bounds_check=EXPERTS * SLOTS - 1, oob_is_err=False).then_inc(scattered, 16)
            with pool.Fori(1, EXPERTS) as e:
                halve_weights(e, True)
            for b in range(2):
                pool.wait_ge(y_stored[b], EXPERTS // 2 * 32)
            for t in range(TILES):
                pool.indirect_dma_start(yg[:, t, :], None, ybuf_d, bass.IndirectOffsetOnAxis(ap=row_i[:, t:t + 1], axis=0)).then_inc(y_in[t // FOLD], 16)

            for b in range(2):
                pool.memset(att3[b][:], 1.0).then_inc(edge_set, 1)
            pool.memset(w3[:], 0.0).then_inc(edge_set, 1)
            pool.memset(b3[:], 0.0).then_inc(edge_set, 1)
            pool.tensor_copy(one_row[:], ones[0:STACK + 1, :]).then_inc(edge_w_ready, 1)
            pool.wait_ge(node_w_in, 16 * 5)
            pool.tensor_copy(wf2s[:, 0], wf2[:]).then_inc(edge_w_ready, 1)
            pool.wait_ge(edge_w_ready, 2)
            pool.tensor_tensor(wf2s[:, 1], wf2[:], wf2s[:, 0].bitcast(F32), ALU.subtract).then_inc(edge_w_ready, 1)

            def copy_gather_indices(c, b, warm):
                if warm:
                    for t in range(GROUP):
                        pool.wait_ge(xg_in[b][t], (c // 2) * 16 if isinstance(c, int) else (c - b) * 8)
                pool.tensor_copy(gidx[b][:], dst_col[:, bass.ds(c * GROUP, GROUP)]).then_inc(gidx_ready, 1)

            def gather(c, b, t, warm):
                waits(pool, pool_passed, (gidx_ready, c + 1), *([(msg_ready, (c - 2) * GROUP + t + 1)] if warm else []))
                pool.indirect_dma_start(xg[b][:, t, :], None, xn_d, bass.IndirectOffsetOnAxis(ap=gidx[b][:, t:t + 1], axis=0)).then_inc(xg_in[b][t], 16)

            def scatter(c, b, t, warm):
                waits(pool, pool_passed, (sidx_ready, c + 1), (sum_copied, c * GROUP + t + 1), *([(added[t], c * 16)] if warm else []))
                pool.indirect_dma_start(agg_d[t], bass.IndirectOffsetOnAxis(ap=sidx[b][:, t:t + 1], axis=0), summed[b][:, t, :], None,
                                        compute_op=ALU.add).then_inc(added[t], 16)

            def edge_chunk(c, b, last=False):
                if not last:
                    warm_next = not isinstance(c, int) or c >= 1
                    copy_gather_indices(c + 1, 1 - b, warm_next)
                for t in range(GROUP):
                    if not last:
                        gather(c + 1, 1 - b, t, warm_next)
                    scatter(c, b, t, not isinstance(c, int) or c >= 1)

            pool.wait_ge(col_in, 32)
            pool.wait_ge(agg_zeroed, N_ZERO * 16)
            pool.wait_ge(xn_stored, 16 * FOLDS)

            def gathers():
                copy_gather_indices(0, 0, False)
                for t in range(GROUP):
                    gather(0, 0, t, False)
                chunks(pool, lambda c, b, n, left: edge_chunk(c, b, not left), 1)

            def rows_low(c, b):
                waits(pool, pool_passed, (xw_high, c + 1))
                pool.tensor_tensor(xws[b][:, 1, :], xw[b][:], xws[b][:, 0, :].bitcast(F32), ALU.subtract).then_inc(xw_low, 1)

            def window_chunk(c, b, n, left):
                if left:
                    rows_low(c + 1, 1 - b)
                for t in range(GROUP):
                    scatter(c, b, t, warm(c, 1))

            def windows():
                rows_low(0, 0)
                chunks(pool, window_chunk, 1)

            by_path(pool, windows, gathers)

            def halve_dense(e, b, warm):
                waits(pool, pool_passed, (dw_in, (e + 1) * 48), *([(d3_mm, (e - 1) * TILES)] if warm else []))
                pool.tensor_copy(dw[b][0][:], dw_full[:]).then_inc(dw_halved, 1)
                waits(pool, pool_passed, (dw_halved, e * 2 + 1))
                pool.tensor_tensor(dw[b][1][:], dw_full[:], dw[b][0][:].bitcast(F32), ALU.subtract).then_inc(dw_halved, 1)

            for e in range(2):
                halve_dense(e, e, False)
            with pool.Fori(1, EXPERTS // 2) as i:
                for b in range(2):
                    halve_dense(i * 2 + b, b, True)

        @block.tensor
        def _(pe):
            pe.wait_ge(consts_ready, 4)

            def turn(k, t, used, count):
                pe.wait_ge(ln_tile, (0, 1, 3)[k] * TILES + t + 1)
                if t >= 2:
                    pe.wait_ge(used, count + t - 1)
                for j in range(KD):
                    ins = pe.transpose(bank[t % 2][:, j * P:(j + 1) * P], xn[:, t, j * HALF:(j + 1) * HALF], ident[0:P, 0:P])
                ins.then_inc(turned, 1)

            pe.wait_ge(waug_ready, 1)

            def table(t):
                pe.wait_ge(turned_copied, t + 1)
                if t >= 2:
                    pe.wait_ge(tab_copied, t - 1)
                for k in range(KD):
                    ins = pe.matmul(bank[2 + t % 2][0:P, 0:TAB], xT[:, k, t * P:(t + 1) * P], waug[:, k, :], start=k == 0, stop=k == KD - 1)
                ins.then_inc(tab_mm, 1)

            for t in range(TILES + 1):
                if t < TILES:
                    turn(0, t, turned_copied, 0)
                if t >= 1:
                    table(t - 1)

            pe.wait_ge(small_w_in, 32)
            for t in range(TILES + 1):
                if t < TILES:
                    turn(1, t, turned_copied, TILES)
                if t >= 1:
                    u = t - 1
                    pe.wait_ge(turned_copied, TILES + u + 1)
                    for j in range(KD):
                        ins = pe.matmul(bank[4][0:P, u * EXPERTS:(u + 1) * EXPERTS], xT[:, j, u * P:(u + 1) * P], gate_w[:, j, :], start=j == 0, stop=j == KD - 1)
                    ins.then_inc(gate_mm, 1)
            pe.wait_ge(count_ready, 1)
            pe.matmul(bank[5][0:P, 0:EXPERTS], upper[:], tot8[:], start=True, stop=True).then_inc(count_mm, 1)

            def expert(e, b, n):
                warm = not isinstance(e, int) or e >= 1
                pe.wait_ge(brow_in[b], n * 16)
                if warm:
                    pe.wait_ge(b_low, e * KD)
                for k in range(KD):
                    for j in range(ROW_TILES):
                        ins = pe.transpose(bank[k][:, j * HALF:(j + 1) * HALF], brow[b][:, j, k * HALF:(k + 1) * HALF], ident[:])
                    ins.then_inc(b_turned, 1)
                pe.wait_ge(w_halved, e * 4 + 2)
                pe.wait_ge(b_low, (e + 1) * KD)
                for f in range(FC):
                    if warm or f >= 4:
                        pe.wait_ge(ff1_act, (e * FC + f - 3) * 2)
                    three_passes(pe, bank[2 + f % 4][:, 0:CAP_EVEN], [[w1[h][:, k, f * HALF:(f + 1) * HALF] for h in range(2)] for k in range(KD)],
                                 [[bT[h][:, k, 0:CAP_EVEN] for h in range(2)] for k in range(KD)]).then_inc(ff1_mm, 1)
                pe.wait_ge(w_halved, (e + 1) * 4)
                pe.wait_ge(ff1_low, (e + 1) * FC)
                for j in range(ROW_TILES):
                    m = HALF if j < ROW_TILES - 1 else LAST_ROWS
                    if warm or j >= 2:
                        pe.wait_ge(ff2_bias, e * ROW_TILES + j - 1)
                    three_passes(pe, bank[6 + j % 2][0:m, 0:D], [[hid[h][:, f, j * HALF:j * HALF + m] for h in range(2)] for f in range(FC)],
                                 [[w2[h][:, f, :] for h in range(2)] for f in range(FC)]).then_inc(ff2_mm, 1)

            for e in range(2):
                expert(e, e, 1)
            with pe.Fori(1, EXPERTS // 2) as i:
                for b in range(2):
                    expert(i * 2 + b, b, i + 1)

            def edge_first(c, b, n):
                pe.wait_ge(attr_in[b], n * 16)
                for a, (lo, hi) in enumerate(PIECES):
                    for k in range(KD):
                        if not isinstance(c, int) or c >= 1:
                            pe.wait_ge(e1_silu, (c - 1) * 4 + 2 * a + k + 1)
                        pe.matmul(bank[2 * a + k][:, 0:hi - lo], wf1[:, k * HALF:(k + 1) * HALF], attr[b][:, lo:hi],
                                  start=True, stop=True).then_inc(e1_mm, 1)

            def edge_filter(c, b, t):
                if t == 0:
                    pe.wait_ge(e1_silu, c * 4 + 2)
                if t == 3:
                    pe.wait_ge(e1_silu, c * 4 + 4)
                g = c * GROUP + t
                if not isinstance(c, int) or g >= 2:
                    pe.wait_ge(filt_ready, g - 1)
                for k in range(KD):
                    ins = pe.matmul(bank[4 + (b + t) % 2][0:P, 0:D], eh[b][:, k, t * P:(t + 1) * P], wf2[:, k, :], start=k == 0, stop=k == KD - 1)
                ins.then_inc(e2_mm, 1)

            def edge_sum(c, b, t):
                g = c * GROUP + t
                pe.wait_ge(msg_ready, g + 1)
                pe.wait_ge(same_ready, c + 1)
                if not isinstance(c, int) or g >= 2:
                    pe.wait_ge(sum_copied, g - 1)
                pe.matmul(bank[6 + (b + t) % 2][0:P, 0:D], same[b][:, t, :], msg[(b + t) % 2][:], start=True, stop=True).then_inc(sum_mm, 1)

            def edge_chunk(c, b, n_next, last=False):
                if not last:
                    edge_first(c + 1, 1 - b, n_next)
                for t in range(GROUP + 1):
                    if t < GROUP:
                        edge_filter(c, b, t)
                    if t >= 1:
                        edge_sum(c, b, t - 1)

            pe.wait_ge(node_w_in, 16 * 5)
            pe.wait_ge(ff2_bias, EXPERTS * ROW_TILES)
            pe.wait_ge(ends_ready, 1)
            for j in range(2):
                ins = pe.transpose(bank[j][0:CHUNKS, 0:P], ends[:, j, :], ident[0:P, 0:P])
            ins.then_inc(ends_turned, 1)
            pe.wait_ge(window_ready, 1)
            for j in range(2):
                ins = pe.transpose(bank[2][0:1, j * CHUNKS:(j + 1) * CHUNKS], span[:, 2 + j:3 + j], ident[0:CHUNKS, 0:CHUNKS])
            ins.then_inc(window_turned, 1)
            pe.wait_ge(window_int, 1)
            pe.matmul(bank[3][:, 0:CHUNKS], ones[0:1, :], window_f[:, 0:CHUNKS], start=True, stop=True).then_inc(window_spread, 1)

            def gathers():
                edge_first(0, 0, 1)
                chunks(pe, lambda c, b, n, left: edge_chunk(c, b, next_n(b, n), not left), 1)

            def window_first(c, b, a):
                if a == 0:
                    pe.wait_ge(att_low, c + 1)
                if warm(c * NT + a, 2):
                    pe.wait_ge(hid_act, (c * NT + a - 1) * 2)
                lo, m = [v * P for v in THIRDS[a]]
                w = m + m % 2
                for k in range(KD):
                    ins = pe.matmul(bank[GROUP + (b + a) % 2][:, k * w:(k + 1) * w], w3s[:, k * HALF:(k + 1) * HALF], att3s[b][:, lo + m - w:lo + m], start=True, stop=True)
                ins.then_inc(hid_mm, 1)

            def window_pair(c, b, t):
                if t == 0:
                    pe.wait_ge(hid_low, c * NT + 1)
                    pe.wait_ge(xw_low, c + 1)
                    pe.wait_ge(hot_ready, c + 1)
                elif t % 2 == 0:
                    pe.wait_ge(hid_low, c * NT + t // 2 + 1)
                if warm(c, 1):
                    pe.wait_ge(msg_ready, (c - 1) * GROUP + t + 1)
                dst = bank[t]
                ts = slice(t * P, (t + 1) * P)
                three_passes(pe, dst[0:P, 0:D], [[eh2[b][h][:, k, ts] for h in range(2)] for k in range(KD)],
                             [[wf2s[:, h, k, :] for h in range(2)] for k in range(KD)], last=False)
                pe.matmul(dst[0:P, 0:D], one_row[:, 0:P], b3s[:], start=False, stop=True)
                for h in range(2):
                    ins = pe.matmul(dst[0:P, D:2 * D], hot[b][:, ts], xws[b][:, h, :], start=h == 0, stop=h == 1)
                ins.then_inc(pair_mm, 1)

            def window_sum(c, b, t):
                g = c * GROUP + t
                pe.wait_ge(msg_ready, g + 1)
                if warm(g, 1):
                    pe.wait_ge(sum_copied, g)
                pe.matmul(bank[7][0:P, 0:D], same[b][:, t, :], msgs[:, t, :], start=True, stop=True).then_inc(sum_mm, 1)

            def window_chunk(c, b, n, left):
                for t in range(GROUP):
                    window_pair(c, b, t)
                    if t == 0:
                        window_first(c, b, 2)
                    elif left and t in (1, 3):
                        window_first(c + 1, 1 - b, t // 2)
                    behind = tiles_behind(c, b, t, 2)
                    if behind:
                        window_sum(*behind)
                if not left:
                    for t in range(GROUP - 2, GROUP):
                        window_sum(c, b, t)

            def windows():
                pe.wait_ge(edge_w_ready, 3)
                pe.wait_ge(stack_ready, 1)
                for a in range(2):
                    window_first(0, 0, a)
                chunks(pe, window_chunk, 1)

            by_path(pe, windows, gathers)

            pe.wait_ge(sum_copied, E_TILES)

            def fold_turn(f):
                pe.wait_ge(agg_ready, f + 1)
                for q in range(FOLD):
                    g = f * FOLD + q
                    if g >= 2:
                        pe.wait_ge(agg_copied, g - 1)
                    for k in range(KD):
                        ins = pe.transpose(bank[g % 2][:, k * P:(k + 1) * P], part[f % 2][0][:, q, k * HALF:(k + 1) * HALF], ident[0:P, 0:P])
                    ins.then_inc(agg_turned, 1)

            def fold_layer(f, w, src, used, need, done, at):
                pe.wait_ge(used, need)
                for a, (lo, hi) in enumerate(PIECES):
                    for o in range(KD):
                        n = f * 4 + a * 2 + o
                        if n >= 2:
                            pe.wait_ge(u_silu if done is u_mm else h_ready, n - 1)
                        for k in range(KD):
                            ins = pe.matmul(bank[at + o][:, 0:hi - lo], w[:, k, o * HALF:(o + 1) * HALF], src[:, k, lo:hi], start=k == 0, stop=k == KD - 1)
                        ins.then_inc(done, 1)

            for f in range(FOLDS + 1):
                if f < FOLDS:
                    fold_turn(f)
                    fold_layer(f, wu1, aggT[f % 2], agg_copied, (f + 1) * FOLD, u_mm, 2)
                if f >= 1:
                    fold_layer(f - 1, wu2, uT[(f - 1) % 2], u_silu, f * 4, h_mm, 4)

            pe.wait_ge(wr_halved, 2)
            for f in range(FOLDS + 1):
                if f < FOLDS:
                    pe.wait_ge(bn_applied, KD * (f + 1))
                    for t in range(f * FOLD, (f + 1) * FOLD):
                        if t >= 2:
                            pe.wait_ge(x3_ready, t - 1)
                        for k in range(KD):
                            ins = pe.transpose(bank[6 + t % 2][0:P, k * HALF:(k + 1) * HALF], xT[:, k, t * P:(t + 1) * P], ident[:])
                        ins.then_inc(bn_turned, 1)
                if f >= 1:
                    for t in range((f - 1) * FOLD, f * FOLD):
                        turn(2, t, x_low, 0)
                    for t in range((f - 1) * FOLD, f * FOLD):
                        pe.wait_ge(x_low, t + 1)
                        three_passes(pe, bank[4][0:P, t * EXPERTS:(t + 1) * EXPERTS], [[xTs[h][:, k, t * P:(t + 1) * P] for h in range(2)] for k in range(KD)],
                                     [[wrs[:, h, k * EXPERTS:(k + 1) * EXPERTS] for h in range(2)] for k in range(KD)]).then_inc(mix_mm, 1)

            def dense_layer(e, b, s, layer):
                at, n = STEPS[s]
                m = n * P
                done, act = ((d1_mm, d1_act), (d2_mm, d2_act))[layer]
                g = e * (NS * KD) + s * KD
                if layer == 1:
                    pe.wait_ge(d1_low, g + KD)
                for o in range(KD):
                    if not isinstance(e, int) or e or s:
                        pe.wait_ge(act, (g + o - 1) * 2)
                    src = xTs if layer == 0 else h1[s % 2]
                    w = m + m % 2
                    lo = at * P + m - w if layer == 0 else 0
                    three_passes(pe, bank[2 * layer + o][:, 0:w], [[dw[b][h][:, layer * KD + k, o * HALF:(o + 1) * HALF] for h in range(2)] for k in range(KD)],
                                 [[src[h][:, k, lo:lo + w] for h in range(2)] for k in range(KD)]).then_inc(done, 1)

            def dense_last(e, b, s):
                at, n = STEPS[s]
                pe.wait_ge(d2_low, e * (NS * KD) + s * KD + KD)
                if isinstance(e, int) and e == 0 and s == 0:
                    pe.wait_ge(mix_shift, 1)
                for q in range(n):
                    g = e * TILES + at + q
                    if not isinstance(e, int) or e or at + q >= 2:
                        pe.wait_ge(d3_added, g - 1)
                    three_passes(pe, bank[4 + (b + at + q) % 2][0:P, 0:D], [[h2[s % 2][h][:, k, q * P:(q + 1) * P] for h in range(2)] for k in range(KD)],
                                 [[dw[b][h][:, 2 * KD + k, :] for h in range(2)] for k in range(KD)]).then_inc(d3_mm, 1)

            def dense_expert(e, b):
                pe.wait_ge(dw_halved, (e + 1) * 2)
                for s in range(NS + 2):
                    if s < NS:
                        dense_layer(e, b, s, 0)
                    if 1 <= s <= NS:
                        dense_layer(e, b, s - 1, 1)
                    if s >= 2:
                        dense_last(e, b, s - 2)

            dense_expert(0, 0)
            pe.wait_ge(mix_ready, 1)
            for t in range(TILES + 1):
                if t < TILES:
                    pe.transpose(bank[6][0:EXPERTS, 0:P], mix[:, t, :], ident[0:P, 0:P]).then_inc(mix_turned, 1)
                    pe.wait_ge(mixT_ready, t + 1)
                if t >= 1:
                    u = t - 1
                    if u >= 1:
                        pe.wait_ge(bo_added, u)
                    pe.matmul(bank[7][0:P, 0:D], mixT[:, u * P:(u + 1) * P], bo[:], start=True, stop=True).then_inc(bo_mm, 1)
            dense_expert(1, 1)
            with pe.Fori(1, EXPERTS // 2) as i:
                for b in range(2):
                    dense_expert(i * 2 + b, b)

        @block.scalar
        def _(act):
            def ln_sqrt(k, f):
                act.wait_ge(ln_var, k * FOLDS + f + 1)
                act.activation(rstd[:, f * FOLD:(f + 1) * FOLD], mv[:, f * FOLD:(f + 1) * FOLD, 1], ACT.Sqrt, bias=eps1[0:P, 0:1]).then_inc(ln_std, 1)

            def turn_copies(k, f):
                for t in range(f * FOLD, (f + 1) * FOLD):
                    act.wait_ge(turned, k * TILES + t + 1)
                    dst = xT if k < 2 else xTs[0]
                    act.activation(dst[:, :, t * P:(t + 1) * P], bank[t % 2][:, 0:KD * P].rearrange("p (k e) -> p k e", k=KD), ACT.Copy).then_inc(turned_copied, 1)

            act.wait_ge(consts_ready, 8)
            for f in range(FOLDS + 1):
                if f < FOLDS:
                    ln_sqrt(0, f)
                if f >= 1:
                    turn_copies(0, f - 1)
            act.wait_ge(vec_in, 32)
            for j, v in enumerate(("v1", "v2")):
                ins = act.activation(scl[:, j, :], chan[:, PAIR_AT[v]:PAIR_AT[v] + EXPERTS * KD], ACT.Sqrt, bias=eps1[:, 1:2])
                ins.then_inc(aff_std, 1)
            for f in range(FOLDS + 1):
                if f < FOLDS:
                    fs = slice(f * FOLD, (f + 1) * FOLD)
                    act.wait_ge(att_shift, f + 1)
                    act.activation(sm8[:, 1, fs, 0:HEADS], sm8[:, 0, fs, 0:HEADS], ACT.Exp).then_inc(att_exp, 1)
                    ln_sqrt(1, f)
                if f >= 1:
                    turn_copies(1, f - 1)
            act.wait_ge(gate_shift, 1)
            act.activation(sm8[:, 2, :, :], sm8[:, 1, :, :], ACT.Exp).then_inc(gate_exp, 1)

            def expert(e):
                for k in range(KD):
                    act.wait_ge(b_turned, e * KD + k + 1)
                    if not isinstance(e, int) or e >= 1:
                        act.wait_ge(ff1_mm, e * FC)
                    act.activation(bT[0][:, k, :], bank[k][:], ACT.Copy).then_inc(b_high, 1)
                for f in range(FC):
                    g = e * FC + f
                    waits(act, act_passed, (ff1_mm, g + 1), *([] if isinstance(e, int) and e == 0 and f < 2 else [(ff1_low, g - 1)]))
                    bias = chan[:, bass.ds(e * FC + FFB1_AT + f, 1)]
                    act.activation(act_full[f % 2][:, 0:CAP_EVEN], bank[2 + f % 4][:, 0:CAP_EVEN], ACT.Relu, bias=bias).then_inc(ff1_act, 1)
                    act.activation(hid[0][:, f, 0:CAP_EVEN], bank[2 + f % 4][:, 0:CAP_EVEN], ACT.Relu, bias=bias).then_inc(ff1_act, 1)

            expert(0)
            with act.Fori(1, EXPERTS) as e:
                expert(e)

            for f in range(FOLDS):
                ln_sqrt(2, f)

            def edge_silu(c, b):
                for a, (lo, hi) in enumerate(PIECES):
                    for k in range(KD):
                        act.wait_ge(e1_mm, c * 4 + 2 * a + k + 1)
                        if not isinstance(c, int) or c >= 2:
                            act.wait_ge(e2_mm, (c - 1) * GROUP)
                        act.activation(eh[b][:, k, lo:hi], bank[2 * a + k][:, 0:hi - lo], ACT.Silu,
                                       bias=chan[:, CH_AT["bf1"] + k:CH_AT["bf1"] + k + 1]).then_inc(e1_silu, 1)

            def edge_chunk(c, b, last=False):
                if not last:
                    edge_silu(c + 1, 1 - b)
                for t in range(GROUP):
                    g = c * GROUP + t
                    act.wait_ge(sum_mm, g + 1)
                    if not isinstance(c, int) or c >= 2:
                        act.wait_ge(added[t], (c - 1) * 16)
                    act.activation(summed[b][:, t, :], bank[6 + (b + t) % 2][0:P, 0:D], ACT.Copy).then_inc(sum_copied, 1)

            def gathers():
                edge_silu(0, 0)
                chunks(act, lambda c, b, n, left: edge_chunk(c, b, not left), 1)

            def inputs_high(c, b, n):
                act.wait_ge(attr_in[b], n * 48)
                if warm(c, 2):
                    act.wait_ge(hid_mm, (c - 1) * NT)
                act.activation(att3s[b][:], att3[b][:], ACT.Copy).then_inc(att_high, 1)

            def rows_high(c, b, n):
                act.wait_ge(srow_in[b], n * 48)
                if warm(c, 2):
                    act.wait_ge(pair_mm, (c - 1) * GROUP)
                act.activation(xws[b][:, 0, :], xw[b][:], ACT.Copy).then_inc(xw_high, 1)

            def window_silu(c, b, a):
                lo, m = [v * P for v in THIRDS[a]]
                act.wait_ge(hid_mm, c * NT + a + 1)
                if warm(c, 1):
                    act.wait_ge(hid_low, (c - 1) * NT + a + 1)
                if warm(c, 2):
                    act.wait_ge(pair_mm, (c - 1) * GROUP)
                w = m + m % 2
                src = bank[GROUP + (b + a) % 2][:, 0:KD * w].rearrange("p (k e) -> p k e", k=KD)[:, :, w - m:w]
                for dst in (eh_full, eh2[b][0]):
                    act.activation(dst[:, :, lo:lo + m], src, ACT.Silu, bias=eps1[:, 2:3]).then_inc(hid_act, 1)

            def window_ends(c, b, t):
                act.wait_ge(pair_mm, c * GROUP + t + 1)
                if warm(c, 1):
                    act.wait_ge(msg_ready, (c - 1) * GROUP + t + 1)
                act.activation(ends_x[:, t, :], bank[t][0:P, D:2 * D], ACT.Copy).then_inc(ends_copied, 1)

            def window_copy(c, b, t):
                act.wait_ge(sum_mm, c * GROUP + t + 1)
                if warm(c, 2):
                    act.wait_ge(added[t], (c - 1) * 16)
                act.activation(summed[b][:, t, :], bank[7][0:P, 0:D], ACT.Copy).then_inc(sum_copied, 1)

            def window_chunk(c, b, n, left):
                for t in range(GROUP):
                    window_ends(c, b, t)
                    if t == 0 and left:
                        rows_high(c + 1, 1 - b, next_n(b, n))
                    elif t == 1:
                        window_silu(c, b, 2)
                    elif t == 3 and left == 2:
                        inputs_high(c + 2, b, n + 1)
                    elif t in (2, 4) and left:
                        window_silu(c + 1, 1 - b, t // 2 - 1)
                    behind = tiles_behind(c, b, t, 2)
                    if behind:
                        window_copy(*behind)
                if not left:
                    for t in range(GROUP - 2, GROUP):
                        window_copy(c, b, t)

            def windows():
                for c in range(2):
                    inputs_high(c, c, 1)
                rows_high(0, 0, 1)
                for a in range(2):
                    window_silu(0, 0, a)
                chunks(act, window_chunk, 2)

            by_path(act, windows, gathers)

            def fold_copies(f):
                for q in range(FOLD):
                    g = f * FOLD + q
                    act.wait_ge(agg_turned, g + 1)
                    if f >= 2:
                        act.wait_ge(u_mm, (f - 1) * 4)
                    act.activation(aggT[f % 2][:, :, q * P:(q + 1) * P], bank[g % 2][:, 0:KD * P].rearrange("p (k e) -> p k e", k=KD), ACT.Copy).then_inc(agg_copied, 1)
                for a, (lo, hi) in enumerate(PIECES):
                    for o in range(KD):
                        act.wait_ge(u_mm, f * 4 + a * 2 + o + 1)
                        if f >= 2:
                            act.wait_ge(h_mm, (f - 1) * 4)
                        act.activation(uT[f % 2][:, o, lo:hi], bank[2 + o][:, 0:hi - lo], ACT.Silu,
                                       bias=chan[:, CH_AT["bu1"] + o:CH_AT["bu1"] + o + 1]).then_inc(u_silu, 1)

            def fold_bias(f):
                for a, (lo, hi) in enumerate(PIECES):
                    for o in range(KD):
                        act.wait_ge(h_mm, f * 4 + a * 2 + o + 1)
                        act.activation(xT[:, o, f * FOLD * P + lo:f * FOLD * P + hi], bank[4 + o][:, 0:hi - lo], ACT.Identity,
                                       bias=chan[:, CH_AT["bu2"] + o:CH_AT["bu2"] + o + 1]).then_inc(h_ready, 1)

            for f in range(FOLDS + 1):
                if f < FOLDS:
                    fold_copies(f)
                if f >= 1:
                    fold_bias(f - 1)
            act.wait_ge(bn_var, 1)
            act.activation(csc[:, 0, :], cmv[:, :, 1], ACT.Sqrt, bias=eps1[:, 0:1]).then_inc(bn_std, 1)
            act.wait_ge(bn_scale, 1)
            for f in range(FOLDS):
                for k in range(KD):
                    act.activation(xT[:, k, f * FOLD * P:(f + 1) * FOLD * P], xT[:, k, f * FOLD * P:(f + 1) * FOLD * P], ACT.Identity,
                                   bias=csc[:, 2, k:k + 1], scale=csc[:, 1, k:k + 1]).then_inc(bn_applied, 1)
            for f in range(FOLDS + 1):
                if f < FOLDS:
                    ln_sqrt(3, f)
                if f >= 1:
                    turn_copies(2, f - 1)
            act.wait_ge(mix_shift, 1)
            act.activation(sm8[:, 1, :, :], sm8[:, 0, :, :], ACT.Exp).then_inc(mix_exp, 1)
            act.wait_ge(aff_ready, 1)
            act.wait_ge(bn_turned, TILES)

            def dense_act(e, s, layer):
                at, n = STEPS[s]
                m = n * P
                mm, done, low, used = ((d1_mm, d1_act, d1_low, d2_mm), (d2_mm, d2_act, d2_low, d3_mm))[layer]
                g = e * (NS * KD) + s * KD
                dst = (h1, h2)[layer][s % 2][0]
                for o in range(KD):
                    need = [] if isinstance(e, int) and e == 0 and s == 0 else [(low, g + o - 1)]
                    if s >= 2:
                        need += [(used, (g - KD) if layer == 0 else e * TILES + STEPS[s - 2][0] + STEPS[s - 2][1])]
                    elif not isinstance(e, int) or e:
                        need += [(used, e * (NS * KD) if layer == 0 else e * TILES)]
                    waits(act, act_passed, (mm, g + o + 1), *need)
                    bias, scale = [v[:, layer, bass.ds(e * KD + o, 1)] for v in (shf, scl)]
                    off = m % 2 if layer == 0 else 0
                    for out_ in (h_full[layer][o][:, 0:m], dst[:, o, 0:m]):
                        act.activation(out_, bank[2 * layer + o][:, off:off + m], ACT.Relu, bias=bias, scale=scale).then_inc(done, 1)

            def dense_expert(e):
                for s in range(NS + 1):
                    if s < NS:
                        dense_act(e, s, 0)
                    if s >= 1:
                        dense_act(e, s - 1, 1)

            dense_expert(0)
            for t in range(TILES):
                act.wait_ge(mix_turned, t + 1)
                act.activation(mixT[:, t * P:(t + 1) * P], bank[6][0:EXPERTS, 0:P], ACT.Copy).then_inc(mixT_ready, 1)
            with act.Fori(1, EXPERTS) as e:
                dense_expert(e)

        @block.vector
        def _(dve):
            chain = Tally(dve_chain)

            def step(ins):
                dve.wait_ge(chain.sem, chain.inc(ins))

            def ln_stats(k, f):
                for t in range(f * FOLD, (f + 1) * FOLD):
                    ins = dve.bn_stats(stats[:, t, :], x[:, t, :])
                step(ins)
                for t in range(f * FOLD, (f + 1) * FOLD):
                    ins = dve.bn_aggr(mv[:, t, :], stats[:, t, :])
                ins.then_inc(ln_var, 1)

            def ln_apply(k, f):
                r = rstd[:, f * FOLD:(f + 1) * FOLD]
                dve.wait_ge(ln_std, k * FOLDS + f + 1)
                step(dve.reciprocal(r, r))
                for t in range(f * FOLD, (f + 1) * FOLD):
                    dve.tensor_scalar(xn[:, t, 0:D], x[:, t, :], mv[:, t, 0:1], rstd[:, t:t + 1], ALU.subtract, ALU.mult).then_inc(ln_tile, 1)

            dve.wait_ge(vec_in, 16)
            dve.wait_ge(gnn_w_in, 16)
            for j, name in enumerate(("attn_l", "attn_r")):
                w4 = waug[:, :, 0:D].rearrange("p k (h d) -> p k h d", d=HEAD_D)
                a4 = row[name].rearrange("p (h d) -> p h d", d=HEAD_D)
                for k in range(KD):
                    ins = dve.tensor_tensor(wprod[:, k * HEADS:(k + 1) * HEADS, :], w4[:, k], a4, ALU.mult)
                step(ins)
                for k in range(KD):
                    ins = dve.tensor_reduce(waug[:, k, D + j * HEADS:D + (j + 1) * HEADS], wprod[:, k * HEADS:(k + 1) * HEADS, :], AX_X, ALU.add)
                if j == 0:
                    step(ins)
            ins.then_inc(waug_ready, 1)

            def table_copies(f):
                for t in range(f * FOLD, (f + 1) * FOLD):
                    dve.wait_ge(tab_mm, t + 1)
                    dve.tensor_copy(tab[:, t, :], bank[2 + t % 2][0:P, 0:TAB]).then_inc(tab_copied, 1)

            for f in range(FOLDS + 2):
                if f < FOLDS:
                    dve.wait_ge(x_in[f], 16)
                    ln_stats(0, f)
                if 1 <= f <= FOLDS:
                    ln_apply(0, f - 1)
                if f >= 2:
                    table_copies(f - 2)

            dve.wait_ge(vec_in, 32)
            dve.wait_ge(aff_std, 2)
            step(dve.reciprocal(scl[:].rearrange("p a b -> p (a b)"), scl[:].rearrange("p a b -> p (a b)")))

            def pair(name):
                return chan[:, PAIR_AT[name]:PAIR_AT[name] + EXPERTS * KD]

            for j in range(2):
                dve.tensor_tensor(shf[:, j, :], pair(f"b{j + 1}"), pair(f"m{j + 1}"), ALU.subtract)
                ins = dve.tensor_tensor(scl[:, j, :], scl[:, j, :], pair(f"g{j + 1}"), ALU.mult)
            step(ins)
            for j in range(2):
                ins = dve.tensor_tensor(shf[:, j, :], shf[:, j, :], scl[:, j, :], ALU.mult)
            step(ins)
            for j in range(2):
                ins = dve.tensor_tensor(shf[:, j, :], shf[:, j, :], pair(f"be{j + 1}"), ALU.add)
            ins.then_inc(aff_ready, 1)
            dve.wait_ge(small_w_in, 32)
            wr_flat = wr[:].rearrange("p k e -> p (k e)")
            dve.tensor_copy(wrs[:, 0, :], wr_flat).then_inc(wr_halved, 1)
            dve.wait_ge(wr_halved, 1)
            dve.tensor_tensor(wrs[:, 1, :], wr_flat, wrs[:, 0, :].bitcast(F32), ALU.subtract).then_inc(wr_halved, 1)

            def attend(f):
                fs = slice(f * FOLD, (f + 1) * FOLD)

                def over_heads(v):
                    return v[:, fs].rearrange("p (t o) -> p t o", o=1).to_broadcast([P, FOLD, HEADS])

                dve.wait_ge(att_in[f], 2 * FOLD * 16)
                s4, e4 = sm8[:, 0, fs, 0:HEADS], sm8[:, 1, fs, 0:HEADS]
                step(dve.tensor_tensor(s4, tsrc[:, fs, :], tdst[:, fs, D + HEADS:TAB], ALU.add))
                step(dve.scalar_tensor_tensor(s4, s4, LEAK, s4, ALU.mult, ALU.max))
                step(dve.tensor_reduce(sm1[:, 0, fs], s4, AX_X, ALU.max))
                dve.tensor_tensor(s4, s4, over_heads(sm1[:, 0, :]), ALU.subtract).then_inc(att_shift, 1)
                dve.wait_ge(att_exp, f + 1)
                step(dve.tensor_reduce(sm1[:, 1, fs], e4, AX_X, ALU.add))
                step(dve.reciprocal(sm1[:, 1, fs], sm1[:, 1, fs]))
                step(dve.tensor_tensor(e4, e4, over_heads(sm1[:, 1, :]), ALU.mult))
                for h in range(HEADS):
                    hd = tdst[:, fs, h * HEAD_D:(h + 1) * HEAD_D]
                    ins = dve.tensor_tensor(hd, hd, sm8[:, 1, fs, h:h + 1].to_broadcast([P, FOLD, HEAD_D]), ALU.mult)
                step(ins)
                step(dve.tensor_tensor(tdst[:, fs, 0:2 * HEAD_D], tdst[:, fs, 0:2 * HEAD_D], tdst[:, fs, 2 * HEAD_D:4 * HEAD_D], ALU.add))
                step(dve.tensor_tensor(tdst[:, fs, 0:HEAD_D], tdst[:, fs, 0:HEAD_D], tdst[:, fs, HEAD_D:2 * HEAD_D], ALU.add))
                for h in range(HEADS):
                    xh = x[:, fs, h * HEAD_D:(h + 1) * HEAD_D]
                    ins = dve.tensor_tensor(xh, xh, tdst[:, fs, 0:HEAD_D], ALU.add)
                step(ins)

            for f in range(FOLDS + 1):
                if f < FOLDS:
                    attend(f)
                    ln_stats(1, f)
                if f >= 1:
                    ln_apply(1, f - 1)

            def bc(v, n):
                return v.rearrange("p (t o) -> p t o", o=1).to_broadcast([P, TILES, n])

            def rowbc(v):
                return v.rearrange("p (o e) -> p o e", o=1).to_broadcast([P, TILES, EXPERTS])

            dve.wait_ge(consts_ready, 8)
            dve.wait_ge(gate_mm, TILES)
            lg, sh, ex, oh, cum, tmp = [sm8[:, j] for j in range(6)]
            g8 = bank[4][0:P, 0:TILES * EXPERTS].rearrange("p (t e) -> p t e", e=EXPERTS)
            step(dve.tensor_tensor(lg, g8, rowbc(row["gate_b"][0:P]), ALU.add))
            step(dve.tensor_reduce(sm1[:, 0, :], lg, AX_X, ALU.max))
            dve.tensor_tensor(sh, lg, bc(sm1[:, 0, :], EXPERTS), ALU.subtract).then_inc(gate_shift, 1)
            step(dve.tensor_tensor(oh, lg, bc(sm1[:, 0, :], EXPERTS), ALU.is_equal))
            step(dve.tensor_tensor(tmp, oh, rowbc(rev[:]), ALU.mult))
            step(dve.tensor_reduce(sm1[:, 1, :], tmp, AX_X, ALU.max))
            step(dve.tensor_tensor(oh, tmp, bc(sm1[:, 1, :], EXPERTS), ALU.is_equal))
            dve.tensor_reduce(tot8[:], oh.rearrange("p t e -> p e t"), AX_X, ALU.add).then_inc(count_ready, 1)
            for e in range(EXPERTS):
                ins = dve.tensor_tensor_scan(cum[:, :, e], ones[0:P, 0:TILES], oh[:, :, e], 0.0, ALU.mult, ALU.add)
            step(ins)
            dve.wait_ge(count_mm, 1)
            step(dve.tensor_scalar(off8[:], bank[5][0:P, 0:EXPERTS], -1.0, None, ALU.add))
            step(dve.tensor_tensor(cum, cum, rowbc(off8[:]), ALU.add))
            dve.tensor_tensor(cum, cum, oh, ALU.mult)
            step(dve.tensor_tensor(tmp, oh, rowbc(eno[:]), ALU.mult))
            dve.tensor_reduce(sm1[:, 2, :], cum, AX_X, ALU.add)
            step(dve.tensor_reduce(sm1[:, 3, :], tmp, AX_X, ALU.add))
            pos, idx, kept, slot, drop, back, gate = [sm1[:, j, :] for j in (2, 3, 4, 5, 6, 7, 8)]
            dve.scalar_tensor_tensor(slot, idx, float(SLOTS), pos, ALU.mult, ALU.add)
            step(dve.tensor_scalar(kept, pos, float(CAP), None, ALU.is_lt))
            step(dve.scalar_tensor_tensor(back, idx, float(CAP), pos, ALU.mult, ALU.add))
            dve.tensor_scalar(drop, kept, -float(DROPPED), float(DROPPED), ALU.mult, ALU.add)
            step(dve.tensor_scalar(back, back, -float(ZERO_ROW), None, ALU.add))
            dve.tensor_tensor(slot, slot, drop, ALU.add)
            step(dve.tensor_tensor(back, back, kept, ALU.mult))
            step(dve.tensor_scalar(back, back, float(ZERO_ROW), None, ALU.add))
            dve.tensor_copy(row_i[:], back)
            dve.tensor_copy(slot_i[:], slot)
            dve.wait_ge(gate_exp, 1)
            step(dve.tensor_reduce(gate, ex, AX_X, ALU.add))
            step(dve.reciprocal(gate, gate))
            dve.tensor_copy(xn[:, :, D], gate).then_inc(slots_ready, 1)

            def expert(e, b, n):
                for k in range(KD):
                    dve.wait_ge(b_high, e * KD + k + 1)
                    dve.tensor_tensor(bT[1][:, k, :], bank[k][:], bT[0][:, k, :].bitcast(F32), ALU.subtract).then_inc(b_low, 1)
                for f in range(FC):
                    dve.wait_ge(ff1_act, (e * FC + f + 1) * 2)
                    dve.tensor_tensor(hid[1][:, f, 0:CAP_EVEN], act_full[f % 2][:, 0:CAP_EVEN], hid[0][:, f, 0:CAP_EVEN].bitcast(F32), ALU.subtract).then_inc(ff1_low, 1)
                if not isinstance(e, int):
                    dve.wait_ge(y_stored[b], n * 32)
                c = e * 12
                for h in range(2):
                    js = [(j, HALF if j < ROW_TILES - 1 else LAST_ROWS) for j in (2 * h, 2 * h + 1)]

                    def both(fn, k, done):
                        for q, (j, m) in enumerate(js):
                            ins = fn(j, m, ytmp[0][q][0:m], ytmp[1][q][0:m], ytmp[2][q][0:m])
                            if k is None:
                                ins.then_inc(done, 1)
                        if k is not None:
                            ins.then_inc(done, 1)
                            dve.wait_ge(done, c + h * 6 + k)

                    for j, m in js:
                        dve.wait_ge(ff2_mm, e * ROW_TILES + j + 1)
                        dve.tensor_tensor(ytmp[0][j % 2][0:m], bank[6 + j % 2][0:m, 0:D], b2[0:m, bass.ds(e * D, D)], ALU.add).then_inc(ff2_bias, 1)
                    dve.wait_ge(ff2_bias, e * ROW_TILES + 2 * h + 2)
                    both(lambda j, m, y, a, z: dve.tensor_scalar(y, y, brow[b][0:m, j, D:ROW], None, ALU.mult), 1, y_chain)
                    both(lambda j, m, y, a, z: dve.tensor_scalar(a, y, -FLT_MAX, FLT_MAX, ALU.max, ALU.min), 2, y_chain)
                    both(lambda j, m, y, a, z: dve.tensor_tensor(z, a, y, ALU.is_equal), 3, y_chain)
                    both(lambda j, m, y, a, z: dve.tensor_tensor(a, a, z, ALU.mult), 4, y_chain)
                    both(lambda j, m, y, a, z: dve.tensor_scalar(z, y, FLT_MAX, None, ALU.is_gt), 5, y_chain)
                    both(lambda j, m, y, a, z: dve.scalar_tensor_tensor(z, y, -FLT_MAX, z, ALU.is_lt, ALU.subtract), 6, y_chain)
                    for q, (j, m) in enumerate(js):
                        ins = dve.scalar_tensor_tensor(yrow[b][0:m, j, :], ytmp[2][q][0:m], -BIG, ytmp[1][q][0:m], ALU.mult, ALU.add)
                    ins.then_inc(y_ready, 1)

            dve.wait_ge(b2_in, 16)
            for e in range(2):
                expert(e, e, 0)
            with dve.Fori(1, EXPERTS // 2) as i:
                for b in range(2):
                    expert(i * 2 + b, b, i)

            dve.wait_ge(col_in, 32)
            step(dve.tensor_copy(dst_f[:], dst_col[:]))
            by_chunk = dst_f[:].rearrange("p (c g) -> p c g", g=GROUP)
            dve.tensor_reduce(ends[:, 0, :], by_chunk, AX_X, ALU.min)
            step(dve.tensor_reduce(ends[:, 1, :], by_chunk, AX_X, ALU.max))
            dve.tensor_copy(src_f[:], src_col[:]).then_inc(ends_ready, 1)
            dve.wait_ge(ends_ready, 1)
            dve.tensor_scalar(to_trash[:], src_f[:], -1.0, trash[:, 0:1], ALU.mult, ALU.add)
            dve.wait_ge(ends_turned, 1)
            dve.tensor_reduce(span[:, 0:1], bank[0][0:CHUNKS, 0:P], AX_X, ALU.min)
            step(dve.tensor_reduce(span[:, 1:2], bank[1][0:CHUNKS, 0:P], AX_X, ALU.max))
            step(dve.tensor_scalar(span[:, 2:3], span[:, 0:1], float(N_NODES - HALF), None, ALU.min))
            step(dve.tensor_tensor(span[:, 3:4], span[:, 1:2], span[:, 2:3], ALU.subtract))
            dve.tensor_scalar(span[:, 3:4], span[:, 3:4], float(HALF), None, ALU.is_lt).then_inc(window_ready, 1)
            dve.wait_ge(window_turned, 1)
            step(dve.tensor_copy(window_f[:], bank[2][0:1, 0:2 * CHUNKS]))
            dve.tensor_reduce(flag_f[:], window_f[:, CHUNKS:2 * CHUNKS], AX_X, ALU.min)
            step(dve.tensor_copy(window[:], window_f[:, 0:CHUNKS]))
            dve.tensor_copy(flag[:], flag_f[:]).then_inc(window_int, 1)
            dve.wait_ge(window_spread, 1)
            dve.tensor_scalar(wstart[:], bank[3][:, 0:CHUNKS], wcol[:, 0:1], None, ALU.add).then_inc(path_ready, 1)

            for f in range(FOLDS + 1):
                if f < FOLDS:
                    fs = slice(f * FOLD, (f + 1) * FOLD)
                    dve.wait_ge(y_in[f], FOLD * 16)
                    step(dve.tensor_tensor(x[:, fs, :], x[:, fs, :], yg[:, fs, :], ALU.add))
                    ln_stats(2, f)
                if f >= 1:
                    ln_apply(2, f - 1)
            dve.wait_ge(ln_tile, 3 * TILES)
            step(dve.tensor_tensor(x[:], x[:], xn[:, :, 0:D], ALU.add))
            dve.wait_ge(edge_w_in, 16 * 7)
            dve.tensor_copy(w3s[:], w3[:])
            step(dve.tensor_copy(b3s[:], b3[:]))
            mid, one = slice(STACK, 2 * STACK), slice(STACK, STACK + 1)
            dve.tensor_tensor(w3s[mid], w3[mid], w3s[mid].bitcast(F32), ALU.subtract)
            dve.tensor_tensor(b3s[one], b3[one], b3s[one].bitcast(F32), ALU.subtract).then_inc(stack_ready, 1)

            def same_node(c, b, loads):
                scol = src_col[:, bass.ds(c * GROUP, GROUP)]
                dve.wait_ge(srow_in[b], loads * 16)
                if warm(c, 2):
                    dve.wait_ge(sum_mm, (c - 1) * GROUP)
                dve.tensor_tensor(same[b][:], srow[b][:], scol.rearrange("p (g o) -> p g o", o=1).to_broadcast([P, GROUP, P]), ALU.is_equal).then_inc(same_ready, 1)
                dve.wait_ge(same_ready, c + 1)

            def earlier_edges(c, b):
                dve.wait_ge(same_ready, c + 1)
                dve.tensor_tensor(earlier[:], same[b][:], before[:].rearrange("p (o e) -> p o e", o=1).to_broadcast([P, GROUP, P]), ALU.mult).then_inc(edge_chain, 1)

            def count_earlier(c):
                dve.wait_ge(edge_chain, c * 3 + 1)
                dve.tensor_reduce(dup[:, 0, :], earlier[:], AX_X, ALU.add).then_inc(edge_chain, 1)

            def choose_rows(c):
                dve.wait_ge(edge_chain, c * 3 + 2)
                dve.scalar_tensor_tensor(dup[:, 1, :], dup[:, 0, :], 0.5, to_trash[:, bass.ds(c * GROUP, GROUP)], ALU.is_gt, ALU.mult).then_inc(edge_chain, 1)

            def scatter_rows(c, b):
                dve.wait_ge(edge_chain, c * 3 + 3)
                if warm(c, 2):
                    for t in range(GROUP):
                        dve.wait_ge(added[t], (c - 1) * 16)
                dve.tensor_tensor(sidx[b][:], dup[:, 1, :], src_f[:, bass.ds(c * GROUP, GROUP)], ALU.add).then_inc(sidx_ready, 1)

            def edge_chunk(c, b, n):
                same_node(c, b, n)
                earlier_edges(c, b)
                count_earlier(c)
                choose_rows(c)
                scatter_rows(c, b)
                for t in range(GROUP):
                    g = c * GROUP + t
                    q = (b + t) % 2
                    dve.wait_ge(e2_mm, g + 1)
                    dve.tensor_tensor(filt[q][:], bank[4 + q][0:P, 0:D], row["bf2"][0:P], ALU.add).then_inc(filt_ready, 1)
                    dve.wait_ge(filt_ready, g + 1)
                    dve.wait_ge(xg_in[b][t], n * 16)
                    if not isinstance(c, int) or g >= 2:
                        dve.wait_ge(sum_mm, g - 1)
                    dve.tensor_tensor(msg[q][:], filt[q][:], xg[b][:, t, :], ALU.mult).then_inc(msg_ready, 1)

            def inputs_low(c, b):
                low = slice(2 * STACK, KS)
                dve.wait_ge(att_high, c + 1)
                dve.tensor_tensor(att3s[b][low], att3[b][low], att3s[b][low].bitcast(F32), ALU.subtract).then_inc(att_low, 1)

            def one_hot(c, b, n):
                dve.wait_ge(srow_in[b], n * 48)
                if warm(c, 2):
                    dve.wait_ge(pair_mm, (c - 1) * GROUP)
                dve.tensor_scalar(hot[b][:], drow[b][:], wstart[:, bass.ds(c, 1)], None, ALU.is_equal).then_inc(hot_ready, 1)

            def window_hidden_low(c, b, a):
                lo, m = [v * P for v in THIRDS[a]]
                dve.wait_ge(hid_act, (c * NT + a + 1) * 2)
                dve.tensor_tensor(eh2[b][1][:, :, lo:lo + m], eh_full[:, :, lo:lo + m], eh2[b][0][:, :, lo:lo + m].bitcast(F32), ALU.subtract).then_inc(hid_low, 1)

            def window_message(c, t):
                dve.wait_ge(ends_copied, c * GROUP + t + 1)
                if warm(c, 1):
                    dve.wait_ge(sum_mm, (c - 1) * GROUP + t + 1)
                dve.tensor_tensor(msgs[:, t, :], bank[t][0:P, 0:D], ends_x[:, t, :], ALU.mult).then_inc(msg_ready, 1)

            def window_chunk(c, b, n, left):
                nxt = (c + 1, 1 - b)
                for t in range(GROUP):
                    window_message(c, t)
                    if t == 0:
                        window_hidden_low(c, b, 1)
                        if left:
                            one_hot(*nxt, next_n(b, n))
                    elif t == 1:
                        earlier_edges(c, b)
                    elif t == 2:
                        window_hidden_low(c, b, 2)
                        if left:
                            same_node(*nxt, 3 * next_n(b, n))
                    elif t == 3:
                        if left:
                            window_hidden_low(*nxt, 0)
                        count_earlier(c)
                    elif t == 4:
                        choose_rows(c)
                        if left == 2:
                            inputs_low(c + 2, b)
                        scatter_rows(c, b)

            def windows():
                for c in range(2):
                    inputs_low(c, c)
                one_hot(0, 0, 1)
                same_node(0, 0, 3)
                window_hidden_low(0, 0, 0)
                chunks(dve, window_chunk, 2)

            by_path(dve, windows, lambda: chunks(dve, lambda c, b, n, left: edge_chunk(c, b, n), 1))

            def stats_of(f):
                for a, (lo, hi) in enumerate(PIECES):
                    for o in range(KD):
                        dve.wait_ge(h_ready, f * 4 + a * 2 + o + 1)
                        ins = dve.bn_stats(cstat[:, o, 2 * f + a, :], xT[:, o, f * FOLD * P + lo:f * FOLD * P + hi])
                return ins

            for f in range(FOLDS):
                dve.wait_ge(part_in[f % 2], (f // 2 + 1) * GROUP * 16)
                p = part[f % 2]
                dve.tensor_tensor(p[1][:], p[1][:], p[2][:], ALU.add)
                step(dve.tensor_tensor(p[0][:], p[0][:], p[3][:], ALU.add))
                step(dve.tensor_tensor(p[1][:], p[1][:], p[4][:], ALU.add))
                dve.tensor_tensor(p[0][:], p[0][:], p[1][:], ALU.add).then_inc(agg_ready, 1)
                if f >= 2:
                    stats_of(f - 2)
            stats_of(FOLDS - 2)
            step(stats_of(FOLDS - 1))
            for k in range(KD):
                ins = dve.bn_aggr(cmv[:, k, :], cstat[:, k].rearrange("p a b -> p (a b)"))
            ins.then_inc(bn_var, 1)
            dve.wait_ge(bn_std, 1)
            step(dve.reciprocal(csc[:, 0, :], csc[:, 0, :]))
            step(dve.tensor_tensor(csc[:, 1, :], csc[:, 0, :], chan[:, CH_AT["gamma"]:CH_AT["gamma"] + KD], ALU.mult))
            step(dve.tensor_tensor(csc[:, 0, :], csc[:, 1, :], cmv[:, :, 0], ALU.mult))
            dve.tensor_tensor(csc[:, 2, :], chan[:, CH_AT["beta"]:CH_AT["beta"] + KD], csc[:, 0, :], ALU.subtract).then_inc(bn_scale, 1)

            def low_copies(f):
                for t in range(f * FOLD, (f + 1) * FOLD):
                    dve.wait_ge(turned_copied, 2 * TILES + t + 1)
                    ts = slice(t * P, (t + 1) * P)
                    dve.tensor_tensor(xTs[1][:, :, ts], bank[t % 2][:, 0:KD * P].rearrange("p (k e) -> p k e", k=KD), xTs[0][:, :, ts].bitcast(F32),
                                      ALU.subtract).then_inc(x_low, 1)

            for f in range(FOLDS + 1):
                if f < FOLDS:
                    for t in range(f * FOLD, (f + 1) * FOLD):
                        dve.wait_ge(bn_turned, t + 1)
                        dve.tensor_tensor(x[:, t, :], x[:, t, :], bank[6 + t % 2][0:P, 0:D], ALU.add).then_inc(x3_ready, 1)
                    dve.wait_ge(x3_ready, (f + 1) * FOLD)
                    ln_stats(3, f)
                    ln_apply(3, f)
                if f >= 1:
                    low_copies(f - 1)
            dve.wait_ge(mix_mm, TILES)
            lg, ex = sm8[:, 0], sm8[:, 1]
            step(dve.tensor_tensor(lg, g8, rowbc(row["br"][0:P]), ALU.add))
            step(dve.tensor_reduce(sm1[:, 0, :], lg, AX_X, ALU.max))
            dve.tensor_tensor(lg, lg, bc(sm1[:, 0, :], EXPERTS), ALU.subtract).then_inc(mix_shift, 1)
            dve.wait_ge(mix_exp, 1)
            step(dve.tensor_reduce(sm1[:, 1, :], ex, AX_X, ALU.add))
            step(dve.reciprocal(sm1[:, 1, :], sm1[:, 1, :]))
            dve.tensor_tensor(mix[:], ex, bc(sm1[:, 1, :], EXPERTS), ALU.mult).then_inc(mix_ready, 1)
            dve.wait_ge(mix_ready, 1)

            def dense_low(e, s, layer):
                at, n = STEPS[s]
                m = n * P
                done, low = ((d1_act, d1_low), (d2_act, d2_low))[layer]
                g = e * (NS * KD) + s * KD
                dst = (h1, h2)[layer][s % 2]
                for o in range(KD):
                    dve.wait_ge(done, (g + o + 1) * 2)
                    dve.tensor_tensor(dst[1][:, o, 0:m], h_full[layer][o][:, 0:m], dst[0][:, o, 0:m].bitcast(F32), ALU.subtract).then_inc(low, 1)

            def dense_add(e, b, s):
                at, n = STEPS[s]
                for t in range(at, at + n):
                    dve.wait_ge(d3_mm, e * TILES + t + 1)
                    if not isinstance(e, int) or e:
                        dve.wait_ge(d3_added, (e - 1) * TILES + t + 1)
                    dve.scalar_tensor_tensor(x[:, t, :], bank[4 + (b + t) % 2][0:P, 0:D], mix[:, t, bass.ds(e, 1)], x[:, t, :],
                                             ALU.mult, ALU.add).then_inc(d3_added, 1)

            def dense_expert(e, b):
                for s in range(NS + 2):
                    if s < NS:
                        dense_low(e, s, 0)
                    if 1 <= s <= NS:
                        dense_low(e, s - 1, 1)
                    if s >= 2:
                        dense_add(e, b, s - 2)

            dense_expert(0, 0)
            dve.wait_ge(d3_added, TILES)
            for t in range(TILES):
                dve.wait_ge(bo_mm, t + 1)
                dve.tensor_tensor(x[:, t, :], x[:, t, :], bank[7][0:P, 0:D], ALU.add).then_inc(bo_added, 1)
            dve.wait_ge(bo_added, TILES)
            dense_expert(1, 1)
            with dve.Fori(1, EXPERTS // 2) as i:
                for b in range(2):
                    dense_expert(i * 2 + b, b)


def _arrange(inputs):
    def get(name):
        return np.asarray(inputs[name])

    def halves(name):
        return get(name).reshape(KD, HALF).T

    def pairs(name):
        return get("L1_ffn_" + name).reshape(EXPERTS, KD, HALF).transpose(2, 0, 1).reshape(HALF, EXPERTS * KD)

    chan = [halves("L1_gnn_" + n) for n in CHAN] + [pairs(n) for n in PAIR]
    chan.append(get("L0_ffn_b1").reshape(EXPERTS, FC, HALF).transpose(2, 0, 1).reshape(HALF, EXPERTS * FC))
    rows = [get("L0_gnn_attn_l"), get("L0_gnn_attn_r"), get("L1_gnn_bf2"), get("L0_ffn_gate_b"), get("L1_ffn_br")]
    arrays = {
        "x": get("x"), "src": get("src"), "dst": get("dst"),
        "src_col": get("src").reshape(E_TILES, P).T, "dst_col": get("dst").reshape(E_TILES, P).T,
        "rbf_t": get("edge_attr_20").T,
        "chan": np.concatenate(chan, axis=1), "rows": np.concatenate([r.reshape(-1) for r in rows]), "b2": get("L0_ffn_b2").reshape(-1),
        "gnn_w": get("L0_gnn_weight"), "gate_w": get("L0_ffn_gate_w"), "w1": get("L0_ffn_w1"), "w2": get("L0_ffn_w2"),
        "wf1": get("L1_gnn_Wf1"), "wf2": get("L1_gnn_Wf2"), "wu1": get("L1_gnn_Wu1"), "wu2": get("L1_gnn_Wu2"),
        "wr": get("L1_ffn_Wr"), "dw1": get("L1_ffn_W1"), "dw2": get("L1_ffn_W2"), "dwo": get("L1_ffn_Wo"),
        "bo": get("L1_ffn_bo"), "bf1": get("L1_gnn_bf1").reshape(1, D), "bf2": get("L1_gnn_bf2").reshape(1, D),
    }
    return {f"in_{k}": np.ascontiguousarray(v) for k, v in arrays.items()}


def kernel(**inputs):
    import concourse.bacc as bacc
    from concourse.bass_utils import run_bass_kernel_spmd

    nc = bacc.Bacc("TRN2", target_bir_lowering=False, num_devices=1)
    arrays = _arrange(inputs)
    A = {k[3:]: nc.dram_tensor(k, v.shape, mybir.dt.from_np(v.dtype), kind="ExternalInput").ap() for k, v in arrays.items()}
    out = nc.dram_tensor("out_0", (N_NODES, D), F32, kind="ExternalOutput").ap()
    build(nc, A, out)
    r = run_bass_kernel_spmd(nc, [arrays], core_ids=[0])
    return r.results[0]["out_0"]
```

```python
from contextlib import ExitStack

import numpy as np

import concourse.bass as bass
from concourse import mybir

F32 = mybir.dt.float32
I32 = mybir.dt.int32
F32R = mybir.dt.float32r
ALU = mybir.AluOpType
ACT = mybir.ActivationFunctionType
AX_X = mybir.AxisListType.X

N_NODES, D = 3125, 256
P = 125
TILES = N_NODES // P
HALF = 128
KD = D // HALF
LN_EPS = 1e-5

HEADS, HEAD_D = 4, 64
TAB = D + 2 * HEADS
LEAK = 0.01

EXPERTS = 8
FF = 1024
FC = FF // HALF
CAP = 489
SLOTS = 512
CAP_EVEN = CAP + CAP % 2
ROW_TILES = SLOTS // HALF
LAST_ROWS = CAP - (ROW_TILES - 1) * HALF
DROPPED = 2 * EXPERTS * SLOTS
ROW = D + 2
Y_ROWS = N_NODES + 1
ZROWS = 4
FLT_MAX = 3.4028234663852886e38
BIG = 10000.0

N_EDGES = 53125
N_RBF = 20
E_TILES = N_EDGES // P
GROUP = 5
CHUNKS = E_TILES // GROUP
CE = GROUP * P
CUT = 3 * P
PIECES = ((0, CUT), (CUT, CE))
AGG_ROWS = N_NODES + P
BN_EPS = 1e-5
STACK = 32
KS = 2 * STACK + N_RBF
THIRDS = [(a, min(2, GROUP - a)) for a in range(0, GROUP, 2)]
NT = len(THIRDS)
FOLD = 5
FOLDS = TILES // FOLD

BN2_EPS = 1e-3
TOK = 4
STEPS = [(s, min(TOK, TILES - s)) for s in range(0, TILES, TOK)]

CHAN = ["bf1", "bu1", "bu2", "gamma", "beta"]
PAIR = ["b1", "g1", "be1", "m1", "v1", "b2", "g2", "be2", "m2", "v2"]
CH_AT = {n: KD * k for k, n in enumerate(CHAN)}
PAIR_AT = {n: KD * len(CHAN) + k * EXPERTS * KD for k, n in enumerate(PAIR)}
FFB1_AT = KD * len(CHAN) + len(PAIR) * EXPERTS * KD
N_CHAN = FFB1_AT + EXPERTS * FC
ROW_AT = {"attn_l": 0, "attn_r": D, "bf2": 2 * D, "gate_b": 3 * D, "br": 3 * D + EXPERTS}
N_ROW = 3 * D + 2 * EXPERTS
PASSES = ((0, 0), (0, 1), (1, 0))


class Tally:

    def __init__(self, sem):
        self.sem, self.n = sem, 0

    def inc(self, instruction, by=1):
        self.n += by
        instruction.then_inc(self.sem, by)
        return self.n


def build(nc, A, out):
    with ExitStack() as ctx:
        def sb(name, shape, dt=F32):
            return ctx.enter_context(nc.sbuf_tensor(name, shape, dt))

        def sem(name):
            return ctx.enter_context(nc.semaphore(name))

        def dram(name, shape):
            return nc.dram_tensor(name, shape, F32).ap()

        psum = ctx.enter_context(nc.psum_tensor("psum", [128, 8, 512], F32))
        bank = [psum[:, i, :] for i in range(8)]

        tab_d = dram("tab_d", [N_NODES, TAB])
        al_d = dram("al_d", [N_NODES, HEADS])
        buf_d = dram("buf_d", [EXPERTS * SLOTS, ROW])
        y_d = dram("y_d", [Y_ROWS, D])
        xn_d = dram("xn_d", [N_NODES, D])
        agg_d = [dram(f"agg{i}_d", [AGG_ROWS, D]) for i in range(GROUP)]

        x = sb("x_sb", [P, TILES, D])
        chan = sb("chan_sb", [HALF, N_CHAN])
        rows = sb("rows_sb", [HALF, N_ROW])
        ident = sb("ident", [128, 128])
        ones = sb("ones", [128, 128])
        before = sb("before", [P, P])
        upper = sb("upper", [P, P])
        trash = sb("trash", [P, 1])
        rev = sb("rev", [P, EXPERTS])
        eno = sb("eno", [P, EXPERTS])
        stats = sb("stats", [P, TILES, 6])
        mv = sb("mv", [P, TILES, 2])
        rstd = sb("rstd", [P, TILES])
        eps1 = sb("eps1", [128, 3])
        sm8 = sb("sm8", [P, 6, TILES, EXPERTS])
        sm1 = sb("sm1", [P, 10, TILES])
        tot8 = sb("tot8", [P, EXPERTS])
        off8 = sb("off8", [P, EXPERTS])
        slot_i = sb("slot_i", [P, TILES], I32)
        e0src = sb("e0src", [P, TILES], I32)
        e0dst = sb("e0dst", [P, TILES], I32)
        wf1 = sb("wf1", [N_RBF, D])
        wf2 = sb("wf2", [HALF, KD, D])
        wu1 = sb("wu1", [HALF, KD, D])
        wu2 = sb("wu2", [HALF, KD, D])
        waug = sb("waug", [HALF, KD, TAB])
        wprod = sb("wprod", [HALF, KD * HEADS, HEAD_D])
        gate_w = sb("gate_w_sb", [HALF, KD, EXPERTS])
        wr = sb("wr_sb", [HALF, KD, EXPERTS])
        bo = sb("bo_sb", [EXPERTS, D])
        mix = sb("mix", [P, TILES, EXPERTS])
        scl = sb("scl", [HALF, 2, EXPERTS * KD])
        shf = sb("shf", [HALF, 2, EXPERTS * KD])
        cstat = sb("cstat", [HALF, KD, 2 * FOLDS, 6])
        cmv = sb("cmv", [HALF, KD, 2])
        csc = sb("csc", [HALF, 3, KD])

        dup = sb("dup", [P, 2, GROUP])
        wcol = sb("wcol", [128, 1])
        row_gate = [sb(f"row_gate{b}", [128, ROW_TILES, 2]) for b in range(2)]
        far = sb("far", [128, ROW_TILES])
        y_row = [sb(f"y_row{b}", [128, ROW_TILES], I32) for b in range(2)]
        flag = sb("flag", [1, 1], I32)
        flag_f = sb("flag_f", [1, 1])
        sidx = [sb(f"sidx{b}", [P, GROUP], I32) for b in range(2)]
        gidx = [sb(f"gidx{b}", [P, GROUP], I32) for b in range(2)]
        wrs = sb("wrs", [HALF, KD, 2 * EXPERTS], F32R)
        add_halves = sb("add_halves", [2 * EXPERTS, EXPERTS])

        base = -(-nc.sbuf_base // 32) * 32 + 96

        def place(name, at, shape, dt=F32):
            return nc.alloc_sbuf_tensor_at(name, shape, dt, offset=base + 4 * at)

        xn = place("xn", -24, [P, TILES, ROW])
        xT = place("xT", 6432, [HALF, KD, N_NODES])
        tab = place("tab", 12688, [P, TILES, TAB])
        tdst = place("tdst", 19288, [P, TILES, TAB])
        tsrc = place("tsrc", 25888, [P, TILES, HEADS])
        zeros = place("zeros", 38304, [128, ZROWS * ROW])
        b2 = place("b2_rows", 6432, [128, EXPERTS * D])
        yrow = [place(f"yrow{b}", 8480 + b * 1024, [128, ROW_TILES, D]) for b in range(2)]
        ytmp = [[place(f"ytmp{a}{b}", 10528 + (a * 2 + b) * D, [128, D]) for b in range(2)] for a in range(3)]
        hid = [place(f"hid{h}", 12688 + h * 4096, [128, FC, SLOTS], F32R) for h in range(2)]
        act_full = [place(f"act_full{b}", 20880 + b * SLOTS, [128, SLOTS]) for b in range(2)]
        bT = [place(f"bT{h}", 21904 + h * 1024, [128, KD, SLOTS], F32R) for h in range(2)]
        brow = [place(f"brow{b}", 23952 + b * 1032, [128, ROW_TILES, ROW]) for b in range(2)]
        w1 = [place(f"w1_{h}", 26016 + h * 2048, [128, KD, FF], F32R) for h in range(2)]
        w2 = [place(f"w2_{h}", 30112 + h * 2048, [128, FC, D], F32R) for h in range(2)]
        w1_full = place("w1_full", 34208, [128, KD, FF])
        w2_full = place("w2_full", 36256, [128, FC, D])
        yg = place("yg", 12688, [P, TILES, D])
        E0 = 12688
        CW = 632
        srow = [place(f"srow{b}", E0 + b * CW, [P, GROUP, P], I32) for b in range(2)]
        attr = [place(f"attr{b}", E0 + 2 * CW + b * CW, [N_RBF, CE]) for b in range(2)]
        same = [place(f"same{b}", E0 + 4 * CW + b * CW, [P, GROUP, P]) for b in range(2)]
        earlier = place("earlier", E0 + 6 * CW, [P, GROUP, P])
        eh = [place(f"eh{b}", E0 + 7 * CW + b * KD * CW, [128, KD, CE]) for b in range(2)]
        xg = [place(f"xg{b}", E0 + 11 * CW + b * GROUP * D, [P, GROUP, D]) for b in range(2)]
        filt = [place(f"filt{b}", E0 + 11 * CW + 2 * GROUP * D + b * D, [P, D]) for b in range(2)]
        msg = [place(f"msg{b}", E0 + 11 * CW + 2 * (GROUP + 1) * D + b * D, [P, D]) for b in range(2)]
        summed = [place(f"summed{b}", E0 + 11 * CW + 2 * (GROUP + 2) * D + b * GROUP * D, [P, GROUP, D]) for b in range(2)]
        src_col = place("src_col_sb", 34208, [P, E_TILES], I32)
        dst_col = place("dst_col_sb", 34640, [P, E_TILES], I32)
        src_f = place("src_f", 30848, [P, E_TILES])
        to_trash = place("to_trash", 31280, [P, E_TILES])
        dst_f = place("dst_f", 19096, [P, E_TILES])
        ends = place("ends", 19528, [P, 2, CHUNKS])
        span = place("span", 19704, [CHUNKS, 4])
        window_f = place("window_f", 19712, [1, 2 * CHUNKS])
        window = place("window", 31712, [1, CHUNKS], I32)
        wstart = place("wstart", 31800, [128, CHUNKS])
        w3 = place("w3", 31888, [KS, D])
        w3s = place("w3s", 32144, [KS, D], F32R)
        b3 = place("b3", 32400, [STACK + 1, D])
        b3s = place("b3s", 32656, [STACK + 1, D], F32R)
        wf2s = place("wf2s", 32912, [HALF, 2, KD, D], F32R)
        one_row = place("one_row", 33936, [STACK + 1, 128], F32R)
        eh_full = place("eh_full", E0 + 7 * CW, [128, KD, CE])
        eh2 = [[place(f"eh2_{b}{h}", 6432 + (2 * b + h) * KD * CW, [128, KD, CE], F32R) for h in range(2)] for b in range(2)]
        xw = [place(f"xw{b}", E0 + 11 * CW + b * D, [HALF, D]) for b in range(2)]
        xws = [place(f"xws{b}", E0 + 11 * CW + 2 * D + b * 2 * D, [HALF, 2, D], F32R) for b in range(2)]
        msgs = place("msgs", E0 + 11 * CW + 6 * D, [P, GROUP, D])
        ends_x = place("ends_x", 35080, [P, GROUP, D])
        drow = [place(f"drow{b}", 25792 + b * CW, [HALF, CE], I32) for b in range(2)]
        hot = [place(f"hot{b}", 25792 + (2 + b) * CW, [HALF, CE], F32R) for b in range(2)]
        att3 = [place(f"att3_{b}", 25792 + (4 + b) * CW, [KS, CE]) for b in range(2)]
        att3s = [place(f"att3s_{b}", 25792 + (6 + b) * CW, [KS, CE], F32R) for b in range(2)]
        part = [[place(f"part{b}_{i}", 12688 + (b * GROUP + i) * FOLD * D, [P, FOLD, D]) for i in range(GROUP)] for b in range(2)]
        aggT = [place(f"aggT{b}", 25488 + b * KD * CW, [128, KD, CE]) for b in range(2)]
        uT = [place(f"uT{b}", 28016 + b * KD * CW, [128, KD, CE]) for b in range(2)]
        raw = [place(f"raw{b}", 29208 + b * 504, [2 * EXPERTS, TOK * P]) for b in range(2)]
        mixT = place("mixT", 0, [EXPERTS, N_NODES])
        h1 = [[place(f"h1_{b}{h}", 6432 + (2 * b + h) * KD * TOK * P, [128, KD, TOK * P], F32R) for h in range(2)] for b in range(2)]
        h_full = [[place(f"h_full{j}{b}", 10432 + (2 * j + b) * 504, [128, TOK * P]) for b in range(2)] for j in range(2)]
        xTs = [place(f"xTs{h}", 12688 + h * 6256, [128, KD, N_NODES], F32R) for h in range(2)]
        h2 = [[place(f"h2_{b}{h}", 25200 + (2 * b + h) * KD * TOK * P, [128, KD, TOK * P], F32R) for h in range(2)] for b in range(2)]
        dw = [[place(f"dw{b}{h}", 30720 + (2 * b + h) * 3 * KD * D, [128, 3 * KD, D], F32R) for h in range(2)] for b in range(2)]
        dw_full = place("dw_full", 36864, [128, 3 * KD, D])

        row = {k: rows[:, v:v + (EXPERTS if k in ("gate_b", "br") else D)]
               for k, v in ROW_AT.items()}

        consts_ready = sem("consts_ready")
        x_in = [sem(f"x_in{f}") for f in range(FOLDS)]
        idx_in = sem("idx_in")
        vec_in = sem("vec_in")
        gnn_w_in = sem("gnn_w_in")
        small_w_in = sem("small_w_in")
        buf_zeroed = sem("buf_zeroed")
        agg_zeroed = sem("agg_zeroed")
        col_in = sem("col_in")
        node_w_in = sem("node_w_in")
        wr_halved = sem("wr_halved")
        dve_chain = sem("dve_chain")
        waug_ready = sem("waug_ready")
        ln_var = sem("ln_var")
        ln_std = sem("ln_std")
        ln_tile = sem("ln_tile")
        turned = sem("turned")
        turned_copied = sem("turned_copied")
        tab_mm = sem("tab_mm")
        tab_copied = sem("tab_copied")
        tab_stored = sem("tab_stored")
        att_in = [sem(f"att_in{f}") for f in range(FOLDS)]
        att_shift = sem("att_shift")
        att_exp = sem("att_exp")
        gate_mm = sem("gate_mm")
        gate_shift = sem("gate_shift")
        gate_exp = sem("gate_exp")
        count_ready = sem("count_ready")
        count_mm = sem("count_mm")
        slots_ready = sem("slots_ready")
        scattered = sem("scattered")
        brow_in = [sem(f"brow_in{b}") for b in range(2)]
        w1_in = sem("w1_in")
        w2_in = sem("w2_in")
        w_high = sem("w_high")
        w_low = sem("w_low")
        b2_in = sem("b2_in")
        b_turned = sem("b_turned")
        gates_taken = sem("gates_taken")
        b_high = sem("b_high")
        b_low = sem("b_low")
        ff1_mm = sem("ff1_mm")
        ff1_act = sem("ff1_act")
        ff1_low = sem("ff1_low")
        ff2_mm = sem("ff2_mm")
        ff2_bias = sem("ff2_bias")
        y_stored = [sem(f"y_stored{b}") for b in range(2)]
        y_chain = sem("y_chain")
        y_ready = sem("y_ready")
        y_in = x_in
        y_added = sem("y_added")
        xn_stored = sem("xn_stored")
        srow_in = [sem(f"srow_in{b}") for b in range(2)]
        attr_in = [sem(f"attr_in{b}") for b in range(2)]
        same_ready = sem("same_ready")
        sidx_ready = sem("sidx_ready")
        gidx_ready = sem("gidx_ready")
        filt_ready = sem("filt_ready")
        msg_ready = sem("msg_ready")
        sum_mm = sem("sum_mm")
        sum_copied = sem("sum_copied")
        xg_in = [[sem(f"xg_in{b}_{t}") for t in range(GROUP)] for b in range(2)]
        added = [sem(f"added{t}") for t in range(GROUP)]
        edge_chain = sem("edge_chain")
        edge_set = sem("edge_set")
        edge_w_in = sem("edge_w_in")
        edge_w_ready = sem("edge_w_ready")
        stack_ready = sem("stack_ready")
        ends_ready = sem("ends_ready")
        ends_turned = sem("ends_turned")
        window_ready = sem("window_ready")
        window_turned = sem("window_turned")
        window_int = sem("window_int")
        window_spread = sem("window_spread")
        path_ready = sem("path_ready")
        att_high = sem("att_high")
        att_low = sem("att_low")
        xw_high = sem("xw_high")
        xw_low = sem("xw_low")
        hot_ready = sem("hot_ready")
        hid_mm = sem("hid_mm")
        hid_act = sem("hid_act")
        hid_low = sem("hid_low")
        pair_mm = sem("pair_mm")
        ends_copied = sem("ends_copied")
        x_residual = sem("x_residual")
        part_in = [sem(f"part_in{b}") for b in range(2)]
        agg_ready = sem("agg_ready")
        agg_turned = sem("agg_turned")
        agg_copied = sem("agg_copied")
        u_mm = sem("u_mm")
        u_silu = sem("u_silu")
        h_mm = sem("h_mm")
        h_ready = sem("h_ready")
        bn_var = sem("bn_var")
        bn_std = sem("bn_std")
        bn_scale = sem("bn_scale")
        bn_applied = sem("bn_applied")
        bn_turned = sem("bn_turned")
        x3_ready = sem("x3_ready")
        x_low = sem("x_low")
        raw_mm = sem("raw_mm")
        raw_copied = sem("raw_copied")
        mix_mm = sem("mix_mm")
        mix_shift = sem("mix_shift")
        mix_exp = sem("mix_exp")
        mix_ready = sem("mix_ready")
        mix_turned = sem("mix_turned")
        mixT_ready = sem("mixT_ready")
        bo_mm = sem("bo_mm")
        bo_added = sem("bo_added")
        aff_std = sem("aff_std")
        aff_ready = sem("aff_ready")
        dw_in = sem("dw_in")
        dw_halved = sem("dw_halved")
        d1_mm = sem("d1_mm")
        d1_act = sem("d1_act")
        d1_low = sem("d1_low")
        d2_mm = sem("d2_mm")
        d2_act = sem("d2_act")
        d2_low = sem("d2_low")
        d3_mm = sem("d3_mm")
        d3_added = sem("d3_added")
        stored = sem("stored")
        sp_passed = sem("sp_passed")
        pool_passed = sem("pool_passed")
        act_passed = sem("act_passed")

        block = ctx.enter_context(nc.Block())

        def waits(eng, passed, *needs):
            for s, v in needs:
                eng.wait_ge(s, v)
            eng.sem_inc(passed, 1)

        def by_path(eng, windows, gathers):
            eng.wait_ge(path_ready, 1)
            all_in = eng.value_load(flag[0:1, 0:1], min_val=0, max_val=1)
            with eng.If(all_in == 1):
                windows()
            with eng.If(all_in == 0):
                gathers()

        def chunks(eng, chunk, ahead):
            chunk(0, 0, 1, 2)
            chunk(1, 1, 1, 2)
            pairs = (CHUNKS - ahead) // 2
            with eng.Fori(1, pairs) as i:
                for b in range(2):
                    chunk(i * 2 + b, b, i + 1, 2)
            for c in range(2 * pairs, CHUNKS):
                chunk(c, c % 2, c // 2 + 1, min(2, CHUNKS - 1 - c))

        def warm(c, n):
            return not isinstance(c, int) or c >= n

        def tiles_behind(c, b, t, n):
            if t >= n:
                return c, b, t - n
            return (c - 1, 1 - b, t - n + GROUP) if warm(c, 1) else None

        def pair_bank(b, t):
            return bank[(0, 1, 2, 0, 1, 2, 0, 1, 2, 3)[b * GROUP + t]]

        def next_n(b, n):
            return n + b

        def experts(eng, expert):
            expert(0, 0, 1)
            expert(1, 1, 1)
            with eng.Fori(1, EXPERTS // 2 - 1) as i:
                for b in range(2):
                    expert(i * 2 + b, b, i + 1)
            expert(EXPERTS - 2, 0, EXPERTS // 2)
            expert(EXPERTS - 1, 1, EXPERTS // 2, last=True)

        def last_bank(e, b, t):
            return bank[4 + (t % 4 if warm(e, 1) else t % 2)]

        def last_bank_free(e, t):
            if not warm(e, 1):
                return t - 1 if t >= 2 else None
            return 1 if t == 3 else max(t - 3, 0)

        def step_behind(e, b, s, n):
            if s >= n:
                return e, b, s - n
            return (e - 1, 1 - b, s - n + NS) if warm(e, 1) else None

        def dense_steps(eng, stages, extra=None):
            def expert(e, b):
                for s in range(NS):
                    for stage, n in stages:
                        at = step_behind(e, b, s, n)
                        if at:
                            stage(*at)
                    if extra and isinstance(e, int) and e == 0:
                        extra(s)

            expert(0, 0)
            expert(1, 1)
            with eng.Fori(1, EXPERTS // 2) as i:
                for b in range(2):
                    expert(i * 2 + b, b)
            for s in range(max(n for _, n in stages)):
                for stage, n in stages:
                    if s < n:
                        stage(EXPERTS - 1, 1, NS + s - n)

        turn_banks = ((0, 1, 6, 7), (0, 1, 2, 3), (0, 1, 2))

        def turn_bank(k, t):
            banks = turn_banks[k]
            return bank[banks[t % len(banks)]]

        NS = len(STEPS)
        N_BUF_ZERO = EXPERTS * SLOTS // (128 * ZROWS)
        N_Y_ZERO = -(-Y_ROWS // (128 * ZROWS))
        N_ZERO = GROUP * -(-AGG_ROWS // (128 * ZROWS))

        def three_passes(pe, dst, lhs, rhs, first=True, last=True):
            n = len(lhs) * len(PASSES)
            at = 0
            for l, r in zip(lhs, rhs):
                for i, j in PASSES:
                    ins = pe.matmul(dst, l[i], r[j], start=first and at == 0, stop=last and at == n - 1)
                    at += 1
            return ins

        @block.sync
        def _(sp):
            xv = A["x"].rearrange("(p t) d -> p t d", t=TILES)
            for f in range(FOLDS):
                sp.dma_start(x[:, f * FOLD:(f + 1) * FOLD, :], xv[:, f * FOLD:(f + 1) * FOLD, :]).then_inc(x_in[f], 16)
                if f == 0:
                    sp.dma_start(rows[:], A["rows"].partition_broadcast(HALF)).then_inc(vec_in, 16)
                    sp.dma_start(waug[:, :, 0:D], A["gnn_w"].rearrange("(k p) d -> p k d", p=HALF)).then_inc(gnn_w_in, 16)
                    sp.dma_start(e0src[:], A["src"][0:N_NODES].rearrange("(p t) -> p t", t=TILES)).then_inc(idx_in, 16)
                    sp.dma_start(e0dst[:], A["dst"][0:N_NODES].rearrange("(p t) -> p t", t=TILES)).then_inc(idx_in, 16)
            sp.dma_start(chan[:], A["chan"]).then_inc(vec_in, 16)
            for w, name in ((gate_w, "gate_w"), (wr, "wr")):
                sp.dma_start(w[:], A[name].rearrange("(k p) e -> p k e", p=HALF)).then_inc(small_w_in, 16)

            def expert_loads(e, warm):
                if warm:
                    waits(sp, sp_passed, (w_low, e * 2 - 1))
                sp.dma_start(w1_full[:], A["w1"][bass.ds(e, 1)].rearrange("o (k p) f -> p (o k) f", p=HALF)).then_inc(w1_in, 16)
                if warm:
                    waits(sp, sp_passed, (w_low, e * 2))
                sp.dma_start(w2_full[:], A["w2"][bass.ds(e, 1)].rearrange("o (k p) f -> p (o k) f", p=HALF)).then_inc(w2_in, 16)

            tv = tab_d.rearrange("(p t) c -> p t c", t=TILES)
            av = al_d.rearrange("(p t) c -> p t c", t=TILES)
            for f in range(FOLDS):
                fs = slice(f * FOLD, (f + 1) * FOLD)
                sp.wait_ge(tab_copied, (f + 1) * FOLD)
                sp.dma_start(tv[:, fs, :], tab[:, fs, :]).then_inc(tab_stored, 16)
                sp.dma_start(av[:, fs, :], tab[:, fs, D:D + HEADS]).then_inc(tab_stored, 16)

            sp.wait_ge(att_in[FOLDS - 2], 2 * FOLD * 16)
            sp.wait_ge(consts_ready, 1)
            step = 128 * ZROWS
            for q in range(0, EXPERTS * SLOTS, step):
                sp.dma_start(buf_d[q:q + step, :].rearrange("(p r) d -> p (r d)", p=128), zeros[:]).then_inc(buf_zeroed, 16)

            expert_loads(0, False)

            def zero_aggregates(which):
                for i in which:
                    for lo in range(0, AGG_ROWS, step):
                        n = min(step, AGG_ROWS - lo)
                        r = ZROWS if n == step else 2
                        sp.dma_start(agg_d[i][lo:lo + n, :].rearrange("(p r) d -> p (r d)", r=r), zeros[0:n // r, 0:r * D]).then_inc(agg_zeroed, 16)

            sp.dma_start(bo[:], A["bo"]).then_inc(node_w_in, 16)
            sp.dma_start(wf1[:], A["wf1"]).then_inc(node_w_in, 16)
            for w, name in ((wf2, "wf2"), (wu1, "wu1"), (wu2, "wu2")):
                sp.dma_start(w[:], A[name].rearrange("(k p) d -> p k d", p=HALF)).then_inc(node_w_in, 16)

            def expert_rows(e, b, warm):
                if warm:
                    waits(sp, sp_passed, (gates_taken, e - 1))
                sp.dma_start(brow[b][:], buf_d[bass.ds(e * SLOTS, SLOTS), :].rearrange("(j p) d -> p j d", p=128)).then_inc(brow_in[b], 16)

            sp.wait_ge(gate_mm, TILES)
            sp.dma_start(b2[:], A["b2"].partition_broadcast(HALF)).then_inc(b2_in, 16)
            sp.wait_ge(scattered, 16 * TILES)
            for b in range(2):
                expert_rows(b, b, False)
            expert_loads(1, True)
            for lo in range(0, Y_ROWS, step):
                n = min(step, Y_ROWS - lo)
                r = ZROWS if n == step else 2
                sp.dma_start(y_d[lo:lo + n, :].rearrange("(p r) d -> p (r d)", r=r), zeros[0:n // r, 0:r * D]).then_inc(buf_zeroed, 16)
            zero_aggregates(range(2))
            with sp.Fori(0, EXPERTS // 2 - 1) as i:
                for b in range(2):
                    expert_rows(i * 2 + 2 + b, b, True)
                    expert_loads(i * 2 + 2 + b, True)
            zero_aggregates(range(2, GROUP))
            sp.wait_ge(w_low, EXPERTS * 2)
            sp.dma_start(src_col[:], A["src_col"]).then_inc(col_in, 16)
            sp.dma_start(dst_col[:], A["dst_col"]).then_inc(col_in, 16)
            for b in range(2):
                sp.wait_ge(y_stored[b], EXPERTS // 2 * ROW_TILES * 16)
            yv = y_d[1:Y_ROWS, :].rearrange("(p t) d -> p t d", t=TILES)
            for f in range(FOLDS):
                fs = slice(f * FOLD, (f + 1) * FOLD)
                sp.dma_start(yg[:, fs, :], yv[:, fs, :]).then_inc(y_in[f], 16)

            sp.wait_ge(edge_set, 4)
            for q in range(3):
                sp.dma_start(w3[q * STACK:q * STACK + N_RBF, :], A["wf1"]).then_inc(edge_w_in, 16)
            for q in range(2):
                sp.dma_start(w3[q * STACK + N_RBF:q * STACK + N_RBF + 1, :], A["bf1"]).then_inc(edge_w_in, 16)
                sp.dma_start(b3[q * STACK:q * STACK + 1, :], A["bf2"]).then_inc(edge_w_in, 16)

            def store_nodes():
                nv = xn_d.rearrange("(p t) d -> p t d", t=TILES)
                for f in range(FOLDS):
                    fs = slice(f * FOLD, (f + 1) * FOLD)
                    sp.wait_ge(ln_tile, 2 * TILES + (f + 1) * FOLD)
                    sp.dma_start(nv[:, fs, :], xn[:, fs, 0:D]).then_inc(xn_stored, 16)

            def window_inputs(c, b):
                if warm(c, 2):
                    waits(sp, sp_passed, (att_low, c - 1))
                for q in range(3):
                    sp.dma_start(att3[b][q * STACK:q * STACK + N_RBF, :], A["rbf_t"][:, bass.ds(c * CE, CE)]).then_inc(attr_in[b], 16)

            def window_ends_of_edges(c, b):
                if warm(c, 2):
                    waits(sp, sp_passed, (same_ready, c - 1))
                    waits(sp, sp_passed, (hot_ready, c - 1))
                at = c * CE
                sp.dma_start(drow[b][:], A["dst"][bass.ds(at, CE)].partition_broadcast(HALF)).then_inc(srow_in[b], 16)
                sp.dma_start(srow[b][:].rearrange("p g e -> p (g e)"), A["src"][bass.ds(at, CE)].partition_broadcast(P)).then_inc(srow_in[b], 16)

            def window_nodes(c, b):
                start = sp.value_load(window[0:1, bass.ds(c, 1)], min_val=0, max_val=N_NODES - HALF)
                if warm(c, 2):
                    waits(sp, sp_passed, (xw_low, c - 1))
                sp.dma_start(xw[b][:], xn_d[bass.ds(start, HALF), :]).then_inc(srow_in[b], 16)

            def window_loads(c, b):
                window_inputs(c, b)
                window_ends_of_edges(c, b)
                window_nodes(c, b)

            def windows():
                for c in range(2):
                    window_inputs(c, c)
                sp.wait_ge(y_added, FOLDS)
                for c in range(2):
                    window_ends_of_edges(c, c)
                store_nodes()
                sp.wait_ge(xn_stored, 16 * FOLDS)
                for c in range(2):
                    window_nodes(c, c)
                with sp.Fori(1, CHUNKS // 2) as i:
                    for b in range(2):
                        window_loads(i * 2 + b, b)
                window_loads(CHUNKS - 1, 0)

            def edge_loads(c, b, warm):
                if warm:
                    waits(sp, sp_passed, (same_ready, c - 1))
                    waits(sp, sp_passed, (hid_mm, 4 * (c - 1)))
                sp.dma_start(srow[b][:].rearrange("p g e -> p (g e)"),
                             A["src"][bass.ds(c * CE, CE)].partition_broadcast(P)).then_inc(srow_in[b], 16)
                sp.dma_start(attr[b][:], A["rbf_t"][:, bass.ds(c * CE, CE)]).then_inc(attr_in[b], 16)

            def gathers():
                store_nodes()
                chunks(sp, lambda c, b, n, left: edge_loads(c, b, warm(c, 2)), 1)

            by_path(sp, windows, gathers)

            def dense_loads(e, warm):
                if warm:
                    waits(sp, sp_passed, (dw_halved, e * 2))
                for j, name in enumerate(("dw1", "dw2", "dwo")):
                    sp.dma_start(dw_full[:, j * KD:(j + 1) * KD, :],
                                 A[name][bass.ds(e, 1)].rearrange("o (k p) d -> p (o k) d", p=HALF)).then_inc(dw_in, 16)

            dense_loads(0, False)

            for i in range(GROUP):
                sp.wait_ge(added[i], 16 * CHUNKS)
            for f in range(FOLDS):
                if f >= 2:
                    sp.wait_ge(agg_turned, (f - 1) * FOLD)
                for i in range(GROUP):
                    src = agg_d[i][0:N_NODES, :].rearrange("(p t) d -> p t d", t=TILES)
                    sp.dma_start(part[f % 2][i][:], src[:, f * FOLD:(f + 1) * FOLD, :]).then_inc(part_in[f % 2], 16)

            with sp.Fori(1, EXPERTS) as e:
                dense_loads(e, True)

            ov = out.rearrange("(p t) d -> p t d", t=TILES)
            for f in range(FOLDS):
                fs = slice(f * FOLD, (f + 1) * FOLD)
                sp.wait_ge(d3_added, (EXPERTS - 1) * TILES + (f + 1) * FOLD)
                sp.dma_start(ov[:, fs, :], x[:, fs, :]).then_inc(stored, 16)
            sp.wait_ge(stored, 16 * FOLDS)

        @block.gpsimd
        def _(pool):
            made = Tally(sem("pool_made"))
            pool.memset(zeros[:], 0.0).then_inc(consts_ready, 1)
            made.inc(pool.memset(ident[:], 0.0))
            made.inc(pool.memset(ones[:], 1.0))
            made.inc(pool.memset(before[:], 1.0))
            made.inc(pool.memset(upper[:], 1.0))
            made.inc(pool.memset(eps1[:, 0:1], LN_EPS))
            made.inc(pool.memset(eps1[:, 1:2], BN2_EPS))
            made.inc(pool.memset(eps1[:, 2:3], 0.0))
            pool.wait_ge(made.sem, made.n)
            pool.affine_select(out=ident[:], in_=ident[:], compare_op=ALU.not_equal, fill=1.0, base=0,
                               pattern=[[-1, 128]], channel_multiplier=1).then_inc(consts_ready, 1)
            pool.affine_select(out=before[:], in_=before[:], compare_op=ALU.is_gt, fill=0.0, base=0,
                               pattern=[[-1, P]], channel_multiplier=1).then_inc(consts_ready, 1)
            pool.affine_select(out=upper[:], in_=upper[:], compare_op=ALU.is_gt, fill=0.0, base=0,
                               pattern=[[1, P]], channel_multiplier=-1).then_inc(consts_ready, 1)
            pool.iota(trash[:], pattern=[[0, 1]], base=N_NODES, channel_multiplier=1,
                      allow_small_or_imprecise_dtypes=True).then_inc(consts_ready, 1)
            pool.iota(xn[:, :, D + 1], pattern=[[1, TILES]], base=1, channel_multiplier=TILES,
                      allow_small_or_imprecise_dtypes=True).then_inc(consts_ready, 1)
            pool.iota(wcol[:], pattern=[[0, 1]], base=0, channel_multiplier=1,
                      allow_small_or_imprecise_dtypes=True).then_inc(consts_ready, 1)
            pool.iota(rev[:], pattern=[[-1, EXPERTS]], base=EXPERTS, channel_multiplier=0,
                      allow_small_or_imprecise_dtypes=True).then_inc(consts_ready, 1)
            pool.iota(eno[:], pattern=[[1, EXPERTS]], base=0, channel_multiplier=0,
                      allow_small_or_imprecise_dtypes=True).then_inc(consts_ready, 1)

            def low_weights(e):
                waits(pool, pool_passed, (w_high, e * 2 + 1))
                pool.tensor_tensor(w1[1][:], w1_full[:], w1[0][:].bitcast(F32), ALU.subtract).then_inc(w_low, 1)
                waits(pool, pool_passed, (w_high, e * 2 + 2))
                pool.tensor_tensor(w2[1][:], w2_full[:], w2[0][:].bitcast(F32), ALU.subtract).then_inc(w_low, 1)

            pool.wait_ge(idx_in, 32)
            pool.wait_ge(tab_stored, 32 * FOLDS)
            for t in range(TILES):
                pool.indirect_dma_start(tdst[:, t, :], None, tab_d, bass.IndirectOffsetOnAxis(ap=e0dst[:, t:t + 1], axis=0)).then_inc(att_in[t // FOLD], 16)
                pool.indirect_dma_start(tsrc[:, t, :], None, al_d, bass.IndirectOffsetOnAxis(ap=e0src[:, t:t + 1], axis=0)).then_inc(att_in[t // FOLD], 16)

            pool.wait_ge(buf_zeroed, 16 * N_BUF_ZERO)
            pool.wait_ge(slots_ready, 1)
            for t in range(TILES):
                pool.indirect_dma_start(buf_d, bass.IndirectOffsetOnAxis(ap=slot_i[:, t:t + 1], axis=0), xn[:, t, :], None,
                                        bounds_check=EXPERTS * SLOTS - 1, oob_is_err=False).then_inc(scattered, 16)
            def scatter_rows(e, b):
                for j in range(ROW_TILES):
                    m = HALF if j < ROW_TILES - 1 else LAST_ROWS
                    waits(pool, pool_passed, (y_ready, e * 2 + j // 2 + 1))
                    pool.indirect_dma_start(y_d, bass.IndirectOffsetOnAxis(ap=y_row[b][0:m, j:j + 1], axis=0), yrow[b][0:m, j, :], None,
                                            bounds_check=N_NODES, oob_is_err=False).then_inc(y_stored[b], 16)

            low_weights(0)
            low_weights(1)
            pool.wait_ge(buf_zeroed, 16 * (N_BUF_ZERO + N_Y_ZERO))
            scatter_rows(0, 0)
            with pool.Fori(1, EXPERTS // 2) as i:
                for b in range(2):
                    low_weights(i * 2 + b)
                    scatter_rows(i * 2 + b - 1, 1 - b)
            scatter_rows(EXPERTS - 1, 1)
            for b in range(2):
                pool.memset(att3[b][:], 1.0).then_inc(edge_set, 1)
            pool.memset(w3[:], 0.0).then_inc(edge_set, 1)
            pool.memset(b3[:], 0.0).then_inc(edge_set, 1)

            for f in range(FOLDS):
                fs = slice(f * FOLD, (f + 1) * FOLD)
                pool.wait_ge(y_in[f], 2 * 16)
                pool.tensor_tensor(x[:, fs, :], x[:, fs, :], yg[:, fs, :], ALU.add).then_inc(y_added, 1)

            pool.tensor_copy(one_row[:], ones[0:STACK + 1, :]).then_inc(edge_w_ready, 1)
            pool.wait_ge(node_w_in, 16 * 5)
            pool.tensor_copy(wf2s[:, 0], wf2[:]).then_inc(edge_w_ready, 1)
            pool.wait_ge(edge_w_ready, 2)
            pool.tensor_tensor(wf2s[:, 1], wf2[:], wf2s[:, 0].bitcast(F32), ALU.subtract).then_inc(edge_w_ready, 1)

            def copy_gather_indices(c, b, warm):
                if warm:
                    for t in range(GROUP):
                        pool.wait_ge(xg_in[b][t], (c // 2) * 16 if isinstance(c, int) else (c - b) * 8)
                pool.tensor_copy(gidx[b][:], dst_col[:, bass.ds(c * GROUP, GROUP)]).then_inc(gidx_ready, 1)

            def gather(c, b, t, warm):
                waits(pool, pool_passed, (gidx_ready, c + 1), *([(msg_ready, (c - 2) * GROUP + t + 1)] if warm else []))
                pool.indirect_dma_start(xg[b][:, t, :], None, xn_d, bass.IndirectOffsetOnAxis(ap=gidx[b][:, t:t + 1], axis=0)).then_inc(xg_in[b][t], 16)

            def scatter(c, b, t, warm):
                waits(pool, pool_passed, (sidx_ready, c + 1), (sum_copied, c * GROUP + t + 1), *([(added[t], c * 16)] if warm else []))
                pool.indirect_dma_start(agg_d[t], bass.IndirectOffsetOnAxis(ap=sidx[b][:, t:t + 1], axis=0), summed[b][:, t, :], None,
                                        compute_op=ALU.add).then_inc(added[t], 16)

            def edge_chunk(c, b, last=False):
                if not last:
                    warm_next = not isinstance(c, int) or c >= 1
                    copy_gather_indices(c + 1, 1 - b, warm_next)
                for t in range(GROUP):
                    if not last:
                        gather(c + 1, 1 - b, t, warm_next)
                    scatter(c, b, t, not isinstance(c, int) or c >= 1)

            pool.wait_ge(col_in, 32)
            pool.wait_ge(agg_zeroed, N_ZERO * 16)
            pool.wait_ge(xn_stored, 16 * FOLDS)

            def gathers():
                copy_gather_indices(0, 0, False)
                for t in range(GROUP):
                    gather(0, 0, t, False)
                chunks(pool, lambda c, b, n, left: edge_chunk(c, b, not left), 1)

            def rows_low(c, b):
                waits(pool, pool_passed, (xw_high, c + 1))
                pool.tensor_tensor(xws[b][:, 1, :], xw[b][:], xws[b][:, 0, :].bitcast(F32), ALU.subtract).then_inc(xw_low, 1)

            def window_chunk(c, b, n, left):
                if left:
                    rows_low(c + 1, 1 - b)
                for t in range(GROUP):
                    scatter(c, b, t, warm(c, 1))

            def windows():
                rows_low(0, 0)
                chunks(pool, window_chunk, 1)

            by_path(pool, windows, gathers)

            def halve_dense(e, b, warm):
                waits(pool, pool_passed, (dw_in, (e + 1) * 48), *([(d3_mm, (e - 1) * TILES)] if warm else []))
                pool.tensor_copy(dw[b][0][:], dw_full[:]).then_inc(dw_halved, 1)
                waits(pool, pool_passed, (dw_halved, e * 2 + 1))
                pool.tensor_tensor(dw[b][1][:], dw_full[:], dw[b][0][:].bitcast(F32), ALU.subtract).then_inc(dw_halved, 1)

            for e in range(2):
                halve_dense(e, e, False)
            with pool.Fori(1, EXPERTS // 2) as i:
                for b in range(2):
                    halve_dense(i * 2 + b, b, True)

        @block.tensor
        def _(pe):
            pe.wait_ge(consts_ready, 4)

            def turn(k, t, used, count):
                pe.wait_ge(ln_tile, (0, 1, 3)[k] * TILES + t + 1)
                n = len(turn_banks[k])
                if t >= n:
                    pe.wait_ge(used, count + t - n + 1)
                for j in range(KD):
                    ins = pe.transpose(turn_bank(k, t)[:, j * P:(j + 1) * P], xn[:, t, j * HALF:(j + 1) * HALF], ident[0:P, 0:P])
                ins.then_inc(turned, 1)

            pe.wait_ge(waug_ready, 1)

            def table(t):
                pe.wait_ge(turned_copied, t + 1)
                if t >= 2:
                    pe.wait_ge(tab_copied, t - 1)
                for k in range(KD):
                    ins = pe.matmul(bank[2 + t % 2][0:P, 0:TAB], xT[:, k, t * P:(t + 1) * P], waug[:, k, :], start=k == 0, stop=k == KD - 1)
                ins.then_inc(tab_mm, 1)

            for t in range(TILES + 1):
                if t < TILES:
                    turn(0, t, turned_copied, 0)
                if t >= 1:
                    table(t - 1)

            pe.wait_ge(small_w_in, 32)
            for t in range(TILES + 1):
                if t < TILES:
                    turn(1, t, turned_copied, TILES)
                if t >= 1:
                    u = t - 1
                    pe.wait_ge(turned_copied, TILES + u + 1)
                    for j in range(KD):
                        ins = pe.matmul(bank[4][0:P, u * EXPERTS:(u + 1) * EXPERTS], xT[:, j, u * P:(u + 1) * P], gate_w[:, j, :], start=j == 0, stop=j == KD - 1)
                    ins.then_inc(gate_mm, 1)
            pe.wait_ge(count_ready, 1)
            pe.matmul(bank[5][0:P, 0:EXPERTS], upper[:], tot8[:], start=True, stop=True).then_inc(count_mm, 1)

            def turn_rows(e, b, n):
                pe.wait_ge(brow_in[b], n * 16)
                if not isinstance(e, int) or e >= 1:
                    pe.wait_ge(b_low, e * KD)
                for k in range(KD):
                    for j in range(ROW_TILES):
                        ins = pe.transpose(bank[k][:, j * HALF:(j + 1) * HALF], brow[b][:, j, k * HALF:(k + 1) * HALF], ident[:])
                    ins.then_inc(b_turned, 1)

            def expert(e, b, n, last=False):
                later = not isinstance(e, int) or e >= 1
                pe.wait_ge(w_high, e * 2 + 1)
                pe.wait_ge(w_low, e * 2 + 1)
                pe.wait_ge(b_low, (e + 1) * KD)
                for f in range(FC):
                    if later or f >= 4:
                        pe.wait_ge(ff1_act, (e * FC + f - 3) * 2)
                    three_passes(pe, bank[2 + f % 4][:, 0:CAP_EVEN], [[w1[h][:, k, f * HALF:(f + 1) * HALF] for h in range(2)] for k in range(KD)],
                                 [[bT[h][:, k, 0:CAP_EVEN] for h in range(2)] for k in range(KD)]).then_inc(ff1_mm, 1)
                if not last:
                    turn_rows(e + 1, 1 - b, next_n(b, n))
                pe.wait_ge(w_high, e * 2 + 2)
                pe.wait_ge(w_low, e * 2 + 2)
                for j in range(ROW_TILES):
                    m = HALF if j < ROW_TILES - 1 else LAST_ROWS
                    if later or j >= 2:
                        pe.wait_ge(ff2_bias, e * ROW_TILES + j - 1)
                    for f in range(FC):
                        if j == 0:
                            pe.wait_ge(ff1_low, e * FC + f + 1)
                        ins = three_passes(pe, bank[6 + j % 2][0:m, 0:D], [[hid[h][:, f, j * HALF:j * HALF + m] for h in range(2)]],
                                           [[w2[h][:, f, :] for h in range(2)]], first=f == 0, last=f == FC - 1)
                    ins.then_inc(ff2_mm, 1)

            turn_rows(0, 0, 1)
            experts(pe, expert)

            def edge_first(c, b, n):
                pe.wait_ge(attr_in[b], n * 16)
                for a, (lo, hi) in enumerate(PIECES):
                    for k in range(KD):
                        if not isinstance(c, int) or c >= 1:
                            pe.wait_ge(hid_act, (c - 1) * 4 + 2 * a + k + 1)
                        pe.matmul(bank[2 * a + k][:, 0:hi - lo], wf1[:, k * HALF:(k + 1) * HALF], attr[b][:, lo:hi],
                                  start=True, stop=True).then_inc(hid_mm, 1)

            def edge_filter(c, b, t):
                if t == 0:
                    pe.wait_ge(hid_act, c * 4 + 2)
                if t == 3:
                    pe.wait_ge(hid_act, c * 4 + 4)
                g = c * GROUP + t
                if not isinstance(c, int) or g >= 2:
                    pe.wait_ge(filt_ready, g - 1)
                for k in range(KD):
                    ins = pe.matmul(bank[4 + (b + t) % 2][0:P, 0:D], eh[b][:, k, t * P:(t + 1) * P], wf2[:, k, :], start=k == 0, stop=k == KD - 1)
                ins.then_inc(pair_mm, 1)

            def edge_sum(c, b, t):
                g = c * GROUP + t
                pe.wait_ge(msg_ready, g + 1)
                pe.wait_ge(same_ready, c + 1)
                if not isinstance(c, int) or g >= 2:
                    pe.wait_ge(sum_copied, g - 1)
                pe.matmul(bank[6 + (b + t) % 2][0:P, 0:D], same[b][:, t, :], msg[(b + t) % 2][:], start=True, stop=True).then_inc(sum_mm, 1)

            def edge_chunk(c, b, n_next, last=False):
                if not last:
                    edge_first(c + 1, 1 - b, n_next)
                for t in range(GROUP + 1):
                    if t < GROUP:
                        edge_filter(c, b, t)
                    if t >= 1:
                        edge_sum(c, b, t - 1)

            pe.wait_ge(node_w_in, 16 * 5)
            pe.wait_ge(ff2_bias, EXPERTS * ROW_TILES)
            pe.wait_ge(ends_ready, 1)
            for j in range(2):
                ins = pe.transpose(bank[j][0:CHUNKS, 0:P], ends[:, j, :], ident[0:P, 0:P])
            ins.then_inc(ends_turned, 1)
            pe.wait_ge(window_ready, 1)
            for j in range(2):
                ins = pe.transpose(bank[2][0:1, j * CHUNKS:(j + 1) * CHUNKS], span[:, 2 + j:3 + j], ident[0:CHUNKS, 0:CHUNKS])
            ins.then_inc(window_turned, 1)
            pe.wait_ge(window_int, 1)
            pe.matmul(bank[3][:, 0:CHUNKS], ones[0:1, :], window_f[:, 0:CHUNKS], start=True, stop=True).then_inc(window_spread, 1)

            def gathers():
                edge_first(0, 0, 1)
                chunks(pe, lambda c, b, n, left: edge_chunk(c, b, next_n(b, n), not left), 1)

            def window_first(c, b, a):
                if a == 0:
                    pe.wait_ge(att_low, c + 1)
                if warm(c * NT + a, 2):
                    pe.wait_ge(hid_act, (c * NT + a - 1) * 2)
                lo, m = [v * P for v in THIRDS[a]]
                w = m + m % 2
                for k in range(KD):
                    ins = pe.matmul(bank[4 + (b + a) % 2][:, k * w:(k + 1) * w], w3s[:, k * HALF:(k + 1) * HALF], att3s[b][:, lo + m - w:lo + m], start=True, stop=True)
                ins.then_inc(hid_mm, 1)

            def window_pair(c, b, t):
                if t == 0:
                    pe.wait_ge(hid_low, c * NT + 1)
                    pe.wait_ge(xw_low, c + 1)
                    pe.wait_ge(hot_ready, c + 1)
                elif t % 2 == 0:
                    pe.wait_ge(hid_low, c * NT + t // 2 + 1)
                if warm(c * GROUP + t, 3):
                    pe.wait_ge(msg_ready, c * GROUP + t - 2)
                dst = pair_bank(b, t)
                ts = slice(t * P, (t + 1) * P)
                three_passes(pe, dst[0:P, 0:D], [[eh2[b][h][:, k, ts] for h in range(2)] for k in range(KD)],
                             [[wf2s[:, h, k, :] for h in range(2)] for k in range(KD)], last=False)
                pe.matmul(dst[0:P, 0:D], one_row[:, 0:P], b3s[:], start=False, stop=True)
                for h in range(2):
                    ins = pe.matmul(dst[0:P, D:2 * D], hot[b][:, ts], xws[b][:, h, :], start=h == 0, stop=h == 1)
                ins.then_inc(pair_mm, 1)

            def window_sum(c, b, t):
                g = c * GROUP + t
                pe.wait_ge(msg_ready, g + 1)
                if warm(g, 2):
                    pe.wait_ge(sum_copied, g - 1)
                pe.matmul(bank[6 + (b + t) % 2][0:P, 0:D], same[b][:, t, :], msgs[:, t, :], start=True, stop=True).then_inc(sum_mm, 1)

            def window_chunk(c, b, n, left):
                for t in range(GROUP):
                    window_pair(c, b, t)
                    if t == 0:
                        window_first(c, b, 2)
                    elif left and t in (1, 3):
                        window_first(c + 1, 1 - b, t // 2)
                    behind = tiles_behind(c, b, t, 2)
                    if behind:
                        window_sum(*behind)
                if not left:
                    for t in range(GROUP - 2, GROUP):
                        window_sum(c, b, t)

            def windows():
                pe.wait_ge(edge_w_ready, 3)
                pe.wait_ge(stack_ready, 1)
                for a in range(2):
                    window_first(0, 0, a)
                chunks(pe, window_chunk, 1)

            by_path(pe, windows, gathers)

            pe.wait_ge(sum_copied, E_TILES)

            def fold_turn(f):
                pe.wait_ge(agg_ready, f + 1)
                for q in range(FOLD):
                    g = f * FOLD + q
                    if g >= 2:
                        pe.wait_ge(agg_copied, g - 1)
                    for k in range(KD):
                        ins = pe.transpose(bank[g % 2][:, k * P:(k + 1) * P], part[f % 2][0][:, q, k * HALF:(k + 1) * HALF], ident[0:P, 0:P])
                    ins.then_inc(agg_turned, 1)

            def fold_layer(f, w, src, used, need, done, at):
                pe.wait_ge(used, need)
                for a, (lo, hi) in enumerate(PIECES):
                    for o in range(KD):
                        n = f * 4 + a * 2 + o
                        if n >= 2:
                            pe.wait_ge(u_silu if done is u_mm else h_ready, n - 1)
                        for k in range(KD):
                            ins = pe.matmul(bank[at + o][:, 0:hi - lo], w[:, k, o * HALF:(o + 1) * HALF], src[:, k, lo:hi], start=k == 0, stop=k == KD - 1)
                        ins.then_inc(done, 1)

            for f in range(FOLDS + 1):
                if f < FOLDS:
                    fold_turn(f)
                    fold_layer(f, wu1, aggT[f % 2], agg_copied, (f + 1) * FOLD, u_mm, 2)
                if f >= 1:
                    fold_layer(f - 1, wu2, uT[(f - 1) % 2], u_silu, f * 4, h_mm, 4)

            pe.wait_ge(wr_halved, 2)
            def turn_back(f):
                pe.wait_ge(bn_applied, KD * (f + 1))
                for t in range(f * FOLD, (f + 1) * FOLD):
                    if t >= 3:
                        pe.wait_ge(x3_ready, t - 2)
                    for k in range(KD):
                        ins = pe.transpose(bank[5 + t % 3][0:P, k * HALF:(k + 1) * HALF], xT[:, k, t * P:(t + 1) * P], ident[:])
                    ins.then_inc(bn_turned, 1)

            def raw_logits(s):
                at, n = STEPS[s]
                w = n * P + n * P % 2
                lo = (at + n) * P - w
                pe.wait_ge(x_low, at + n)
                if s >= 1:
                    pe.wait_ge(raw_copied, s)
                for h, m in ((0, 2 * EXPERTS), (1, EXPERTS)):
                    for k in range(KD):
                        ins = pe.matmul(bank[4][0:m, 0:w], wrs[:, k, 0:m], xTs[h][:, k, lo:lo + w], start=h == 0 and k == 0, stop=h == 1 and k == KD - 1)
                ins.then_inc(raw_mm, 1)

            def mix_logits(s):
                at, n = STEPS[s]
                pe.wait_ge(raw_copied, s + 1)
                for q in range(n):
                    ins = pe.matmul(bank[3][0:P, (at + q) * EXPERTS:(at + q + 1) * EXPERTS], raw[s % 2][:, q * P:(q + 1) * P], add_halves[:], start=True, stop=True)
                ins.then_inc(mix_mm, 1)

            todo = list(range(NS))
            for f in range(FOLDS + 2):
                if f < FOLDS:
                    turn_back(f)
                if 1 <= f <= FOLDS:
                    for t in range((f - 1) * FOLD, f * FOLD):
                        turn(2, t, x_low, 0)
                while todo and sum(STEPS[todo[0]]) <= (f - 1) * FOLD:
                    s = todo.pop(0)
                    raw_logits(s)
                    if s >= 1:
                        mix_logits(s - 1)
            mix_logits(NS - 1)

            def dense_layer(e, b, s, layer):
                at, n = STEPS[s]
                m = n * P
                done, act = ((d1_mm, d1_act), (d2_mm, d2_act))[layer]
                g = e * (NS * KD) + s * KD
                if layer == 0 and s == 0:
                    pe.wait_ge(dw_halved, (e + 1) * 2)
                if layer == 1:
                    pe.wait_ge(d1_low, g + KD)
                    if isinstance(e, int) and e == 0 and s == 0:
                        pe.wait_ge(mix_shift, 1)
                for o in range(KD):
                    if not isinstance(e, int) or e or s:
                        pe.wait_ge(act, (g + o - 1) * 2)
                    src = xTs if layer == 0 else h1[(b + s) % 2]
                    w = m + m % 2
                    lo = at * P + m - w if layer == 0 else 0
                    three_passes(pe, bank[2 * layer + o][:, 0:w], [[dw[b][h][:, layer * KD + k, o * HALF:(o + 1) * HALF] for h in range(2)] for k in range(KD)],
                                 [[src[h][:, k, lo:lo + w] for h in range(2)] for k in range(KD)]).then_inc(done, 1)

            def dense_last(e, b, s):
                at, n = STEPS[s]
                pe.wait_ge(d2_low, e * (NS * KD) + s * KD + KD)
                for q in range(n):
                    if isinstance(e, int) and e == 0:
                        bias_product(at + q - 1)
                    elif isinstance(e, int) and e == 1 and at + q == 0:
                        bias_product(TILES - 1)
                    free = last_bank_free(e, at + q)
                    if free is not None:
                        pe.wait_ge(d3_added, e * TILES + free)
                    three_passes(pe, last_bank(e, b, at + q)[0:P, 0:D], [[h2[(b + s) % 2][h][:, k, q * P:(q + 1) * P] for h in range(2)] for k in range(KD)],
                                 [[dw[b][h][:, 2 * KD + k, :] for h in range(2)] for k in range(KD)]).then_inc(d3_mm, 1)

            def bias_product(t):
                if t < 0:
                    return
                if t % TOK == 0:
                    pe.wait_ge(mixT_ready, t // TOK + 1)
                if t >= 1:
                    pe.wait_ge(bo_added, t)
                pe.matmul(bank[7][0:P, 0:D], mixT[:, t * P:(t + 1) * P], bo[:], start=True, stop=True).then_inc(bo_mm, 1)

            def turn_mix(s):
                at, n = STEPS[s]
                if s == 0:
                    pe.wait_ge(mix_ready, 1)
                else:
                    pe.wait_ge(mixT_ready, s)
                for q in range(n):
                    ins = pe.transpose(bank[6][0:EXPERTS, q * P:(q + 1) * P], mix[:, at + q, :], ident[0:P, 0:P])
                ins.then_inc(mix_turned, 1)

            dense_steps(pe, ((lambda e, b, s: dense_layer(e, b, s, 0), 0), (lambda e, b, s: dense_layer(e, b, s, 1), 1), (dense_last, 2)),
                        turn_mix)

        @block.scalar
        def _(act):
            def ln_sqrt(k, f):
                act.wait_ge(ln_var, k * FOLDS + f + 1)
                act.activation(rstd[:, f * FOLD:(f + 1) * FOLD], mv[:, f * FOLD:(f + 1) * FOLD, 1], ACT.Sqrt, bias=eps1[0:P, 0:1]).then_inc(ln_std, 1)

            def turn_copies(k, f):
                for t in range(f * FOLD, (f + 1) * FOLD):
                    act.wait_ge(turned, k * TILES + t + 1)
                    dst = xT if k < 2 else xTs[0]
                    act.activation(dst[:, :, t * P:(t + 1) * P], turn_bank(k, t)[:, 0:KD * P].rearrange("p (k e) -> p k e", k=KD), ACT.Copy).then_inc(turned_copied, 1)

            act.wait_ge(consts_ready, 9)
            for f in range(FOLDS + 1):
                if f < FOLDS:
                    ln_sqrt(0, f)
                if f >= 1:
                    turn_copies(0, f - 1)
            act.wait_ge(vec_in, 32)
            for j, v in enumerate(("v1", "v2")):
                ins = act.activation(scl[:, j, :], chan[:, PAIR_AT[v]:PAIR_AT[v] + EXPERTS * KD], ACT.Sqrt, bias=eps1[:, 1:2])
                ins.then_inc(aff_std, 1)
            for f in range(FOLDS + 2):
                if f < FOLDS:
                    fs = slice(f * FOLD, (f + 1) * FOLD)
                    act.wait_ge(att_shift, f + 1)
                    act.activation(sm8[:, 1, fs, 0:HEADS], sm8[:, 0, fs, 0:HEADS], ACT.Exp).then_inc(att_exp, 1)
                if f >= 2:
                    turn_copies(1, f - 2)
                if f < FOLDS:
                    ln_sqrt(1, f)
            act.wait_ge(gate_shift, 1)
            act.activation(sm8[:, 2, :, :], sm8[:, 1, :, :], ACT.Exp).then_inc(gate_exp, 1)

            def rows_high(e):
                for k in range(KD):
                    act.wait_ge(b_turned, e * KD + k + 1)
                    act.activation(bT[0][:, k, :], bank[k][:], ACT.Copy).then_inc(b_high, 1)

            def expert(e, last=False):
                for f in range(FC):
                    g = e * FC + f
                    waits(act, act_passed, (ff1_mm, g + 1), *([] if isinstance(e, int) and e == 0 and f < 2 else [(ff1_low, g - 1)]))
                    bias = chan[:, bass.ds(e * FC + FFB1_AT + f, 1)]
                    act.activation(act_full[f % 2][:, 0:CAP_EVEN], bank[2 + f % 4][:, 0:CAP_EVEN], ACT.Relu, bias=bias).then_inc(ff1_act, 1)
                    act.activation(hid[0][:, f, 0:CAP_EVEN], bank[2 + f % 4][:, 0:CAP_EVEN], ACT.Relu, bias=bias).then_inc(ff1_act, 1)
                if not last:
                    rows_high(e + 1)
                    act.wait_ge(w1_in, (e + 2) * 16)
                    act.activation(w1[0][:], w1_full[:], ACT.Copy).then_inc(w_high, 1)
                    act.wait_ge(w2_in, (e + 2) * 16)
                    act.wait_ge(ff2_mm, (e + 1) * ROW_TILES)
                    act.activation(w2[0][:], w2_full[:], ACT.Copy).then_inc(w_high, 1)

            act.wait_ge(w1_in, 16)
            act.wait_ge(gate_mm, TILES)
            act.activation(w1[0][:], w1_full[:], ACT.Copy).then_inc(w_high, 1)
            act.wait_ge(w2_in, 16)
            act.activation(w2[0][:], w2_full[:], ACT.Copy).then_inc(w_high, 1)
            rows_high(0)
            expert(0)
            with act.Fori(1, EXPERTS - 1) as e:
                expert(e)
            expert(EXPERTS - 1, last=True)

            for f in range(FOLDS):
                ln_sqrt(2, f)

            def edge_silu(c, b):
                for a, (lo, hi) in enumerate(PIECES):
                    for k in range(KD):
                        act.wait_ge(hid_mm, c * 4 + 2 * a + k + 1)
                        if not isinstance(c, int) or c >= 2:
                            act.wait_ge(pair_mm, (c - 1) * GROUP)
                        act.activation(eh[b][:, k, lo:hi], bank[2 * a + k][:, 0:hi - lo], ACT.Silu,
                                       bias=chan[:, CH_AT["bf1"] + k:CH_AT["bf1"] + k + 1]).then_inc(hid_act, 1)

            def edge_chunk(c, b, last=False):
                if not last:
                    edge_silu(c + 1, 1 - b)
                for t in range(GROUP):
                    g = c * GROUP + t
                    act.wait_ge(sum_mm, g + 1)
                    if not isinstance(c, int) or c >= 2:
                        act.wait_ge(added[t], (c - 1) * 16)
                    act.activation(summed[b][:, t, :], bank[6 + (b + t) % 2][0:P, 0:D], ACT.Copy).then_inc(sum_copied, 1)

            def gathers():
                edge_silu(0, 0)
                chunks(act, lambda c, b, n, left: edge_chunk(c, b, not left), 1)

            def inputs_high(c, b, n):
                act.wait_ge(attr_in[b], n * 48)
                if warm(c, 2):
                    act.wait_ge(hid_mm, (c - 1) * NT)
                act.activation(att3s[b][:], att3[b][:], ACT.Copy).then_inc(att_high, 1)

            def rows_high(c, b, n):
                act.wait_ge(srow_in[b], n * 48)
                if warm(c, 2):
                    act.wait_ge(pair_mm, (c - 1) * GROUP)
                act.activation(xws[b][:, 0, :], xw[b][:], ACT.Copy).then_inc(xw_high, 1)

            def window_silu(c, b, a):
                lo, m = [v * P for v in THIRDS[a]]
                act.wait_ge(hid_mm, c * NT + a + 1)
                if warm(c, 1):
                    act.wait_ge(hid_low, (c - 1) * NT + a + 1)
                if warm(c, 2):
                    act.wait_ge(pair_mm, (c - 1) * GROUP)
                w = m + m % 2
                src = bank[4 + (b + a) % 2][:, 0:KD * w].rearrange("p (k e) -> p k e", k=KD)[:, :, w - m:w]
                for dst in (eh_full, eh2[b][0]):
                    act.activation(dst[:, :, lo:lo + m], src, ACT.Silu, bias=eps1[:, 2:3]).then_inc(hid_act, 1)

            def window_ends(c, b, t):
                act.wait_ge(pair_mm, c * GROUP + t + 1)
                if warm(c, 1):
                    act.wait_ge(msg_ready, (c - 1) * GROUP + t + 1)
                act.activation(ends_x[:, t, :], pair_bank(b, t)[0:P, D:2 * D], ACT.Copy).then_inc(ends_copied, 1)

            def window_copy(c, b, t):
                act.wait_ge(sum_mm, c * GROUP + t + 1)
                if warm(c, 2):
                    act.wait_ge(added[t], (c - 1) * 16)
                act.activation(summed[b][:, t, :], bank[6 + (b + t) % 2][0:P, 0:D], ACT.Copy).then_inc(sum_copied, 1)

            def window_chunk(c, b, n, left):
                for t in range(GROUP):
                    behind = tiles_behind(c, b, t, 3)
                    if behind:
                        window_copy(*behind)
                    window_ends(c, b, t)
                    if t == 0 and left:
                        rows_high(c + 1, 1 - b, next_n(b, n))
                    elif t == 1:
                        window_silu(c, b, 2)
                    elif t == 3 and left == 2:
                        inputs_high(c + 2, b, n + 1)
                    elif t in (2, 4) and left:
                        window_silu(c + 1, 1 - b, t // 2 - 1)
                if not left:
                    for t in range(GROUP - 3, GROUP):
                        window_copy(c, b, t)

            def windows():
                for c in range(2):
                    inputs_high(c, c, 1)
                for a in range(2):
                    window_silu(0, 0, a)
                rows_high(0, 0, 1)
                chunks(act, window_chunk, 2)

            by_path(act, windows, gathers)

            def fold_copies(f):
                for q in range(FOLD):
                    g = f * FOLD + q
                    act.wait_ge(agg_turned, g + 1)
                    if f >= 2:
                        act.wait_ge(u_mm, (f - 1) * 4)
                    act.activation(aggT[f % 2][:, :, q * P:(q + 1) * P], bank[g % 2][:, 0:KD * P].rearrange("p (k e) -> p k e", k=KD), ACT.Copy).then_inc(agg_copied, 1)
                for a, (lo, hi) in enumerate(PIECES):
                    for o in range(KD):
                        act.wait_ge(u_mm, f * 4 + a * 2 + o + 1)
                        if f >= 2:
                            act.wait_ge(h_mm, (f - 1) * 4)
                        act.activation(uT[f % 2][:, o, lo:hi], bank[2 + o][:, 0:hi - lo], ACT.Silu,
                                       bias=chan[:, CH_AT["bu1"] + o:CH_AT["bu1"] + o + 1]).then_inc(u_silu, 1)

            def fold_bias(f):
                for a, (lo, hi) in enumerate(PIECES):
                    for o in range(KD):
                        act.wait_ge(h_mm, f * 4 + a * 2 + o + 1)
                        act.activation(xT[:, o, f * FOLD * P + lo:f * FOLD * P + hi], bank[4 + o][:, 0:hi - lo], ACT.Identity,
                                       bias=chan[:, CH_AT["bu2"] + o:CH_AT["bu2"] + o + 1]).then_inc(h_ready, 1)

            for f in range(FOLDS + 1):
                if f < FOLDS:
                    fold_copies(f)
                if f >= 1:
                    fold_bias(f - 1)
            act.wait_ge(bn_var, 1)
            act.activation(csc[:, 0, :], cmv[:, :, 1], ACT.Sqrt, bias=eps1[:, 0:1]).then_inc(bn_std, 1)
            act.wait_ge(bn_scale, 1)
            for f in range(FOLDS):
                for k in range(KD):
                    act.activation(xT[:, k, f * FOLD * P:(f + 1) * FOLD * P], xT[:, k, f * FOLD * P:(f + 1) * FOLD * P], ACT.Identity,
                                   bias=csc[:, 2, k:k + 1], scale=csc[:, 1, k:k + 1]).then_inc(bn_applied, 1)
            def raw_copies(s):
                at, n = STEPS[s]
                m = n * P
                act.wait_ge(raw_mm, s + 1)
                if s >= 2:
                    act.wait_ge(mix_mm, s - 1)
                act.activation(raw[s % 2][:, 0:m], bank[4][0:2 * EXPERTS, m % 2:m % 2 + m], ACT.Copy).then_inc(raw_copied, 1)

            todo = list(range(NS))
            for f in range(FOLDS + 2):
                if f < FOLDS:
                    ln_sqrt(3, f)
                if 1 <= f <= FOLDS:
                    turn_copies(2, f - 1)
                while todo and sum(STEPS[todo[0]]) <= (f - 1) * FOLD:
                    raw_copies(todo.pop(0))
            act.wait_ge(mix_shift, 1)
            act.activation(sm8[:, 1, :, :], sm8[:, 0, :, :], ACT.Exp).then_inc(mix_exp, 1)
            act.wait_ge(aff_ready, 1)
            act.wait_ge(bn_turned, TILES)

            def dense_act(e, b, s, layer):
                at, n = STEPS[s]
                m = n * P
                mm, done, low, used = ((d1_mm, d1_act, d1_low, d2_mm), (d2_mm, d2_act, d2_low, d3_mm))[layer]
                g = e * (NS * KD) + s * KD
                dst = (h1, h2)[layer][(b + s) % 2][0]
                for o in range(KD):
                    before = step_behind(e, b, s, 2)
                    need = [(low, g + o - 1)] if step_behind(e, b, s, 1) else []
                    if before:
                        was, _, at_step = before
                        end = STEPS[at_step][0] + STEPS[at_step][1]
                        need += [(used, g - KD if layer == 0 else was * TILES + end)]
                    waits(act, act_passed, (mm, g + o + 1), *need)
                    bias, scale = [v[:, layer, bass.ds(e * KD + o, 1)] for v in (shf, scl)]
                    off = m % 2 if layer == 0 else 0
                    for out_ in (h_full[layer][o][:, 0:m], dst[:, o, 0:m]):
                        act.activation(out_, bank[2 * layer + o][:, off:off + m], ACT.Relu, bias=bias, scale=scale).then_inc(done, 1)

            def mix_copies(s):
                at, n = STEPS[s]
                act.wait_ge(mix_turned, s + 1)
                act.activation(mixT[:, at * P:(at + n) * P], bank[6][0:EXPERTS, 0:n * P], ACT.Copy).then_inc(mixT_ready, 1)

            dense_steps(act, ((lambda e, b, s: dense_act(e, b, s, 0), 0), (lambda e, b, s: dense_act(e, b, s, 1), 1)), mix_copies)

        @block.vector
        def _(dve):
            chain = Tally(dve_chain)

            def step(ins):
                dve.wait_ge(chain.sem, chain.inc(ins))

            def ln_stats(k, f):
                for t in range(f * FOLD, (f + 1) * FOLD):
                    ins = dve.bn_stats(stats[:, t, :], x[:, t, :])
                step(ins)
                for t in range(f * FOLD, (f + 1) * FOLD):
                    ins = dve.bn_aggr(mv[:, t, :], stats[:, t, :])
                ins.then_inc(ln_var, 1)

            def ln_apply(k, f):
                r = rstd[:, f * FOLD:(f + 1) * FOLD]
                dve.wait_ge(ln_std, k * FOLDS + f + 1)
                step(dve.reciprocal(r, r))
                for t in range(f * FOLD, (f + 1) * FOLD):
                    dve.tensor_scalar(xn[:, t, 0:D], x[:, t, :], mv[:, t, 0:1], rstd[:, t:t + 1], ALU.subtract, ALU.mult).then_inc(ln_tile, 1)

            dve.wait_ge(vec_in, 16)
            dve.wait_ge(gnn_w_in, 16)
            for j, name in enumerate(("attn_l", "attn_r")):
                w4 = waug[:, :, 0:D].rearrange("p k (h d) -> p k h d", d=HEAD_D)
                a4 = row[name].rearrange("p (h d) -> p h d", d=HEAD_D)
                for k in range(KD):
                    ins = dve.tensor_tensor(wprod[:, k * HEADS:(k + 1) * HEADS, :], w4[:, k], a4, ALU.mult)
                step(ins)
                for k in range(KD):
                    ins = dve.tensor_reduce(waug[:, k, D + j * HEADS:D + (j + 1) * HEADS], wprod[:, k * HEADS:(k + 1) * HEADS, :], AX_X, ALU.add)
                if j == 0:
                    step(ins)
            ins.then_inc(waug_ready, 1)

            def table_copies(f):
                for t in range(f * FOLD, (f + 1) * FOLD):
                    dve.wait_ge(tab_mm, t + 1)
                    dve.tensor_copy(tab[:, t, :], bank[2 + t % 2][0:P, 0:TAB]).then_inc(tab_copied, 1)

            for f in range(FOLDS + 2):
                if f < FOLDS:
                    dve.wait_ge(x_in[f], 16)
                    ln_stats(0, f)
                if 1 <= f <= FOLDS:
                    ln_apply(0, f - 1)
                if f >= 2:
                    table_copies(f - 2)

            dve.wait_ge(vec_in, 32)
            dve.wait_ge(aff_std, 2)
            step(dve.reciprocal(scl[:].rearrange("p a b -> p (a b)"), scl[:].rearrange("p a b -> p (a b)")))

            def pair(name):
                return chan[:, PAIR_AT[name]:PAIR_AT[name] + EXPERTS * KD]

            for j in range(2):
                dve.tensor_tensor(shf[:, j, :], pair(f"b{j + 1}"), pair(f"m{j + 1}"), ALU.subtract)
                ins = dve.tensor_tensor(scl[:, j, :], scl[:, j, :], pair(f"g{j + 1}"), ALU.mult)
            step(ins)
            for j in range(2):
                ins = dve.tensor_tensor(shf[:, j, :], shf[:, j, :], scl[:, j, :], ALU.mult)
            step(ins)
            for j in range(2):
                ins = dve.tensor_tensor(shf[:, j, :], shf[:, j, :], pair(f"be{j + 1}"), ALU.add)
            ins.then_inc(aff_ready, 1)
            dve.wait_ge(small_w_in, 32)
            dve.wait_ge(consts_ready, 9)
            dve.tensor_copy(wrs[:, :, 0:EXPERTS], wr[:]).then_inc(wr_halved, 1)
            dve.wait_ge(wr_halved, 1)
            dve.tensor_tensor(wrs[:, :, EXPERTS:2 * EXPERTS], wr[:], wrs[:, :, 0:EXPERTS].bitcast(F32), ALU.subtract)
            dve.tensor_tensor(add_halves[:], ident[0:2 * EXPERTS, 0:EXPERTS], ident[0:2 * EXPERTS, EXPERTS:2 * EXPERTS], ALU.add).then_inc(wr_halved, 1)

            def attend(f):
                fs = slice(f * FOLD, (f + 1) * FOLD)

                def over_heads(v):
                    return v[:, fs].rearrange("p (t o) -> p t o", o=1).to_broadcast([P, FOLD, HEADS])

                dve.wait_ge(att_in[f], 2 * FOLD * 16)
                s4, e4 = sm8[:, 0, fs, 0:HEADS], sm8[:, 1, fs, 0:HEADS]
                step(dve.tensor_tensor(s4, tsrc[:, fs, :], tdst[:, fs, D + HEADS:TAB], ALU.add))
                step(dve.scalar_tensor_tensor(s4, s4, LEAK, s4, ALU.mult, ALU.max))
                step(dve.tensor_reduce(sm1[:, 0, fs], s4, AX_X, ALU.max))
                dve.tensor_tensor(s4, s4, over_heads(sm1[:, 0, :]), ALU.subtract).then_inc(att_shift, 1)
                dve.wait_ge(att_exp, f + 1)
                step(dve.tensor_reduce(sm1[:, 1, fs], e4, AX_X, ALU.add))
                step(dve.reciprocal(sm1[:, 1, fs], sm1[:, 1, fs]))
                step(dve.tensor_tensor(e4, e4, over_heads(sm1[:, 1, :]), ALU.mult))
                for h in range(HEADS):
                    hd = tdst[:, fs, h * HEAD_D:(h + 1) * HEAD_D]
                    ins = dve.tensor_tensor(hd, hd, sm8[:, 1, fs, h:h + 1].to_broadcast([P, FOLD, HEAD_D]), ALU.mult)
                step(ins)
                step(dve.tensor_tensor(tdst[:, fs, 0:2 * HEAD_D], tdst[:, fs, 0:2 * HEAD_D], tdst[:, fs, 2 * HEAD_D:4 * HEAD_D], ALU.add))
                step(dve.tensor_tensor(tdst[:, fs, 0:HEAD_D], tdst[:, fs, 0:HEAD_D], tdst[:, fs, HEAD_D:2 * HEAD_D], ALU.add))
                for h in range(HEADS):
                    xh = x[:, fs, h * HEAD_D:(h + 1) * HEAD_D]
                    ins = dve.tensor_tensor(xh, xh, tdst[:, fs, 0:HEAD_D], ALU.add)
                step(ins)

            for f in range(FOLDS + 1):
                if f < FOLDS:
                    attend(f)
                    ln_stats(1, f)
                if f >= 1:
                    ln_apply(1, f - 1)

            def bc(v, n):
                return v.rearrange("p (t o) -> p t o", o=1).to_broadcast([P, TILES, n])

            def rowbc(v):
                return v.rearrange("p (o e) -> p o e", o=1).to_broadcast([P, TILES, EXPERTS])

            dve.wait_ge(consts_ready, 9)
            dve.wait_ge(gate_mm, TILES)
            lg, sh, ex, oh, cum, tmp = [sm8[:, j] for j in range(6)]
            g8 = bank[4][0:P, 0:TILES * EXPERTS].rearrange("p (t e) -> p t e", e=EXPERTS)
            step(dve.tensor_tensor(lg, g8, rowbc(row["gate_b"][0:P]), ALU.add))
            step(dve.tensor_reduce(sm1[:, 0, :], lg, AX_X, ALU.max))
            dve.tensor_tensor(sh, lg, bc(sm1[:, 0, :], EXPERTS), ALU.subtract).then_inc(gate_shift, 1)
            step(dve.tensor_tensor(oh, lg, bc(sm1[:, 0, :], EXPERTS), ALU.is_equal))
            step(dve.tensor_tensor(tmp, oh, rowbc(rev[:]), ALU.mult))
            step(dve.tensor_reduce(sm1[:, 1, :], tmp, AX_X, ALU.max))
            step(dve.tensor_tensor(oh, tmp, bc(sm1[:, 1, :], EXPERTS), ALU.is_equal))
            dve.tensor_reduce(tot8[:], oh.rearrange("p t e -> p e t"), AX_X, ALU.add).then_inc(count_ready, 1)
            for e in range(EXPERTS):
                ins = dve.tensor_tensor_scan(cum[:, :, e], ones[0:P, 0:TILES], oh[:, :, e], 0.0, ALU.mult, ALU.add)
            step(ins)
            dve.wait_ge(count_mm, 1)
            step(dve.tensor_scalar(off8[:], bank[5][0:P, 0:EXPERTS], -1.0, None, ALU.add))
            step(dve.tensor_tensor(cum, cum, rowbc(off8[:]), ALU.add))
            dve.tensor_tensor(cum, cum, oh, ALU.mult)
            step(dve.tensor_tensor(tmp, oh, rowbc(eno[:]), ALU.mult))
            dve.tensor_reduce(sm1[:, 2, :], cum, AX_X, ALU.add)
            step(dve.tensor_reduce(sm1[:, 3, :], tmp, AX_X, ALU.add))
            pos, idx, kept, slot, drop, gate = [sm1[:, j, :] for j in (2, 3, 4, 5, 6, 8)]
            dve.scalar_tensor_tensor(slot, idx, float(SLOTS), pos, ALU.mult, ALU.add)
            step(dve.tensor_scalar(kept, pos, float(CAP), None, ALU.is_lt))
            step(dve.tensor_scalar(drop, kept, -float(DROPPED), float(DROPPED), ALU.mult, ALU.add))
            step(dve.tensor_tensor(slot, slot, drop, ALU.add))
            dve.tensor_copy(slot_i[:], slot)
            dve.wait_ge(gate_exp, 1)
            step(dve.tensor_reduce(gate, ex, AX_X, ALU.add))
            step(dve.reciprocal(gate, gate))
            dve.tensor_copy(xn[:, :, D], gate).then_inc(slots_ready, 1)

            def rows_low(e, b):
                for k in range(KD):
                    dve.wait_ge(b_high, e * KD + k + 1)
                    if k == KD - 1:
                        dve.tensor_copy(row_gate[b][:], brow[b][:, :, D:ROW]).then_inc(gates_taken, 1)
                    dve.tensor_tensor(bT[1][:, k, :], bank[k][:], bT[0][:, k, :].bitcast(F32), ALU.subtract).then_inc(b_low, 1)

            def expert(e, b, n, last=False):
                for f in range(FC):
                    dve.wait_ge(ff1_act, (e * FC + f + 1) * 2)
                    dve.tensor_tensor(hid[1][:, f, 0:CAP_EVEN], act_full[f % 2][:, 0:CAP_EVEN], hid[0][:, f, 0:CAP_EVEN].bitcast(F32), ALU.subtract).then_inc(ff1_low, 1)
                if not last:
                    rows_low(e + 1, 1 - b)
                if warm(e, 2):
                    dve.wait_ge(y_stored[b], (n - 1) * ROW_TILES * 16)
                c = e * 13
                dve.tensor_scalar(far[:], row_gate[b][:, :, 1], 0.5, float(DROPPED), ALU.is_lt, ALU.mult).then_inc(y_chain, 1)
                dve.wait_ge(y_chain, c + 1)
                dve.tensor_tensor(y_row[b][:], row_gate[b][:, :, 1], far[:], ALU.add)
                for h in range(2):
                    js = [(j, HALF if j < ROW_TILES - 1 else LAST_ROWS) for j in (2 * h, 2 * h + 1)]

                    def both(fn, k, done):
                        for q, (j, m) in enumerate(js):
                            ins = fn(j, m, ytmp[0][q][0:m], ytmp[1][q][0:m], ytmp[2][q][0:m])
                            if k is None:
                                ins.then_inc(done, 1)
                        if k is not None:
                            ins.then_inc(done, 1)
                            dve.wait_ge(done, c + 1 + h * 6 + k)

                    for j, m in js:
                        dve.wait_ge(ff2_mm, e * ROW_TILES + j + 1)
                        dve.tensor_tensor(ytmp[0][j % 2][0:m], bank[6 + j % 2][0:m, 0:D], b2[0:m, bass.ds(e * D, D)], ALU.add).then_inc(ff2_bias, 1)
                    dve.wait_ge(ff2_bias, e * ROW_TILES + 2 * h + 2)
                    both(lambda j, m, y, a, z: dve.tensor_scalar(y, y, row_gate[b][0:m, j, 0:1], None, ALU.mult), 1, y_chain)
                    both(lambda j, m, y, a, z: dve.tensor_scalar(a, y, -FLT_MAX, FLT_MAX, ALU.max, ALU.min), 2, y_chain)
                    both(lambda j, m, y, a, z: dve.tensor_tensor(z, a, y, ALU.is_equal), 3, y_chain)
                    both(lambda j, m, y, a, z: dve.tensor_tensor(a, a, z, ALU.mult), 4, y_chain)
                    both(lambda j, m, y, a, z: dve.tensor_scalar(z, y, FLT_MAX, None, ALU.is_gt), 5, y_chain)
                    both(lambda j, m, y, a, z: dve.scalar_tensor_tensor(z, y, -FLT_MAX, z, ALU.is_lt, ALU.subtract), 6, y_chain)
                    for q, (j, m) in enumerate(js):
                        ins = dve.scalar_tensor_tensor(yrow[b][0:m, j, :], ytmp[2][q][0:m], -BIG, ytmp[1][q][0:m], ALU.mult, ALU.add)
                    ins.then_inc(y_ready, 1)

            dve.wait_ge(b2_in, 16)
            rows_low(0, 0)
            experts(dve, expert)

            dve.wait_ge(col_in, 32)
            step(dve.tensor_copy(dst_f[:], dst_col[:]))
            by_chunk = dst_f[:].rearrange("p (c g) -> p c g", g=GROUP)
            dve.tensor_reduce(ends[:, 0, :], by_chunk, AX_X, ALU.min)
            step(dve.tensor_reduce(ends[:, 1, :], by_chunk, AX_X, ALU.max))
            dve.tensor_copy(src_f[:], src_col[:]).then_inc(ends_ready, 1)
            dve.wait_ge(ends_ready, 1)
            dve.tensor_scalar(to_trash[:], src_f[:], -1.0, trash[:, 0:1], ALU.mult, ALU.add)
            dve.wait_ge(ends_turned, 1)
            dve.tensor_reduce(span[:, 0:1], bank[0][0:CHUNKS, 0:P], AX_X, ALU.min)
            step(dve.tensor_reduce(span[:, 1:2], bank[1][0:CHUNKS, 0:P], AX_X, ALU.max))
            step(dve.tensor_scalar(span[:, 2:3], span[:, 0:1], float(N_NODES - HALF), None, ALU.min))
            step(dve.tensor_tensor(span[:, 3:4], span[:, 1:2], span[:, 2:3], ALU.subtract))
            dve.tensor_scalar(span[:, 3:4], span[:, 3:4], float(HALF), None, ALU.is_lt).then_inc(window_ready, 1)
            dve.wait_ge(window_turned, 1)
            step(dve.tensor_copy(window_f[:], bank[2][0:1, 0:2 * CHUNKS]))
            dve.tensor_reduce(flag_f[:], window_f[:, CHUNKS:2 * CHUNKS], AX_X, ALU.min)
            step(dve.tensor_copy(window[:], window_f[:, 0:CHUNKS]))
            dve.tensor_copy(flag[:], flag_f[:]).then_inc(window_int, 1)
            dve.wait_ge(window_spread, 1)
            dve.tensor_scalar(wstart[:], bank[3][:, 0:CHUNKS], wcol[:, 0:1], None, ALU.add).then_inc(path_ready, 1)

            for f in range(FOLDS + 1):
                if f < FOLDS:
                    fs = slice(f * FOLD, (f + 1) * FOLD)
                    dve.wait_ge(y_added, f + 1)
                    ln_stats(2, f)
                if f >= 1:
                    ln_apply(2, f - 1)
            dve.wait_ge(ln_tile, 3 * TILES)
            dve.wait_ge(edge_w_in, 16 * 7)
            dve.tensor_copy(w3s[:], w3[:])
            step(dve.tensor_copy(b3s[:], b3[:]))
            mid, one = slice(STACK, 2 * STACK), slice(STACK, STACK + 1)
            dve.tensor_tensor(w3s[mid], w3[mid], w3s[mid].bitcast(F32), ALU.subtract)
            dve.tensor_tensor(b3s[one], b3[one], b3s[one].bitcast(F32), ALU.subtract).then_inc(stack_ready, 1)

            def same_node(c, b, loads):
                scol = src_col[:, bass.ds(c * GROUP, GROUP)]
                dve.wait_ge(srow_in[b], loads * 16)
                if warm(c, 2):
                    dve.wait_ge(sum_mm, (c - 1) * GROUP)
                dve.tensor_tensor(same[b][:], srow[b][:], scol.rearrange("p (g o) -> p g o", o=1).to_broadcast([P, GROUP, P]), ALU.is_equal).then_inc(same_ready, 1)
                dve.wait_ge(same_ready, c + 1)

            def earlier_edges(c, b):
                dve.wait_ge(same_ready, c + 1)
                dve.tensor_tensor(earlier[:], same[b][:], before[:].rearrange("p (o e) -> p o e", o=1).to_broadcast([P, GROUP, P]), ALU.mult).then_inc(edge_chain, 1)

            def count_earlier(c):
                dve.wait_ge(edge_chain, c * 3 + 1)
                dve.tensor_reduce(dup[:, 0, :], earlier[:], AX_X, ALU.add).then_inc(edge_chain, 1)

            def choose_rows(c):
                dve.wait_ge(edge_chain, c * 3 + 2)
                dve.scalar_tensor_tensor(dup[:, 1, :], dup[:, 0, :], 0.5, to_trash[:, bass.ds(c * GROUP, GROUP)], ALU.is_gt, ALU.mult).then_inc(edge_chain, 1)

            def scatter_rows(c, b):
                dve.wait_ge(edge_chain, c * 3 + 3)
                if warm(c, 2):
                    for t in range(GROUP):
                        dve.wait_ge(added[t], (c - 1) * 16)
                dve.tensor_tensor(sidx[b][:], dup[:, 1, :], src_f[:, bass.ds(c * GROUP, GROUP)], ALU.add).then_inc(sidx_ready, 1)

            def edge_chunk(c, b, n):
                same_node(c, b, n)
                earlier_edges(c, b)
                count_earlier(c)
                choose_rows(c)
                scatter_rows(c, b)
                for t in range(GROUP):
                    g = c * GROUP + t
                    q = (b + t) % 2
                    dve.wait_ge(pair_mm, g + 1)
                    dve.tensor_tensor(filt[q][:], bank[4 + q][0:P, 0:D], row["bf2"][0:P], ALU.add).then_inc(filt_ready, 1)
                    dve.wait_ge(filt_ready, g + 1)
                    dve.wait_ge(xg_in[b][t], n * 16)
                    if not isinstance(c, int) or g >= 2:
                        dve.wait_ge(sum_mm, g - 1)
                    dve.tensor_tensor(msg[q][:], filt[q][:], xg[b][:, t, :], ALU.mult).then_inc(msg_ready, 1)

            def inputs_low(c, b):
                low = slice(2 * STACK, KS)
                dve.wait_ge(att_high, c + 1)
                dve.tensor_tensor(att3s[b][low], att3[b][low], att3s[b][low].bitcast(F32), ALU.subtract).then_inc(att_low, 1)

            def one_hot(c, b, n):
                dve.wait_ge(srow_in[b], n * 48)
                if warm(c, 2):
                    dve.wait_ge(pair_mm, (c - 1) * GROUP)
                dve.tensor_scalar(hot[b][:], drow[b][:], wstart[:, bass.ds(c, 1)], None, ALU.is_equal).then_inc(hot_ready, 1)

            def window_hidden_low(c, b, a):
                lo, m = [v * P for v in THIRDS[a]]
                dve.wait_ge(hid_act, (c * NT + a + 1) * 2)
                dve.tensor_tensor(eh2[b][1][:, :, lo:lo + m], eh_full[:, :, lo:lo + m], eh2[b][0][:, :, lo:lo + m].bitcast(F32), ALU.subtract).then_inc(hid_low, 1)

            def window_message(c, b, t):
                dve.wait_ge(ends_copied, c * GROUP + t + 1)
                if warm(c, 1):
                    dve.wait_ge(sum_mm, (c - 1) * GROUP + t + 1)
                dve.tensor_tensor(msgs[:, t, :], pair_bank(b, t)[0:P, 0:D], ends_x[:, t, :], ALU.mult).then_inc(msg_ready, 1)

            def window_chunk(c, b, n, left):
                nxt = (c + 1, 1 - b)
                for t in range(GROUP):
                    window_message(c, b, t)
                    if t == 0:
                        window_hidden_low(c, b, 1)
                        if left:
                            one_hot(*nxt, next_n(b, n))
                    elif t == 1:
                        earlier_edges(c, b)
                    elif t == 2:
                        window_hidden_low(c, b, 2)
                        if left:
                            same_node(*nxt, 3 * next_n(b, n))
                    elif t == 3:
                        if left:
                            window_hidden_low(*nxt, 0)
                        count_earlier(c)
                    elif t == 4:
                        choose_rows(c)
                        if left == 2:
                            inputs_low(c + 2, b)
                        scatter_rows(c, b)

            def windows():
                for c in range(2):
                    inputs_low(c, c)
                window_hidden_low(0, 0, 0)
                one_hot(0, 0, 1)
                same_node(0, 0, 3)
                chunks(dve, window_chunk, 2)

            by_path(dve, windows, lambda: chunks(dve, lambda c, b, n, left: edge_chunk(c, b, n), 1))

            dve.tensor_tensor(x[:], x[:], xn[:, :, 0:D], ALU.add).then_inc(x_residual, 1)
            def stats_of(f):
                for a, (lo, hi) in enumerate(PIECES):
                    for o in range(KD):
                        dve.wait_ge(h_ready, f * 4 + a * 2 + o + 1)
                        ins = dve.bn_stats(cstat[:, o, 2 * f + a, :], xT[:, o, f * FOLD * P + lo:f * FOLD * P + hi])
                return ins

            for f in range(FOLDS):
                dve.wait_ge(part_in[f % 2], (f // 2 + 1) * GROUP * 16)
                p = part[f % 2]
                dve.tensor_tensor(p[1][:], p[1][:], p[2][:], ALU.add)
                step(dve.tensor_tensor(p[0][:], p[0][:], p[3][:], ALU.add))
                step(dve.tensor_tensor(p[1][:], p[1][:], p[4][:], ALU.add))
                dve.tensor_tensor(p[0][:], p[0][:], p[1][:], ALU.add).then_inc(agg_ready, 1)
                if f >= 2:
                    stats_of(f - 2)
            stats_of(FOLDS - 2)
            step(stats_of(FOLDS - 1))
            for k in range(KD):
                ins = dve.bn_aggr(cmv[:, k, :], cstat[:, k].rearrange("p a b -> p (a b)"))
            ins.then_inc(bn_var, 1)
            dve.wait_ge(bn_std, 1)
            step(dve.reciprocal(csc[:, 0, :], csc[:, 0, :]))
            step(dve.tensor_tensor(csc[:, 1, :], csc[:, 0, :], chan[:, CH_AT["gamma"]:CH_AT["gamma"] + KD], ALU.mult))
            step(dve.tensor_tensor(csc[:, 0, :], csc[:, 1, :], cmv[:, :, 0], ALU.mult))
            dve.tensor_tensor(csc[:, 2, :], chan[:, CH_AT["beta"]:CH_AT["beta"] + KD], csc[:, 0, :], ALU.subtract).then_inc(bn_scale, 1)

            def low_copies(f):
                for t in range(f * FOLD, (f + 1) * FOLD):
                    dve.wait_ge(turned_copied, 2 * TILES + t + 1)
                    ts = slice(t * P, (t + 1) * P)
                    dve.tensor_tensor(xTs[1][:, :, ts], turn_bank(2, t)[:, 0:KD * P].rearrange("p (k e) -> p k e", k=KD), xTs[0][:, :, ts].bitcast(F32),
                                      ALU.subtract).then_inc(x_low, 1)

            dve.wait_ge(x_residual, 1)
            for f in range(FOLDS + 1):
                if f < FOLDS:
                    for t in range(f * FOLD, (f + 1) * FOLD):
                        dve.wait_ge(bn_turned, t + 1)
                        dve.tensor_tensor(x[:, t, :], x[:, t, :], bank[5 + t % 3][0:P, 0:D], ALU.add).then_inc(x3_ready, 1)
                    dve.wait_ge(x3_ready, (f + 1) * FOLD)
                    ln_stats(3, f)
                if f >= 1:
                    low_copies(f - 1)
                if f < FOLDS:
                    ln_apply(3, f)
            dve.wait_ge(mix_mm, NS)
            lg, ex = sm8[:, 0], sm8[:, 1]
            g8 = bank[3][0:P, 0:TILES * EXPERTS].rearrange("p (t e) -> p t e", e=EXPERTS)
            step(dve.tensor_tensor(lg, g8, rowbc(row["br"][0:P]), ALU.add))
            step(dve.tensor_reduce(sm1[:, 0, :], lg, AX_X, ALU.max))
            dve.tensor_tensor(lg, lg, bc(sm1[:, 0, :], EXPERTS), ALU.subtract).then_inc(mix_shift, 1)
            dve.wait_ge(mix_exp, 1)
            step(dve.tensor_reduce(sm1[:, 1, :], ex, AX_X, ALU.add))
            step(dve.reciprocal(sm1[:, 1, :], sm1[:, 1, :]))
            dve.tensor_tensor(mix[:], ex, bc(sm1[:, 1, :], EXPERTS), ALU.mult).then_inc(mix_ready, 1)
            dve.wait_ge(mix_ready, 1)

            def dense_low(e, b, s, layer, halves=(0, 1)):
                at, n = STEPS[s]
                m = n * P
                done, low = ((d1_act, d1_low), (d2_act, d2_low))[layer]
                g = e * (NS * KD) + s * KD
                dst = (h1, h2)[layer][(b + s) % 2]
                for o in halves:
                    dve.wait_ge(done, (g + o + 1) * 2)
                    dve.tensor_tensor(dst[1][:, o, 0:m], h_full[layer][o][:, 0:m], dst[0][:, o, 0:m].bitcast(F32), ALU.subtract).then_inc(low, 1)

            def add_bias(t):
                dve.wait_ge(bo_mm, t + 1)
                dve.wait_ge(d3_added, t + 1)
                dve.tensor_tensor(x[:, t, :], x[:, t, :], bank[7][0:P, 0:D], ALU.add).then_inc(bo_added, 1)

            def dense_add(e, b, s, half):
                at, n = STEPS[s]
                half_n = -(-n // 2)
                for t in (range(at, at + half_n), range(at + half_n, at + n))[half]:
                    if isinstance(e, int) and e == 0 and t >= 1:
                        add_bias(t - 1)
                    dve.wait_ge(d3_mm, e * TILES + t + 1)
                    if isinstance(e, int) and e == 1:
                        if t == 0:
                            add_bias(TILES - 1)
                        dve.wait_ge(bo_added, t + 1)
                    elif not isinstance(e, int):
                        dve.wait_ge(d3_added, (e - 1) * TILES + t + 1)
                    dve.scalar_tensor_tensor(x[:, t, :], last_bank(e, b, t)[0:P, 0:D], mix[:, t, bass.ds(e, 1)], x[:, t, :],
                                             ALU.mult, ALU.add).then_inc(d3_added, 1)

            dense_steps(dve, ((lambda e, b, s: dense_low(e, b, s, 0), 0), (lambda e, b, s: dense_low(e, b, s, 1, (0,)), 1),
                              (lambda e, b, s: dense_add(e, b, s, 0), 2), (lambda e, b, s: dense_low(e, b, s, 1, (1,)), 1),
                              (lambda e, b, s: dense_add(e, b, s, 1), 2)))


def _arrange(inputs):
    def get(name):
        return np.asarray(inputs[name])

    def halves(name):
        return get(name).reshape(KD, HALF).T

    def pairs(name):
        return get("L1_ffn_" + name).reshape(EXPERTS, KD, HALF).transpose(2, 0, 1).reshape(HALF, EXPERTS * KD)

    chan = [halves("L1_gnn_" + n) for n in CHAN] + [pairs(n) for n in PAIR]
    chan.append(get("L0_ffn_b1").reshape(EXPERTS, FC, HALF).transpose(2, 0, 1).reshape(HALF, EXPERTS * FC))
    rows = [get("L0_gnn_attn_l"), get("L0_gnn_attn_r"), get("L1_gnn_bf2"), get("L0_ffn_gate_b"), get("L1_ffn_br")]
    arrays = {
        "x": get("x"), "src": get("src"), "dst": get("dst"),
        "src_col": get("src").reshape(E_TILES, P).T, "dst_col": get("dst").reshape(E_TILES, P).T,
        "rbf_t": get("edge_attr_20").T,
        "chan": np.concatenate(chan, axis=1), "rows": np.concatenate([r.reshape(-1) for r in rows]), "b2": get("L0_ffn_b2").reshape(-1),
        "gnn_w": get("L0_gnn_weight"), "gate_w": get("L0_ffn_gate_w"), "w1": get("L0_ffn_w1"), "w2": get("L0_ffn_w2"),
        "wf1": get("L1_gnn_Wf1"), "wf2": get("L1_gnn_Wf2"), "wu1": get("L1_gnn_Wu1"), "wu2": get("L1_gnn_Wu2"),
        "wr": get("L1_ffn_Wr"), "dw1": get("L1_ffn_W1"), "dw2": get("L1_ffn_W2"), "dwo": get("L1_ffn_Wo"),
        "bo": get("L1_ffn_bo"), "bf1": get("L1_gnn_bf1").reshape(1, D), "bf2": get("L1_gnn_bf2").reshape(1, D),
    }
    return {f"in_{k}": np.ascontiguousarray(v) for k, v in arrays.items()}


def kernel(**inputs):
    import concourse.bacc as bacc
    from concourse.bass_utils import run_bass_kernel_spmd

    nc = bacc.Bacc("TRN2", target_bir_lowering=False, num_devices=1)
    arrays = _arrange(inputs)
    A = {k[3:]: nc.dram_tensor(k, v.shape, mybir.dt.from_np(v.dtype), kind="ExternalInput").ap() for k, v in arrays.items()}
    out = nc.dram_tensor("out_0", (N_NODES, D), F32, kind="ExternalOutput").ap()
    build(nc, A, out)
    r = run_bass_kernel_spmd(nc, [arrays], core_ids=[0])
    return r.results[0]["out_0"]
```
